# Optimizing a Trainium2 kernel written in Bass

```python
import numpy as np
import jax
import jax.numpy as jnp

def _softmax(x, axis=-1):
    return jax.nn.softmax(x, axis=axis)

def _gelu(x):
    return jax.nn.gelu(x, approximate=True)

def _silu(x):
    return jax.nn.silu(x)

def _sigmoid(x):
    return jax.nn.sigmoid(x)

def _layernorm(x, axis=-1, eps=1e-05):
    m = jnp.mean(x, axis=axis, keepdims=True)
    v = jnp.var(x, axis=axis, keepdims=True)
    return (x - m) / jnp.sqrt(v + eps)

def _scatter_add(tgt, idx, src, axis=0):
    return tgt.at[idx].add(src)

def _segment_sum(src, seg, n):
    return jax.ops.segment_sum(src, seg, n)
kernel_name = 'mk_decoder_preln_d1_seqx_r4_574ece'

def setup_inputs(seed: int=0):
    np.random.seed(seed)
    _w = jnp.asarray

    def _rec_inputs():
        import jax
        import jax.numpy as jnp
        _rk = jax.random.key(seed)
        x = 7.22e-05 + 1 * jax.random.normal(jax.random.fold_in(_rk, 1), (32, 100, 512), jnp.float32)
        _lenS = 100 - jax.random.randint(jax.random.fold_in(_rk, 7), (32,), 0, max(1, 100 // 4) + 1, jnp.int32)
        _lenS2 = 361 - jax.random.randint(jax.random.fold_in(_rk, 8), (32,), 0, max(1, 361 // 4) + 1, jnp.int32)
        _ctx_512P = jax.random.normal(jax.random.fold_in(_rk, 11), (32, 16, 128), jnp.float32)
        _ctx_512c = jax.random.dirichlet(jax.random.fold_in(_rk, 511), 0.3 * jnp.ones((16,), jnp.float32), (32, 361))
        _ctx_512t = jnp.einsum('bsk,bkd->bsd', _ctx_512c, _ctx_512P)
        _ctx_512t = _ctx_512t * jax.lax.rsqrt(jnp.mean(jnp.square(_ctx_512t)) + 1e-12) * 0.953939
        ctx_512 = -0.000514642 + 1.00011 * (_ctx_512t + 0.3 * jax.random.normal(jax.random.fold_in(_rk, 611), (32, 361, 128), jnp.float32))
        return (x, ctx_512)
    x, ctx_512 = _rec_inputs()

    def _L0_attn_setup():
        import jax, jax.numpy as jnp
        import numpy as np
        EPS = 1e-06

        def rms_norm(x, scale):
            x32 = x.astype(jnp.float32)
            mean2 = jnp.mean(jnp.square(x32), axis=-1, keepdims=True)
            return x32 * jax.lax.rsqrt(mean2 + EPS) * scale
        key = jax.random.key(seed)
        ks = jax.random.split(key, 7)
        B, S, E, H, D = (2, 512, 512, 16, 128)
        w_std = 1.0 / np.sqrt(E)
        x = jax.random.normal(ks[0], (B, S, E), jnp.float32)
        wq = jax.random.normal(ks[1], (E, H, D), jnp.float32) * w_std
        wk = jax.random.normal(ks[2], (E, H, D), jnp.float32) * w_std
        wv = jax.random.normal(ks[3], (E, H, D), jnp.float32) * w_std
        wo = jax.random.normal(ks[4], (H, D, E), jnp.float32) * (1.0 / np.sqrt(H * D))
        q_scale = jnp.ones((D,), jnp.float32)
        k_scale = jnp.ones((D,), jnp.float32)
        return {'x': x, 'wq': wq, 'wk': wk, 'wv': wv, 'wo': wo, 'q_scale': q_scale, 'k_scale': k_scale}
    _L0_attn_all = _L0_attn_setup()
    _L0_attn_in = {k: v for k, v in _L0_attn_all.items() if k in ('wq', 'wk', 'wv', 'wo', 'q_scale', 'k_scale')}
    del _L0_attn_all

    def _L0_xattn_setup():
        import jax, jax.numpy as jnp
        import numpy as np
        B, S, H, NH, L = (2, 512, 512, 16, 128)
        HD = H // NH
        key = jax.random.key(seed)
        k1, k2, k3, k4, k5 = jax.random.split(key, 5)
        scale = 0.02
        return {'q': jax.random.normal(k1, (B, S, H), dtype=jnp.float32), 'latent_kv': jax.random.normal(k2, (B, S, L), dtype=jnp.float32), 'Wq': jax.random.normal(k3, (H, H), dtype=jnp.float32) * scale, 'Wkv_expand': jax.random.normal(k4, (2 * H, L), dtype=jnp.float32) * scale, 'Wout': jax.random.normal(k5, (H, H), dtype=jnp.float32) * scale}
    _L0_xattn_all = _L0_xattn_setup()
    _L0_xattn_in = {k: v for k, v in _L0_xattn_all.items() if k in ('Wq', 'Wkv_expand', 'Wout')}
    del _L0_xattn_all

    def _L0_ffn_setup():
        import jax, jax.numpy as jnp
        import numpy as np
        B, S, D = (4, 512, 512)
        DFF = 1408
        E, K, R = (8, 2, 16)
        SCALING = 32.0 / 16.0
        key = jax.random.key(seed)
        ks = jax.random.split(key, 12)
        s = lambda k, shape, scale: jax.random.normal(k, shape, dtype=jnp.float32) * scale
        return {'x': s(ks[0], (B, S, D), 1.0), 'Wg': s(ks[1], (DFF, D), 0.02), 'Wu': s(ks[2], (DFF, D), 0.02), 'Wd': s(ks[3], (D, DFF), 0.02), 'Wr': s(ks[4], (E, D), 0.02), 'Ag': s(ks[5], (E, R, D), 0.02), 'Bg': s(ks[6], (E, DFF, R), 0.02), 'Au': s(ks[7], (E, R, D), 0.02), 'Bu': s(ks[8], (E, DFF, R), 0.02), 'Ad': s(ks[9], (E, R, DFF), 0.02), 'Bd': s(ks[10], (E, D, R), 0.02)}
    _L0_ffn_all = _L0_ffn_setup()
    _L0_ffn_in = {k: v for k, v in _L0_ffn_all.items() if k in ('Wg', 'Wu', 'Wd', 'Wr', 'Ag', 'Bg', 'Au', 'Bu', 'Ad', 'Bd')}
    del _L0_ffn_all
    return {'x': x, 'ctx_512': ctx_512, 'L0_attn_wq': _L0_attn_in['wq'], 'L0_attn_wk': _L0_attn_in['wk'], 'L0_attn_wv': _L0_attn_in['wv'], 'L0_attn_wo': _L0_attn_in['wo'], 'L0_attn_q_scale': _L0_attn_in['q_scale'], 'L0_attn_k_scale': _L0_attn_in['k_scale'], 'L0_xattn_Wq': _L0_xattn_in['Wq'], 'L0_xattn_Wkv_expand': _L0_xattn_in['Wkv_expand'], 'L0_xattn_Wout': _L0_xattn_in['Wout'], 'L0_ffn_Wg': _L0_ffn_in['Wg'], 'L0_ffn_Wu': _L0_ffn_in['Wu'], 'L0_ffn_Wd': _L0_ffn_in['Wd'], 'L0_ffn_Wr': _L0_ffn_in['Wr'], 'L0_ffn_Ag': _L0_ffn_in['Ag'], 'L0_ffn_Bg': _L0_ffn_in['Bg'], 'L0_ffn_Au': _L0_ffn_in['Au'], 'L0_ffn_Bu': _L0_ffn_in['Bu'], 'L0_ffn_Ad': _L0_ffn_in['Ad'], 'L0_ffn_Bd': _L0_ffn_in['Bd']}

def reference(x, ctx_512, L0_attn_wq, L0_attn_wk, L0_attn_wv, L0_attn_wo, L0_attn_q_scale, L0_attn_k_scale, L0_xattn_Wq, L0_xattn_Wkv_expand, L0_xattn_Wout, L0_ffn_Wg, L0_ffn_Wu, L0_ffn_Wd, L0_ffn_Wr, L0_ffn_Ag, L0_ffn_Bg, L0_ffn_Au, L0_ffn_Bu, L0_ffn_Ad, L0_ffn_Bd):
    import jax
    import jax.numpy as jnp

    def _L0_attn_ref(x, wq, wk, wv, wo, q_scale, k_scale):
        import jax, jax.numpy as jnp
        import numpy as np
        EPS = 1e-06

        def rms_norm(x, scale):
            x32 = x.astype(jnp.float32)
            mean2 = jnp.mean(jnp.square(x32), axis=-1, keepdims=True)
            return x32 * jax.lax.rsqrt(mean2 + EPS) * scale
        q = jnp.einsum('bse,ehd->bshd', x, wq)
        k = jnp.einsum('bse,ehd->bshd', x, wk)
        v = jnp.einsum('bse,ehd->bshd', x, wv)
        qn = rms_norm(q, q_scale)
        kn = rms_norm(k, k_scale)
        scores = jnp.einsum('bqhd,bkhd->bhqk', qn, kn)
        attn = jax.nn.softmax(scores, axis=-1)
        out = jnp.einsum('bhqk,bkhd->bqhd', attn, v)
        return jnp.einsum('bqhd,hde->bqe', out, wo)

    def _L0_xattn_ref(q, latent_kv, Wq, Wkv_expand, Wout):
        import jax, jax.numpy as jnp
        import numpy as np
        B, S, H, NH, L = (2, 512, 512, 16, 128)
        HD = H // NH
        b, sq, _ = q.shape
        sk = latent_kv.shape[1]
        qp = q @ Wq.T
        kv = latent_kv @ Wkv_expand.T
        k, v = jnp.split(kv, 2, axis=-1)
        qh = qp.reshape(b, sq, NH, HD).transpose(0, 2, 1, 3)
        kh = k.reshape(b, sk, NH, HD).transpose(0, 2, 1, 3)
        vh = v.reshape(b, sk, NH, HD).transpose(0, 2, 1, 3)
        inv_sqrt_d = 1.0 / jnp.sqrt(jnp.float32(HD))
        scores = jnp.einsum('bhqd,bhkd->bhqk', qh, kh) * inv_sqrt_d
        causal = jnp.tril(jnp.ones((sq, sk), dtype=bool))
        scores = jnp.where(causal, scores, jnp.finfo(scores.dtype).min)
        attn = jax.nn.softmax(scores, axis=-1)
        out = jnp.einsum('bhqk,bhkd->bhqd', attn, vh)
        out = out.transpose(0, 2, 1, 3).reshape(b, sq, H)
        return out @ Wout.T

    def _L0_ffn_ref(x, Wg, Wu, Wd, Wr, Ag, Bg, Au, Bu, Ad, Bd):
        import jax, jax.numpy as jnp
        import numpy as np
        B, S, D = (4, 512, 512)
        DFF = 1408
        E, K, R = (8, 2, 16)
        SCALING = 32.0 / 16.0
        b, s, d = x.shape
        xf = x.reshape(-1, d)
        gate_base = xf @ Wg.T
        up_base = xf @ Wu.T
        base_out = jax.nn.silu(gate_base) * up_base @ Wd.T
        router_logits = xf @ Wr.T
        probs = jax.nn.softmax(router_logits.astype(jnp.float32), axis=-1)
        topw, topi = jax.lax.top_k(probs, K)
        topw = topw.astype(x.dtype)
        expert_w = jnp.sum(jax.nn.one_hot(topi, E, dtype=x.dtype) * topw[..., None], axis=1)

        def expert_step(acc, params):
            Ag_e, Bg_e, Au_e, Bu_e, Ad_e, Bd_e, we = params
            g_lora = xf @ Ag_e.T @ Bg_e.T * SCALING
            u_lora = xf @ Au_e.T @ Bu_e.T * SCALING
            h = jax.nn.silu(gate_base + g_lora) * (up_base + u_lora)
            d_delta = h @ Ad_e.T @ Bd_e.T * SCALING
            return (acc + d_delta * we[:, None], None)
        acc0 = jnp.zeros_like(base_out)
        acc, _ = jax.lax.scan(expert_step, acc0, (Ag, Bg, Au, Bu, Ad, Bd, expert_w.T))
        return (base_out + acc).reshape(b, s, d)
    x = x + _L0_attn_ref(_layernorm(x, axis=-1), L0_attn_wq, L0_attn_wk, L0_attn_wv, L0_attn_wo, L0_attn_q_scale, L0_attn_k_scale)
    x = x + _L0_xattn_ref(_layernorm(x, axis=-1), ctx_512, L0_xattn_Wq, L0_xattn_Wkv_expand, L0_xattn_Wout)
    x = x + _L0_ffn_ref(_layernorm(x, axis=-1), L0_ffn_Wg, L0_ffn_Wu, L0_ffn_Wd, L0_ffn_Wr, L0_ffn_Ag, L0_ffn_Bg, L0_ffn_Au, L0_ffn_Bu, L0_ffn_Ad, L0_ffn_Bd)
    return x

_drawn_inputs = setup_inputs


def setup_inputs(seed=0):
    import zlib

    import numpy as np

    out = dict(_drawn_inputs(seed))
    spreads = {'L0_attn_q_scale': (1.0, 0.2), 'L0_attn_k_scale': (1.0, 0.2)}
    factors = {'L0_xattn_Wq': 8.0,
     'L0_ffn_Wr': 8.0,
     'L0_ffn_Ag': 8.0,
     'L0_ffn_Bg': 8.0,
     'L0_ffn_Au': 8.0,
     'L0_ffn_Bu': 8.0,
     'L0_ffn_Ad': 8.0,
     'L0_ffn_Bd': 8.0,
     'L0_ffn_Wd': 55.868}
    for name, (base, spread) in spreads.items():
        noise = np.random.default_rng([zlib.crc32(name.encode()), seed]).standard_normal(out[name].shape)
        drawn = base * np.exp(spread * noise) if base else spread * noise
        out[name] = jnp.asarray(drawn.astype(out[name].dtype))
    for name, factor in factors.items():
        out[name] = (out[name] * factor).astype(out[name].dtype)
    return out
```

```python
from contextlib import ExitStack

import numpy as np

import concourse.bass as bass
from concourse import mybir

ALU = mybir.AluOpType
ACT = mybir.ActivationFunctionType
AX = mybir.AxisListType
F32 = mybir.dt.float32
F16 = mybir.dt.float16
BF16 = mybir.dt.bfloat16

P = 128
S = 100
E = 512
KC = E // P
H = 16
D = 128
HG = 4
NHG = H // HG
GB = 5
X_SCALE = 16.0
W_SCALE = 64.0
V_SCALE = 8.0


F = 1408
FC = F // P
NE = 8
R = 16
L = 128
CD = E // H
CV_SCALE = 32.0
H_SCALE = 8.0
LORA = 2.0
MEM = 53200


def tiles_of(nb):
    n = -(-nb * S // P)
    assert nb * S % n == 0
    return n, nb * S // n


def attention_plan(nb):
    nt, tm = tiles_of(nb)
    steps = NHG * nb
    proj, turn, wo = ([[] for _ in range(steps + 1)] for _ in range(3))
    turn[0].append(nt - 1)
    for hg in range(NHG):
        for t in range(nt):
            if hg:
                at = t if nb > nt else 0
                proj[(hg - 1) * nb + at].append(hg * nt + t)
                turn[(hg - 1) * nb + at + 1].append(hg * nt + t)
            last = -(-(t + 1) * tm // S) - 1
            wo[hg * nb + last + 1].append(hg * nt + t)
    return proj, turn, wo


def decoder_layer(nc, x, wq, wk, wv, wo, q_scale, k_scale, ctxT_in, cwq, cwkv_in, cwo, wg, wu, wd,
                  ag, au, ad, bg, bu, bd, wr, x1, out):
    NB = x.shape[0] // S
    FULL, REST = NB // GB, NB % GB
    NT, TM = tiles_of(GB)
    GS = GB * S

    with ExitStack() as ctx:
        def sb(name, shape, dt):
            return ctx.enter_context(nc.sbuf_tensor(name, shape, dt))

        def sem(name):
            return ctx.enter_context(nc.semaphore(name))

        mem = sb("mem", [P, MEM], F32)

        class Cut:

            def __init__(self, at):
                self.at = at

            def __call__(self, shape, dt=F32):
                n = int(np.prod(shape))
                words = n if dt == F32 else (n + 1) // 2
                ap = mem[:, self.at:self.at + words]
                self.at += words
                assert self.at <= MEM, self.at
                if dt != F32:
                    ap = ap.bitcast(dt)
                names = "abcd"[:len(shape)]
                sizes = {k: v for k, v in zip(names, shape)}
                return ap.rearrange(f"p ({' '.join(names)}) -> p {' '.join(names)}", **sizes)

        cut = Cut(0)
        ident = cut([P])
        ident16 = cut([P], BF16)
        mask = cut([HG, S], BF16)
        half = cut([16])
        qks = cut([4])
        rank = cut([NT, NE])
        phase_start = cut.at

        wqkv_hi = cut([KC, 3, H * D], F16)
        wqkv_lo = cut([KC, 3, H * D], F16)
        wo_hi = cut([H, E], F16)
        wo_lo = cut([H, E], F16)
        xin = cut([NT, E])
        xres = cut([NT, E])
        xT_hi = cut([KC, GS], F16)
        xT_lo = cut([KC, GS], F16)
        stage_a = Cut(cut.at)([2, KC, 512])
        qkT = cut([2, HG, GS + 12])[:, :, :, 0:GS]
        oT_hi = cut([HG, GS], F16)
        oT_lo = cut([HG, GS], F16)
        v = cut([2, HG * D])
        qk = cut([2, 2 * HG, D])
        sq = cut([2 * HG, D])
        probs = cut([2, HG, S])
        pT = cut([HG, S])
        bst = cut([NT, 6])
        mv = cut([NT, 2])
        var = cut([NT])
        rstd = cut([NT])
        ss = cut([2, 2 * HG])
        ms = cut([2, 2 * HG])
        rr = cut([2, 2 * HG])
        mx = cut([HG])
        den = cut([HG])
        rden = cut([HG])

        cut = Cut(phase_start)
        cwq_hi, cwq_lo = cut([KC, E], F16), cut([KC, E], F16)
        cwo_hi, cwo_lo = cut([KC, E], F16), cut([KC, E], F16)
        cwkv = cut([2 * E])
        wg_hi, wg_lo = cut([KC, F], F16), cut([KC, F], F16)
        wu_hi, wu_lo = cut([KC, F], F16), cut([KC, F], F16)
        wd_hi, wd_lo = cut([FC, E], F16), cut([FC, E], F16)
        ag_hi, ag_lo = cut([KC, P], F16), cut([KC, P], F16)
        au_hi, au_lo = cut([KC, P], F16), cut([KC, P], F16)
        ad_hi, ad_lo = cut([FC, P], F16), cut([FC, P], F16)
        bg_hi, bg_lo = cut([F], F16), cut([F], F16)
        bu_hi, bu_lo = cut([F], F16), cut([F], F16)
        bd_hi, bd_lo = cut([E], F16), cut([E], F16)
        wr_hi, wr_lo = cut([KC, NE], F16), cut([KC, NE], F16)
        stats = [cut([NT, 6]), cut([NT, 2]), cut([NT]), cut([NT])]
        y = cut([NT, E])
        yT_hi, yT_lo = cut([KC, GS], F16), cut([KC, GS], F16)
        part_start = cut.at
        stage_b = Cut(part_start)([2, 2048])
        yn = cut([NT, E])
        shared_end = cut.at
        qpT = cut([KC, GS])
        ckT = cut([KC, GS])
        ctxT = cut([GS])
        cv = cut([GB, E])
        cprobs = cut([4, HG, S])
        cpT = cut([2, HG, S])
        cmx = cut([4, HG])
        cden = cut([2, H])
        crden = cut([2, H])
        on = cut([E])
        coT_hi, coT_lo = cut([KC, GS], F16), cut([KC, GS], F16)
        cut = Cut(shared_end)
        spread = yn[:, :, :].rearrange("p t (k e r) -> p t k e r", k=4, e=NE)
        rt = {n: cut([NT, NE]) for n in ("l", "p", "a", "b")}
        col = {n: cut([NT]) for n in ("m", "d", "r", "w1", "w2")}
        sel = cut([4, NT, NE])
        msk = cut([4, GS])
        tmp = cut([4, GS])
        am_hi, am_lo = cut([4, GS], F16), cut([4, GS], F16)
        hb_hi, hb_lo = cut([FC, GS], F16), cut([FC, GS], F16)
        gb = cut([GS])
        ub = cut([GS])
        gate = cut([3, GS])
        up = cut([2, GS])
        hh = cut([3, GS])
        hs_hi, hs_lo = cut([2, GS], F16), cut([2, GS], F16)
        d_hi, d_lo = cut([GS], F16), cut([GS], F16)

        ps = ctx.enter_context(nc.psum_tensor("ps", [P, 8, 512], F32))
        ps_qk, ps_T = ps[:, 0:2, :], ps[:, 2:4, :]
        ps_vw, ps_s, ps_pT, ps_o = (ps[:, b, :] for b in range(4, 8))

        names = ("ident0 ident half scales wld0 wld1 whi wlo qkl qks "
                 "xin xres bst mv var rstd xn lnT xhi xlo "
                 "qkp raw sq ss ms rr qkn qkT qTe kTe vp ve s mx sub exp den rden norm pTp pTe "
                 "o ohi olo w add x1")
        s = {n: sem("s_" + n) for n in names.split()}
        names = ("wld0 wld1 whi wlo wkv mask rank y ctx out bst mv var rstd yn lnT lnhi lnlo "
                 "qp qpe ck cke v ve sc mx sub exp den rden pT pTe pv on oT ohi olo w x2 "
                 "rl lg top rexp chain spread mT mTe a am ahi alo base gb sg0 ub lora gs us sgs "
                 "h hhi hlo ad dt dsum dhi dlo yp add")
        c = {n: sem("c_" + n) for n in names.split()}
        block = ctx.enter_context(nc.Block())

        N_STEP, N_QK = NHG * GB, NHG * NT

        plans = {GB: attention_plan(GB)}
        if REST:
            plans[REST] = attention_plan(REST)

        w_src = [w.rearrange("(c p) n -> p c n", p=P) for w in (wq, wk, wv)]
        wo_src = wo.rearrange("(h d) n -> d h n", d=D)
        PIECES = [(m, hg) for hg in range(NHG) for m in range(4)]

        B_PIECES = []

        def flat(ap):
            return ap if len(ap.shape) == 2 else ap.rearrange("p a b -> p (a b)")

        def add_pieces(hi, lo, src, chunks, width):
            step = max(1, 2048 // width)
            src = src.rearrange("(c p) n -> p c n", p=P)
            for a in range(0, chunks, step):
                b = min(chunks, a + step)
                B_PIECES.append((flat(hi)[:, a * width:b * width], flat(lo)[:, a * width:b * width],
                                 src[:, a:b, :], (b - a), width))

        add_pieces(cwq_hi, cwq_lo, cwq, KC, E)
        add_pieces(cwo_hi, cwo_lo, cwo, KC, E)
        add_pieces(wr_hi, wr_lo, wr, KC, NE)
        add_pieces(ag_hi, ag_lo, ag, KC, P)
        add_pieces(au_hi, au_lo, au, KC, P)
        add_pieces(wg_hi, wg_lo, wg, KC, F)
        add_pieces(wu_hi, wu_lo, wu, KC, F)
        add_pieces(bg_hi, bg_lo, bg, 1, F)
        add_pieces(bu_hi, bu_lo, bu, 1, F)
        add_pieces(ad_hi, ad_lo, ad, FC, P)
        add_pieces(wd_hi, wd_lo, wd, FC, E)
        add_pieces(bd_hi, bd_lo, bd, 1, E)
        GROUPS = FULL + (REST > 0)
        N_ALL_QK = FULL * NHG * NT + (NHG * tiles_of(REST)[0] if REST else 0)
        LINKS = 18

        def piece(m, hg, hi):
            if m < 3:
                return (wqkv_hi if hi else wqkv_lo)[:, :, m, hg * 512:(hg + 1) * 512]
            return (wo_hi if hi else wo_lo)[:, hg * HG:(hg + 1) * HG, :]

        @block.sync
        def _(sp):
            sp.dma_start(qks[:, 0:1], q_scale).then_inc(s["scales"], 16)
            sp.dma_start(qks[:, 1:2], k_scale).then_inc(s["scales"], 16)

            def group(g, nb):
                nt, tm = tiles_of(nb)
                t0 = sp.snap(g * GS) if nb == GB else g * GS
                src = x[bass.ds(t0, nt * tm), :].rearrange("(t p) e -> p t e", p=tm)
                dst = x1[bass.ds(t0, nt * tm), :].rearrange("(t p) e -> p t e", p=tm)
                sp.wait_ge(s["lnT"], g * NT)
                sp.dma_start(xin[0:tm, 0:nt, :], src).then_inc(s["xin"], 16)
                sp.wait_ge(s["x1"], g * 16)
                sp.dma_start(xres[0:tm, 0:nt, :], src).then_inc(s["xres"], 16)
                sp.wait_ge(s["add"], g * N_QK + NHG * nt)
                sp.dma_start(dst, xres[0:tm, 0:nt, :]).then_inc(s["x1"], 16)

            for n, (m, hg) in enumerate(PIECES):
                if n >= 2:
                    sp.wait_ge(s["wlo"], n - 1)
                src = (w_src[m][:, :, hg * 512:(hg + 1) * 512] if m < 3
                       else wo_src[:, hg * HG:(hg + 1) * HG, :])
                sp.dma_start(stage_a[:, n % 2, :, :], src).then_inc(s[f"wld{n % 2}"], 16)
            with sp.Fori(0, FULL) as g:
                group(g, GB)
            if REST:
                group(FULL, REST)
            sp.wait_ge(s["x1"], 16 * (FULL + (REST > 0)))

            sp.dma_start(cwkv[:, :], cwkv_in).then_inc(c["wkv"], 16)
            for n, (_, _, src, chunks, width) in enumerate(B_PIECES):
                if n >= 2:
                    sp.wait_ge(c["wlo"], n - 1)
                sp.dma_start(stage_b[:, n % 2, 0:chunks * width].rearrange(
                    "p (c n) -> p c n", c=chunks), src).then_inc(c[f"wld{n % 2}"], 16)

            def layer(g, nb):
                nt, tm = tiles_of(nb)
                t0 = sp.snap(g * GS) if nb == GB else g * GS
                b0 = sp.snap(g * GB) if nb == GB else g * GB
                src = x1[bass.ds(t0, nt * tm), :].rearrange("(t p) e -> p t e", p=tm)
                dst = out[bass.ds(t0, nt * tm), :].rearrange("(t p) e -> p t e", p=tm)
                keys = ctxT_in[bass.ds(b0, nb), :, 0:S].rearrange("b l k -> l b k")
                sp.wait_ge(c["out"], g * 16)
                sp.dma_start(y[0:tm, 0:nt, :], src).then_inc(c["y"], 16)
                sp.dma_start(ctxT[:, 0:nb * S].rearrange("l (b k) -> l b k", b=nb),
                             keys).then_inc(c["ctx"], 16)
                sp.wait_ge(c["add"], g * NT + nt)
                sp.dma_start(dst, y[0:tm, 0:nt, :]).then_inc(c["out"], 16)

            sp.wait_ge(c["wlo"], len(B_PIECES))
            with sp.Fori(0, FULL) as g:
                layer(g, GB)
            if REST:
                layer(FULL, REST)
            sp.wait_ge(c["out"], 16 * GROUPS)

        @block.gpsimd
        def _(pool):
            pool.memset(half[:, :], -0.5).then_inc(s["half"], 1)
            pool.memset(ident[:, :], 0.0).then_inc(s["ident0"], 1)
            pool.wait_ge(s["ident0"], 1)
            pool.affine_select(out=ident[:, :], in_=ident[:, :], compare_op=ALU.not_equal, fill=1.0,
                               base=0, pattern=[[-1, P]], channel_multiplier=1).then_inc(s["ident"], 1)
            pool.wait_ge(s["half"], 1)
            pool.memset(ident16[:, :], 0.0).then_inc(c["mask"], 1)
            pool.memset(mask[:, :, :], 0.0).then_inc(c["mask"], 1)
            pool.wait_ge(c["mask"], 2)
            pool.affine_select(out=ident16[:, :], in_=ident16[:, :], compare_op=ALU.not_equal,
                               fill=1.0, base=0, pattern=[[-1, P]],
                               channel_multiplier=1).then_inc(c["mask"], 1)
            pool.affine_select(out=mask[0:S, :, :], in_=mask[0:S, :, :], compare_op=ALU.is_ge,
                               fill=-1e30, base=0, pattern=[[0, HG], [-1, S]],
                               channel_multiplier=1).then_inc(c["mask"], 1)
            for e in range(NE):
                pool.memset(rank[:, :, e:e + 1], float(NE - e)).then_inc(c["rank"], 1)

            def group(g, nb):
                nt, tm = tiles_of(nb)
                proj, turn, _ = plans[nb]
                b_step, b_qk = g * N_STEP, g * N_QK

                def rms(u):
                    i = u % 2
                    pool.wait_ge(s["raw"], b_qk + u + 1)
                    pool.wait_ge(s["ss"], b_qk + u)
                    pool.tensor_tensor(sq[0:tm, :, :], qk[0:tm, i, :, :], qk[0:tm, i, :, :],
                                       ALU.mult).then_inc(s["sq"], 1)
                    pool.wait_ge(s["ms"], b_qk + u + 1)
                    pool.tensor_tensor(rr[0:tm, i, :], ms[0:tm, i, :], half[0:tm, 0:2 * HG],
                                       ALU.pow).then_inc(s["rr"], 1)

                pool.wait_ge(s["var"], g + 1)
                pool.tensor_tensor(rstd[0:tm, 0:nt], var[0:tm, 0:nt], half[0:tm, 0:nt],
                                   ALU.pow).then_inc(s["rstd"], 1)
                for u in range(nt):
                    rms(u)
                for n in range(NHG * nb):
                    for u in (proj[n - 1] if n else []):
                        rms(u)
                    pool.wait_ge(s["rden"], b_step + n + 1)
                    pool.tensor_tensor(probs[0:S, n % 2, :, :], probs[0:S, n % 2, :, :],
                                       rden[0:S, :].unsqueeze(2).to_broadcast([S, HG, S]),
                                       ALU.mult).then_inc(s["norm"], 1)

            with pool.Fori(0, FULL) as g:
                group(g, GB)
            if REST:
                group(FULL, REST)

            def layer(g, nb):
                nt, tm = tiles_of(nb)
                gs = nb * S
                for k in range(2):
                    pool.wait_ge(c["var"], g * 2 + k + 1)
                    pool.tensor_tensor(stats[3][0:tm, 0:nt], stats[2][0:tm, 0:nt], half[0:tm, 0:nt],
                                       ALU.pow).then_inc(c["rstd"], 1)
                for j in range(FC):
                    if j == 0:
                        pool.wait_ge(c["hlo"], g * 3 * FC)
                    for i in range(3):
                        if i == 0:
                            pool.wait_ge(c["sg0"], g * FC + j + 1)
                            pool.wait_ge(c["ub"], g * FC + j + 1)
                        else:
                            pool.wait_ge(c["sgs"], g * 2 * FC + 2 * j + i)
                            pool.wait_ge(c["us"], g * 2 * FC + 2 * j + i)
                        if j:
                            pool.wait_ge(c["hlo"], g * 3 * FC + 3 * (j - 1) + i + 1)
                        pool.tensor_tensor(hh[:, i, 0:gs], gate[:, i, 0:gs],
                                           ub[:, 0:gs] if i == 0 else up[:, i - 1, 0:gs],
                                           ALU.mult).then_inc(c["h"], 1)

            with pool.Fori(0, FULL) as g:
                layer(g, GB)
            if REST:
                layer(FULL, REST)

        @block.scalar
        def _(act):
            for n, (m, hg) in enumerate(PIECES):
                act.wait_ge(s[f"wld{n % 2}"], 16 * (n // 2 + 1))
                act.activation(piece(m, hg, True), stage_a[:, n % 2, :, :], ACT.Copy,
                               scale=W_SCALE).then_inc(s["whi"], 1)

            def group(g, nb):
                nt, tm = tiles_of(nb)
                proj, turn, _ = plans[nb]
                b_step, b_qk, b_t = g * N_STEP, g * N_QK, g * NT

                def take_raw(u):
                    act.wait_ge(s["qkp"], b_qk + u + 1)
                    act.wait_ge(s["qkT"], b_qk + max(u - 1, 0))
                    act.activation(qk[0:tm, u % 2, :, :], ps_qk[0:tm, :, :].rearrange(
                        "p a (h d) -> p (a h) d", d=D), ACT.Copy).then_inc(s["raw"], 1)

                def take_qT(u):
                    act.wait_ge(s["qkT"], b_qk + u + 1)
                    t = u % nt
                    act.activation(qkT[:, 0, :, t * tm:(t + 1) * tm],
                                   ps_T[:, 0, 0:HG * tm].rearrange("p (h t) -> p h t", h=HG),
                                   ACT.Copy, scale=qks[:, 2:3]).then_inc(s["qTe"], 1)

                for t in range(nt):
                    act.wait_ge(s["lnT"], b_t + t + 1)
                    act.activation(xT_hi[:, :, t * tm:(t + 1) * tm],
                                   ps_T[:, t % 2, 0:KC * tm].rearrange("p (c t) -> p c t", c=KC),
                                   ACT.Copy).then_inc(s["xhi"], 1)
                for u in range(nt):
                    take_raw(u)
                    if u:
                        take_qT(u - 1)
                for n in range(NHG * nb + 1):
                    if n:
                        act.wait_ge(s["pTp"], b_step + n)
                        act.wait_ge(s["o"], b_step + n - 1)
                        act.activation(pT[0:S, :, :], ps_pT[0:S, 0:HG * S].rearrange(
                            "p (h t) -> p h t", h=HG), ACT.Copy).then_inc(s["pTe"], 1)
                    if n < NHG * nb:
                        act.wait_ge(s["sub"], b_step + n + 1)
                        act.activation(probs[0:S, n % 2, :, :], probs[0:S, n % 2, :, :],
                                       ACT.Exp).then_inc(s["exp"], 1)
                        act.wait_ge(s["vp"], b_step + n + 1)
                        act.wait_ge(s["o"], b_step + max(n - 1, 0))
                        act.activation(v[0:S, n % 2, :], ps_vw[0:S, :], ACT.Copy,
                                       scale=V_SCALE / (X_SCALE * W_SCALE)).then_inc(s["ve"], 1)
                    if n:
                        b = (n - 1) % nb
                        act.wait_ge(s["o"], b_step + n)
                        act.activation(oT_hi[:, :, b * S:(b + 1) * S],
                                       ps_o[:, 0:HG * S].rearrange("p (h t) -> p h t", h=HG),
                                       ACT.Copy).then_inc(s["ohi"], 1)
                    for u in turn[n]:
                        take_qT(u)
                    for u in proj[n]:
                        take_raw(u)

            with act.Fori(0, FULL) as g:
                group(g, GB)
            if REST:
                group(FULL, REST)

            for n, (hi, _, _, chunks, width) in enumerate(B_PIECES):
                act.wait_ge(c[f"wld{n % 2}"], 16 * (n // 2 + 1))
                act.activation(hi, stage_b[:, n % 2, 0:chunks * width], ACT.Copy,
                               scale=W_SCALE).then_inc(c["whi"], 1)

            def layer(g, nb):
                nt, tm = tiles_of(nb)
                gs = nb * S

                def take_hi(k):
                    for t in range(nt):
                        act.wait_ge(c["lnT"], g * 2 * NT + k * nt + t + 1)
                        act.activation(yT_hi[:, :, t * tm:(t + 1) * tm],
                                       ps[:, 6 + t % 2, 0:KC * tm].rearrange(
                                           "p (c t) -> p c t", c=KC),
                                       ACT.Copy).then_inc(c["lnhi"], 1)

                take_hi(0)
                for m in range(KC):
                    act.wait_ge(c["qp"], g * KC + m + 1)
                    act.activation(qpT[:, m, 0:gs], ps[:, m, 0:gs], ACT.Copy,
                                   scale=float(CD) ** -0.5 / (X_SCALE * W_SCALE)
                                   ).then_inc(c["qpe"], 1)
                for b in range(nb):
                    act.wait_ge(c["v"], g * GB + b + 1)
                    act.activation(cv[0:S, b, :], ps[0:S, 6 + b % 2, :], ACT.Copy,
                                   scale=CV_SCALE).then_inc(c["ve"], 1)
                for b in range(nb + 2):
                    if b >= 2:
                        act.wait_ge(c["oT"], g * GB + b - 1)
                        act.activation(coT_hi[:, :, (b - 2) * S:(b - 1) * S],
                                       ps[:, 6 + b % 2, 0:KC * S].rearrange("p (c t) -> p c t", c=KC),
                                       ACT.Copy).then_inc(c["ohi"], 1)
                    for i in range(4):
                        if 1 <= b <= nb:
                            r = 4 * (b - 1) + i
                            act.wait_ge(c["pT"], g * 4 * GB + r + 1)
                            if r >= 2:
                                act.wait_ge(c["pv"], g * 4 * GB + r - 1)
                            act.activation(cpT[0:S, r % 2, :, :],
                                           ps[0:S, 4, 0:HG * S].rearrange("p (h t) -> p h t", h=HG),
                                           ACT.Copy).then_inc(c["pTe"], 1)
                        if b < nb:
                            act.wait_ge(c["sub"], g * 4 * GB + 4 * b + i + 1)
                            act.activation(cprobs[0:S, i, :, :], cprobs[0:S, i, :, :],
                                           ACT.Exp).then_inc(c["exp"], 1)
                take_hi(1)
                act.wait_ge(c["top"], g + 1)
                act.activation(rt["p"][0:tm, 0:nt, :], rt["p"][0:tm, 0:nt, :],
                               ACT.Exp).then_inc(c["rexp"], 1)
                for k in range(4):
                    act.wait_ge(c["mT"], g * 4 + k + 1)
                    act.activation(msk[:, k, 0:gs], ps[:, 2 + k % 2, 0:gs],
                                   ACT.Copy).then_inc(c["mTe"], 1)
                for i in range(4):
                    act.wait_ge(c["am"], g * 4 + i + 1)
                    act.activation(am_hi[:, i, 0:gs], tmp[:, i, 0:gs], ACT.Copy).then_inc(c["ahi"], 1)
                for j in range(FC):
                    def half_h(i, jj):
                        n = g * 3 * FC + 3 * jj + i + 1
                        act.wait_ge(c["h"], n)
                        if i == 0:
                            act.activation(hb_hi[:, jj, 0:gs], hh[:, 0, 0:gs],
                                           ACT.Copy).then_inc(c["hhi"], 1)
                        else:
                            if jj:
                                act.wait_ge(c["ad"], g * FC + jj)
                            act.activation(hs_hi[:, i - 1, 0:gs], hh[:, i, 0:gs],
                                           ACT.Copy).then_inc(c["hhi"], 1)

                    act.wait_ge(c["base"], g * 2 * FC + 2 * j + 1)
                    if j:
                        act.wait_ge(c["gs"], g * 2 * FC + 2 * j)
                    act.activation(gb[:, 0:gs], ps[:, 0, 0:gs], ACT.Copy).then_inc(c["gb"], 1)
                    if j:
                        act.wait_ge(c["h"], g * 3 * FC + 3 * (j - 1) + 1)
                    act.activation(gate[:, 0, 0:gs], ps[:, 0, 0:gs], ACT.Silu,
                                   scale=1 / (X_SCALE * W_SCALE)).then_inc(c["sg0"], 1)
                    if j:
                        half_h(1, j - 1)
                        half_h(2, j - 1)
                    act.wait_ge(c["base"], g * 2 * FC + 2 * j + 2)
                    if j:
                        act.wait_ge(c["us"], g * 2 * FC + 2 * j)
                    act.activation(ub[:, 0:gs], ps[:, 1, 0:gs], ACT.Copy,
                                   scale=H_SCALE / (X_SCALE * W_SCALE)).then_inc(c["ub"], 1)
                    half_h(0, j)
                    for i in (1, 2):
                        act.wait_ge(c["gs"], g * 2 * FC + 2 * j + i)
                        act.activation(gate[:, i, 0:gs], gate[:, i, 0:gs], ACT.Silu,
                                       scale=1 / (X_SCALE * W_SCALE)).then_inc(c["sgs"], 1)
                half_h(1, FC - 1)
                half_h(2, FC - 1)
                act.wait_ge(c["dsum"], g + 1)
                act.activation(d_hi[:, 0:gs], tmp[:, 0, 0:gs], ACT.Copy).then_inc(c["dhi"], 1)

            with act.Fori(0, FULL) as g:
                layer(g, GB)
            if REST:
                layer(FULL, REST)

        @block.vector
        def _(dve):
            dve.wait_ge(s["scales"], 32)
            dve.tensor_tensor(qks[:, 2:3], qks[:, 0:1], qks[:, 1:2], ALU.mult).then_inc(s["qks"], 1)
            for n, (m, hg) in enumerate(PIECES):
                dve.wait_ge(s["whi"], n + 1)
                dve.scalar_tensor_tensor(out=piece(m, hg, False), in0=stage_a[:, n % 2, :, :],
                                         scalar=W_SCALE, in1=piece(m, hg, True), op0=ALU.mult,
                                         op1=ALU.subtract).then_inc(s["wlo"], 1)

            def group(g, nb):
                nt, tm = tiles_of(nb)
                proj, turn, wo_at = plans[nb]
                b_step, b_qk, b_t = g * N_STEP, g * N_QK, g * NT

                def mean_square(u):
                    i = u % 2
                    dve.wait_ge(s["sq"], b_qk + u + 1)
                    dve.tensor_reduce(ss[0:tm, i, :], sq[0:tm, :, :], AX.X, ALU.add).then_inc(s["ss"], 1)
                    dve.wait_ge(s["ss"], b_qk + u + 1)
                    dve.tensor_scalar(ms[0:tm, i, :], ss[0:tm, i, :], 1.0 / D,
                                      1e-6 * (X_SCALE * W_SCALE) ** 2, ALU.mult,
                                      ALU.add).then_inc(s["ms"], 1)

                def scale_qk(u):
                    i = u % 2
                    dve.wait_ge(s["rr"], b_qk + u + 1)
                    dve.tensor_tensor(qk[0:tm, i, :, :], qk[0:tm, i, :, :],
                                      rr[0:tm, i, :].unsqueeze(2).to_broadcast([tm, 2 * HG, D]),
                                      ALU.mult).then_inc(s["qkn"], 1)

                def take_kT(u):
                    dve.wait_ge(s["qkT"], b_qk + u + 1)
                    t = u % nt
                    dve.tensor_copy(qkT[:, 1, :, t * tm:(t + 1) * tm],
                                    ps_T[:, 1, 0:HG * tm].rearrange("p (h t) -> p h t", h=HG)
                                    ).then_inc(s["kTe"], 1)

                def add_wo(w):
                    t = w % nt
                    dve.wait_ge(s["w"], b_qk + w + 1)
                    if w == 0:
                        dve.wait_ge(s["xres"], (g + 1) * 16)
                    dve.wait_ge(s["add"], b_qk + w)
                    dve.scalar_tensor_tensor(out=xres[0:tm, t, :], in0=ps_vw[0:tm, :],
                                             scalar=1.0 / (V_SCALE * W_SCALE), in1=xres[0:tm, t, :],
                                             op0=ALU.mult, op1=ALU.add).then_inc(s["add"], 1)

                dve.wait_ge(s["xin"], (g + 1) * 16)
                for t in range(nt):
                    dve.bn_stats(bst[0:tm, t, :], xin[0:tm, t, :]).then_inc(s["bst"], 1)
                dve.wait_ge(s["bst"], b_t + nt)
                dve.memset(var[0:tm, 0:nt], 0.0)
                for t in range(nt):
                    dve.bn_aggr(mv[0:tm, t, :], bst[0:tm, t, :]).then_inc(s["mv"], 1)
                dve.wait_ge(s["mv"], b_t + nt)
                dve.tensor_scalar(var[0:tm, 0:nt], mv[0:tm, 0:nt, 1], 1e-5, 1 / X_SCALE ** 2, ALU.add,
                                  ALU.mult).then_inc(s["var"], 1)
                dve.wait_ge(s["rstd"], g + 1)
                for t in range(nt):
                    dve.tensor_scalar(xin[0:tm, t, :], xin[0:tm, t, :], mv[0:tm, t, 0:1],
                                      rstd[0:tm, t:t + 1], ALU.subtract,
                                      ALU.mult).then_inc(s["xn"], 1)
                for t in range(nt):
                    dve.wait_ge(s["xhi"], b_t + t + 1)
                    dve.tensor_tensor(xT_lo[:, :, t * tm:(t + 1) * tm],
                                      ps_T[:, t % 2, 0:KC * tm].rearrange("p (c t) -> p c t", c=KC),
                                      xT_hi[:, :, t * tm:(t + 1) * tm],
                                      ALU.subtract).then_inc(s["xlo"], 1)
                for u in range(nt):
                    mean_square(u)
                    scale_qk(u)
                    if u:
                        take_kT(u - 1)
                for n in range(NHG * nb + 1):
                    if n:
                        for w in wo_at[n - 1]:
                            add_wo(w)
                    if n < NHG * nb:
                        sc = ps_s[0:S, 0:HG * S].rearrange("p (h t) -> p h t", h=HG)
                        dve.wait_ge(s["s"], b_step + n + 1)
                        dve.tensor_reduce(mx[0:S, :], sc, AX.X, ALU.max).then_inc(s["mx"], 1)
                        dve.wait_ge(s["mx"], b_step + n + 1)
                        dve.wait_ge(s["pTp"], b_step + max(n - 1, 0))
                        dve.tensor_tensor(probs[0:S, n % 2, :, :], sc,
                                          mx[0:S, :].unsqueeze(2).to_broadcast([S, HG, S]),
                                          ALU.subtract).then_inc(s["sub"], 1)
                    for u in (proj[n - 1] if n else []):
                        mean_square(u)
                    if n < NHG * nb:
                        dve.wait_ge(s["exp"], b_step + n + 1)
                        dve.tensor_reduce(den[0:S, :], probs[0:S, n % 2, :, :], AX.X,
                                          ALU.add).then_inc(s["den"], 1)
                        dve.wait_ge(s["den"], b_step + n + 1)
                        dve.wait_ge(s["norm"], b_step + n)
                        dve.reciprocal(rden[0:S, :], den[0:S, :]).then_inc(s["rden"], 1)
                    for u in (proj[n - 1] if n else []):
                        scale_qk(u)
                    if n:
                        b = (n - 1) % nb
                        dve.wait_ge(s["ohi"], b_step + n)
                        dve.tensor_tensor(oT_lo[:, :, b * S:(b + 1) * S],
                                          ps_o[:, 0:HG * S].rearrange("p (h t) -> p h t", h=HG),
                                          oT_hi[:, :, b * S:(b + 1) * S],
                                          ALU.subtract).then_inc(s["olo"], 1)
                    for u in turn[n]:
                        take_kT(u)
                for w in wo_at[NHG * nb]:
                    add_wo(w)

            with dve.Fori(0, FULL) as g:
                group(g, GB)
            if REST:
                group(FULL, REST)

            for n, (hi, lo, _, chunks, width) in enumerate(B_PIECES):
                dve.wait_ge(c["whi"], n + 1)
                dve.scalar_tensor_tensor(out=lo, in0=stage_b[:, n % 2, 0:chunks * width],
                                         scalar=W_SCALE, in1=hi, op0=ALU.mult,
                                         op1=ALU.subtract).then_inc(c["wlo"], 1)

            def layer(g, nb):
                nt, tm = tiles_of(nb)
                gs = nb * S

                def norm_rows(k):
                    bst, mv, var, rstd = stats
                    n0 = g * 2 * NT + k * nt
                    for t in range(nt):
                        dve.bn_stats(bst[0:tm, t, :], y[0:tm, t, :]).then_inc(c["bst"], 1)
                    dve.wait_ge(c["bst"], n0 + nt)
                    dve.memset(var[0:tm, 0:nt], 0.0)
                    for t in range(nt):
                        dve.bn_aggr(mv[0:tm, t, :], bst[0:tm, t, :]).then_inc(c["mv"], 1)
                    dve.wait_ge(c["mv"], n0 + nt)
                    dve.tensor_scalar(var[0:tm, 0:nt], mv[0:tm, 0:nt, 1], 1e-5, 1 / X_SCALE ** 2,
                                      ALU.add, ALU.mult).then_inc(c["var"], 1)
                    dve.wait_ge(c["rstd"], g * 2 + k + 1)
                    for t in range(nt):
                        dve.tensor_scalar(yn[0:tm, t, :], y[0:tm, t, :], mv[0:tm, t, 0:1],
                                          rstd[0:tm, t:t + 1], ALU.subtract,
                                          ALU.mult).then_inc(c["yn"], 1)
                    for t in range(nt):
                        dve.wait_ge(c["lnhi"], n0 + t + 1)
                        dve.tensor_tensor(yT_lo[:, :, t * tm:(t + 1) * tm],
                                          ps[:, 6 + t % 2, 0:KC * tm].rearrange(
                                              "p (c t) -> p c t", c=KC),
                                          yT_hi[:, :, t * tm:(t + 1) * tm],
                                          ALU.subtract).then_inc(c["lnlo"], 1)

                dve.wait_ge(c["y"], (g + 1) * 16)
                norm_rows(0)
                for m in range(KC):
                    dve.wait_ge(c["ck"], g * KC + m + 1)
                    dve.tensor_copy(ckT[:, m, 0:gs], ps[:, 4 + m % 2, 0:gs]).then_inc(c["cke"], 1)
                for b in range(nb + 2):
                    if b >= 2:
                        dve.wait_ge(c["ohi"], g * GB + b - 1)
                        dve.tensor_tensor(coT_lo[:, :, (b - 2) * S:(b - 1) * S],
                                          ps[:, 6 + b % 2, 0:KC * S].rearrange("p (c t) -> p c t", c=KC),
                                          coT_hi[:, :, (b - 2) * S:(b - 1) * S],
                                          ALU.subtract).then_inc(c["olo"], 1)
                    if b < nb:
                        for i in range(4):
                            n = g * 4 * GB + 4 * b + i
                            sc = ps[0:S, i, 0:HG * S].rearrange("p (h t) -> p h t", h=HG)
                            dve.wait_ge(c["sc"], n + 1)
                            dve.tensor_reduce(cmx[0:S, i, :], sc, AX.X, ALU.max).then_inc(c["mx"], 1)
                            if b:
                                dve.wait_ge(c["pT"], n - 3)
                            dve.wait_ge(c["mx"], n + 1)
                            dve.tensor_tensor(cprobs[0:S, i, :, :], sc,
                                              cmx[0:S, i, :].unsqueeze(2).to_broadcast([S, HG, S]),
                                              ALU.subtract).then_inc(c["sub"], 1)
                    if 1 <= b <= nb:
                        dve.wait_ge(c["pv"], g * 4 * GB + 4 * b)
                        dve.wait_ge(c["oT"], g * GB + max(b - 2, 0))
                        dve.tensor_tensor(on[0:S, :].rearrange("p (h d) -> p h d", h=H),
                                          ps[0:S, 5, :].rearrange("p (h d) -> p h d", h=H),
                                          crden[0:S, (b - 1) % 2, :].unsqueeze(2).to_broadcast(
                                              [S, H, CD]), ALU.mult).then_inc(c["on"], 1)
                    if b < nb:
                        for i in range(4):
                            dve.wait_ge(c["exp"], g * 4 * GB + 4 * b + i + 1)
                            dve.tensor_reduce(cden[0:S, b % 2, i::4], cprobs[0:S, i, :, :], AX.X,
                                              ALU.add).then_inc(c["den"], 1)
                        dve.wait_ge(c["den"], g * 4 * GB + 4 * b + 4)
                        dve.reciprocal(crden[0:S, b % 2, :], cden[0:S, b % 2, :]).then_inc(c["rden"], 1)
                        dve.wait_ge(c["rden"], g * GB + b + 1)
                for t in range(nt):
                    dve.wait_ge(c["w"], g * NT + t + 1)
                    dve.scalar_tensor_tensor(out=y[0:tm, t, :], in0=ps[0:tm, 6 + t % 2, :],
                                             scalar=1 / (CV_SCALE * W_SCALE), in1=y[0:tm, t, :],
                                             op0=ALU.mult, op1=ALU.add).then_inc(c["x2"], 1)
                dve.wait_ge(c["x2"], g * NT + nt)
                norm_rows(1)

                dve.wait_ge(c["rl"], g + 1)
                chain = [g * LINKS]

                def link(ins):
                    ins.then_inc(c["chain"], 1)
                    chain[0] = chain[0] + 1
                    dve.wait_ge(c["chain"], chain[0])

                def wide(name):
                    return col[name][0:tm, 0:nt].unsqueeze(2).to_broadcast([tm, nt, NE])

                lg, p, a, z = (rt[n][0:tm, 0:nt, :] for n in "lpab")
                link(dve.tensor_scalar(lg, ps[0:tm, 4, 0:nt * NE].rearrange("p (t e) -> p t e", e=NE),
                                       1 / (X_SCALE * W_SCALE), None, ALU.mult))
                link(dve.tensor_reduce(col["m"][0:tm, 0:nt], lg, AX.X, ALU.max))
                dve.tensor_tensor(p, lg, wide("m"), ALU.subtract).then_inc(c["top"], 1)
                dve.wait_ge(c["rexp"], g + 1)
                link(dve.tensor_reduce(col["d"][0:tm, 0:nt], p, AX.X, ALU.add))
                link(dve.reciprocal(col["r"][0:tm, 0:nt], col["d"][0:tm, 0:nt]))
                link(dve.tensor_tensor(p, p, wide("r"), ALU.mult))
                for k, w in enumerate(("w1", "w2")):
                    link(dve.tensor_reduce(col[w][0:tm, 0:nt], p, AX.X, ALU.max))
                    link(dve.tensor_tensor(a, p, wide(w), ALU.is_equal))
                    link(dve.tensor_tensor(a, a, rank[0:tm, 0:nt, :], ALU.mult))
                    link(dve.tensor_reduce(col["m"][0:tm, 0:nt], a, AX.X, ALU.max))
                    link(dve.tensor_tensor(sel[0:tm, k, 0:nt, :], a, wide("m"), ALU.is_equal))
                    link(dve.tensor_tensor(sel[0:tm, 2 + k, 0:nt, :], sel[0:tm, k, 0:nt, :], wide(w),
                                           ALU.mult))
                    if k == 0:
                        link(dve.scalar_tensor_tensor(out=p, in0=sel[0:tm, 0, 0:nt, :], scalar=-2.0,
                                                      in1=p, op0=ALU.mult, op1=ALU.add))
                for k in range(4):
                    dve.tensor_copy(spread[0:tm, 0:nt, k, :, :],
                                    sel[0:tm, k, 0:nt, :].unsqueeze(3).to_broadcast([tm, nt, NE, R])
                                    ).then_inc(c["spread"], 1)

                for i in range(4):
                    if i == 0:
                        dve.wait_ge(c["mTe"], g * 4 + 4)
                        dve.wait_ge(c["a"], g * 2 + 2)
                    dve.scalar_tensor_tensor(out=tmp[:, i, 0:gs], in0=ps[:, i // 2, 0:gs],
                                             scalar=X_SCALE * LORA / (X_SCALE * W_SCALE),
                                             in1=msk[:, i % 2, 0:gs], op0=ALU.mult,
                                             op1=ALU.mult).then_inc(c["am"], 1)
                for i in range(4):
                    dve.wait_ge(c["ahi"], g * 4 + i + 1)
                    dve.tensor_tensor(am_lo[:, i, 0:gs], tmp[:, i, 0:gs], am_hi[:, i, 0:gs],
                                      ALU.subtract).then_inc(c["alo"], 1)
                def lo_h(i, j):
                    dve.wait_ge(c["hhi"], g * 3 * FC + 3 * j + i + 1)
                    hi = hb_hi[:, j, 0:gs] if i == 0 else hs_hi[:, i - 1, 0:gs]
                    lo = hb_lo[:, j, 0:gs] if i == 0 else hs_lo[:, i - 1, 0:gs]
                    dve.tensor_tensor(lo, hh[:, i, 0:gs], hi, ALU.subtract).then_inc(c["hlo"], 1)

                for j in range(FC):
                    if j:
                        lo_h(1, j - 1)
                        lo_h(2, j - 1)
                    for i in (1, 2):
                        dve.wait_ge(c["lora"], g * 4 * FC + 4 * j + 2 * i)
                        dve.wait_ge(c["gb"], g * FC + j + 1)
                        if j:
                            dve.wait_ge(c["h"], g * 3 * FC + 3 * (j - 1) + i + 1)
                        dve.tensor_tensor(gate[:, i, 0:gs], ps[:, 2 * i, 0:gs], gb[:, 0:gs],
                                          ALU.add).then_inc(c["gs"], 1)
                        dve.wait_ge(c["ub"], g * FC + j + 1)
                        dve.scalar_tensor_tensor(out=up[:, i - 1, 0:gs], in0=ps[:, 2 * i + 1, 0:gs],
                                                 scalar=H_SCALE / (X_SCALE * W_SCALE),
                                                 in1=ub[:, 0:gs], op0=ALU.mult,
                                                 op1=ALU.add).then_inc(c["us"], 1)
                        if i == 1:
                            lo_h(0, j)
                lo_h(1, FC - 1)
                lo_h(2, FC - 1)
                dve.wait_ge(c["ad"], g * FC + FC)
                for i in range(2):
                    dve.scalar_tensor_tensor(out=tmp[:, i, 0:gs], in0=ps[:, 6 + i, 0:gs],
                                             scalar=LORA / W_SCALE, in1=msk[:, 2 + i, 0:gs],
                                             op0=ALU.mult, op1=ALU.mult).then_inc(c["dt"], 1)
                dve.wait_ge(c["dt"], g * 2 + 2)
                dve.tensor_tensor(tmp[:, 0, 0:gs], tmp[:, 0, 0:gs], tmp[:, 1, 0:gs],
                                  ALU.add).then_inc(c["dsum"], 1)
                dve.wait_ge(c["dhi"], g + 1)
                dve.tensor_tensor(d_lo[:, 0:gs], tmp[:, 0, 0:gs], d_hi[:, 0:gs],
                                  ALU.subtract).then_inc(c["dlo"], 1)
                for t in range(nt):
                    dve.wait_ge(c["yp"], g * NT + t + 1)
                    dve.scalar_tensor_tensor(out=y[0:tm, t, :], in0=ps[0:tm, t, :],
                                             scalar=1 / (H_SCALE * W_SCALE), in1=y[0:tm, t, :],
                                             op0=ALU.mult, op1=ALU.add).then_inc(c["add"], 1)

            with dve.Fori(0, FULL) as g:
                layer(g, GB)
            if REST:
                layer(FULL, REST)

        @block.tensor
        def _(pe):
            pe.wait_ge(s["ident"], 1)
            pe.wait_ge(s["wlo"], len(PIECES))

            def three(out_ap, pairs, first=True):
                mm = None
                for i, (ah, al, bh, bl) in enumerate(pairs):
                    pe.matmul(out_ap, ah, bh, start=(i == 0), stop=False)
                    pe.matmul(out_ap, ah, bl, start=False, stop=False)
                    mm = pe.matmul(out_ap, al, bh, start=False, stop=(i == len(pairs) - 1))
                return mm

            def group(g, nb):
                nt, tm = tiles_of(nb)
                proj, turn, wo_at = plans[nb]
                b_step, b_qk, b_t = g * N_STEP, g * N_QK, g * NT

                def project_qk(u):
                    hg, t = u // nt, u % nt
                    if hg == 0:
                        pe.wait_ge(s["xlo"], b_t + t + 1)
                    pe.wait_ge(s["raw"], b_qk + u)
                    for m in range(2):
                        mm = three(ps_qk[0:tm, m, :], [
                            (xT_hi[:, c, t * tm:(t + 1) * tm], xT_lo[:, c, t * tm:(t + 1) * tm],
                             wqkv_hi[:, c, m, hg * 512:(hg + 1) * 512],
                             wqkv_lo[:, c, m, hg * 512:(hg + 1) * 512]) for c in range(KC)])
                    mm.then_inc(s["qkp"], 1)

                def turn_qk(u):
                    pe.wait_ge(s["qkn"], b_qk + u + 1)
                    pe.wait_ge(s["qTe"], b_qk + u)
                    pe.wait_ge(s["kTe"], b_qk + u)
                    for m in range(2):
                        for h in range(HG):
                            mm = pe.transpose(ps_T[:, m, h * tm:(h + 1) * tm],
                                              qk[0:tm, u % 2, m * HG + h, :], ident[0:tm, 0:tm])
                    mm.then_inc(s["qkT"], 1)

                def project_out(w, n):
                    hg, t = w // nt, w % nt
                    pe.wait_ge(s["olo"], b_step + n)
                    pe.wait_ge(s["add"], b_qk + w)
                    pe.wait_ge(s["ve"], b_step + min(n + 1, NHG * nb))
                    three(ps_vw[0:tm, :], [
                        (oT_hi[:, h, t * tm:(t + 1) * tm], oT_lo[:, h, t * tm:(t + 1) * tm],
                         wo_hi[:, hg * HG + h, :], wo_lo[:, hg * HG + h, :])
                        for h in range(HG)]).then_inc(s["w"], 1)

                pe.wait_ge(s["qTe"], b_qk)
                pe.wait_ge(s["kTe"], b_qk)
                for t in range(nt):
                    pe.wait_ge(s["xn"], b_t + t + 1)
                    if t >= 2:
                        pe.wait_ge(s["xlo"], b_t + t - 1)
                    for c in range(KC):
                        mm = pe.transpose(ps_T[:, t % 2, c * tm:(c + 1) * tm],
                                          xin[0:tm, t, c * P:(c + 1) * P], ident[0:tm, 0:tm])
                    mm.then_inc(s["lnT"], 1)
                for u in range(nt):
                    project_qk(u)
                    if u:
                        turn_qk(u - 1)
                wo_done = 0
                for n in range(NHG * nb + 1):
                    hg, b = n // nb, n % nb
                    if n < NHG * nb:
                        u = hg * nt + -(-S * (b + 1) // tm)
                        pe.wait_ge(s["qTe"], b_qk + u)
                        pe.wait_ge(s["kTe"], b_qk + u)
                        pe.wait_ge(s["sub"], b_step + n)
                        for h in range(HG):
                            mm = pe.matmul(ps_s[0:S, h * S:(h + 1) * S],
                                           qkT[:, 0, h, b * S:(b + 1) * S],
                                           qkT[:, 1, h, b * S:(b + 1) * S], start=True, stop=True)
                        mm.then_inc(s["s"], 1)
                    if n:
                        pe.wait_ge(s["norm"], b_step + n)
                        pe.wait_ge(s["pTe"], b_step + n - 1)
                        for h in range(HG):
                            mm = pe.transpose(ps_pT[0:S, h * S:(h + 1) * S],
                                              probs[0:S, (n - 1) % 2, h, :], ident[0:S, 0:S])
                        mm.then_inc(s["pTp"], 1)
                    if n < NHG * nb:
                        pe.wait_ge(s["ve"], b_step + n)
                        pe.wait_ge(s["add"], b_qk + wo_done)
                        three(ps_vw[0:S, :], [
                            (xT_hi[:, c, b * S:(b + 1) * S], xT_lo[:, c, b * S:(b + 1) * S],
                             wqkv_hi[:, c, 2, hg * 512:(hg + 1) * 512],
                             wqkv_lo[:, c, 2, hg * 512:(hg + 1) * 512])
                            for c in range(KC)]).then_inc(s["vp"], 1)
                    if n:
                        pe.wait_ge(s["pTe"], b_step + n)
                        pe.wait_ge(s["ve"], b_step + n)
                        pe.wait_ge(s["olo"], b_step + n - 1)
                        for h in range(HG):
                            mm = pe.matmul(ps_o[:, h * S:(h + 1) * S],
                                           v[0:S, (n - 1) % 2, h * D:(h + 1) * D],
                                           pT[0:S, h, :], start=True, stop=True)
                        mm.then_inc(s["o"], 1)
                    for u in turn[n]:
                        turn_qk(u)
                    for u in proj[n]:
                        project_qk(u)
                    for w in wo_at[n]:
                        project_out(w, n)
                        wo_done += 1

            with pe.Fori(0, FULL) as g:
                group(g, GB)
            if REST:
                group(FULL, REST)

            pe.wait_ge(c["wlo"], len(B_PIECES))
            pe.wait_ge(c["wkv"], 16)
            pe.wait_ge(c["mask"], 4)
            pe.wait_ge(c["rank"], NE)

            def layer(g, nb):
                nt, tm = tiles_of(nb)
                gs = nb * S

                def turn_rows(k):
                    for t in range(nt):
                        pe.wait_ge(c["yn"], g * 2 * NT + k * nt + t + 1)
                        if t >= 2:
                            pe.wait_ge(c["lnlo"], g * 2 * NT + k * nt + t - 1)
                        for e in range(KC):
                            mm = pe.transpose(ps[:, 6 + t % 2, e * tm:(e + 1) * tm],
                                              yn[0:tm, t, e * P:(e + 1) * P], ident[0:tm, 0:tm])
                        mm.then_inc(c["lnT"], 1)

                def wide(out_ap, w_hi, w_lo, a, b):
                    return three(out_ap, [(w_hi[:, e, a:b], w_lo[:, e, a:b],
                                           yT_hi[:, e, 0:gs], yT_lo[:, e, 0:gs]) for e in range(KC)])

                turn_rows(0)
                pe.wait_ge(c["lnlo"], g * 2 * NT + nt)
                for m in range(KC):
                    wide(ps[:, m, 0:gs], cwq_hi, cwq_lo, m * P, (m + 1) * P).then_inc(c["qp"], 1)
                pe.wait_ge(c["ctx"], (g + 1) * 16)
                for m in range(KC):
                    if m >= 2:
                        pe.wait_ge(c["cke"], g * KC + m - 1)
                    pe.matmul(ps[:, 4 + m % 2, 0:gs], cwkv[:, m * P:(m + 1) * P], ctxT[:, 0:gs],
                              start=True, stop=True).then_inc(c["ck"], 1)
                for b in range(nb):
                    if b >= 2:
                        pe.wait_ge(c["ve"], g * GB + b - 1)
                    pe.matmul(ps[0:S, 6 + b % 2, :], ctxT[:, b * S:(b + 1) * S], cwkv[:, E:2 * E],
                              start=True, stop=True).then_inc(c["v"], 1)
                pe.wait_ge(c["qpe"], g * KC + KC)
                pe.wait_ge(c["cke"], g * KC + KC)
                for b in range(nb + 2):
                    if b < nb:
                        for i in range(4):
                            pe.wait_ge(c["sub"], g * 4 * GB + max(4 * (b - 1) + i + 1, 0))
                            pe.matmul(ps[0:S, i, 0:HG * S], ident16[0:S, 0:S],
                                      mask[0:S, :, :].rearrange("p h k -> p (h k)"),
                                      start=True, stop=False)
                        for m in range(KC):
                            for i in range(4):
                                r0 = i * CD
                                mm = pe.matmul(ps[0:S, i, m * S:(m + 1) * S],
                                               qpT[r0:r0 + CD, m, b * S:(b + 1) * S],
                                               ckT[r0:r0 + CD, m, b * S:(b + 1) * S],
                                               start=False, stop=(m == KC - 1))
                                if m == KC - 1:
                                    mm.then_inc(c["sc"], 1)
                    if b >= 2:
                        pe.wait_ge(c["on"], g * GB + b - 1)
                        pe.wait_ge(c["ve"], g * GB + nb)
                        if b >= 4:
                            pe.wait_ge(c["olo"], g * GB + b - 3)
                        for e in range(KC):
                            mm = pe.transpose(ps[:, 6 + b % 2, e * S:(e + 1) * S],
                                              on[0:S, e * P:(e + 1) * P], ident[0:S, 0:S])
                        mm.then_inc(c["oT"], 1)
                    if 1 <= b <= nb:
                        def mix(i):
                            n = 4 * (b - 1) + i
                            pe.wait_ge(c["pTe"], g * 4 * GB + n + 1)
                            if i == 0:
                                pe.wait_ge(c["on"], g * GB + b - 1)
                                pe.wait_ge(c["ve"], g * GB + nb)
                            for m in range(KC):
                                h = 4 * m + i
                                mm = pe.matmul(ps[0:S, 5, h * CD:(h + 1) * CD], cpT[0:S, n % 2, m, :],
                                               cv[0:S, b - 1, h * CD:(h + 1) * CD],
                                               start=True, stop=True)
                            mm.then_inc(c["pv"], 1)

                        for i in range(4):
                            n = 4 * (b - 1) + i
                            pe.wait_ge(c["exp"], g * 4 * GB + n + 1)
                            pe.wait_ge(c["pTe"], g * 4 * GB + n)
                            for m in range(KC):
                                mm = pe.transpose(ps[0:S, 4, m * S:(m + 1) * S],
                                                  cprobs[0:S, i, m, :], ident[0:S, 0:S])
                            mm.then_inc(c["pT"], 1)
                            if i:
                                mix(i - 1)
                        mix(3)
                pe.wait_ge(c["olo"], g * GB + nb)
                for t in range(nt):
                    if t >= 2:
                        pe.wait_ge(c["x2"], g * NT + t - 1)
                    three(ps[0:tm, 6 + t % 2, :], [
                        (coT_hi[:, e, t * tm:(t + 1) * tm], coT_lo[:, e, t * tm:(t + 1) * tm],
                         cwo_hi[:, e, :], cwo_lo[:, e, :]) for e in range(KC)]).then_inc(c["w"], 1)
                turn_rows(1)
                pe.wait_ge(c["lnlo"], g * 2 * NT + 2 * nt)
                for t in range(nt):
                    mm = three(ps[0:tm, 4, t * NE:(t + 1) * NE], [
                        (yT_hi[:, e, t * tm:(t + 1) * tm], yT_lo[:, e, t * tm:(t + 1) * tm],
                         wr_hi[:, e, :], wr_lo[:, e, :]) for e in range(KC)])
                mm.then_inc(c["rl"], 1)
                wide(ps[:, 0, 0:gs], ag_hi, ag_lo, 0, P).then_inc(c["a"], 1)
                wide(ps[:, 1, 0:gs], au_hi, au_lo, 0, P).then_inc(c["a"], 1)
                for k in range(4):
                    pe.wait_ge(c["spread"], g * 4 + k + 1)
                    if k >= 2:
                        pe.wait_ge(c["mTe"], g * 4 + k - 1)
                    for t in range(nt):
                        mm = pe.transpose(ps[:, 2 + k % 2, t * tm:(t + 1) * tm],
                                          spread[0:tm, t, k, :, :].rearrange("p e r -> p (e r)"),
                                          ident[0:tm, 0:tm])
                    mm.then_inc(c["mT"], 1)

                def down_factors(j):
                    pe.wait_ge(c["hlo"], g * 3 * FC + 3 * j + 3)
                    for i in range(2):
                        pe.matmul(ps[:, 6 + i, 0:gs], ad_hi[:, j, :], hs_hi[:, i, 0:gs],
                                  start=(j == 0), stop=False)
                        pe.matmul(ps[:, 6 + i, 0:gs], ad_hi[:, j, :], hs_lo[:, i, 0:gs],
                                  start=False, stop=False)
                        mm = pe.matmul(ps[:, 6 + i, 0:gs], ad_lo[:, j, :], hs_hi[:, i, 0:gs],
                                       start=False, stop=(j == FC - 1))
                    mm.then_inc(c["ad"], 1)

                pe.wait_ge(c["am"], g * 4 + 4)
                for j in range(FC):
                    f0, f1 = j * P, (j + 1) * P
                    if j:
                        pe.wait_ge(c["sg0"], g * FC + j)
                        pe.wait_ge(c["gb"], g * FC + j)
                    wide(ps[:, 0, 0:gs], wg_hi, wg_lo, f0, f1).then_inc(c["base"], 1)
                    if j:
                        pe.wait_ge(c["ub"], g * FC + j)
                    wide(ps[:, 1, 0:gs], wu_hi, wu_lo, f0, f1).then_inc(c["base"], 1)
                    if j == 0:
                        pe.wait_ge(c["alo"], g * 4 + 4)
                    for i in range(2):
                        if j:
                            pe.wait_ge(c["gs"], g * 2 * FC + 2 * (j - 1) + i + 1)
                            pe.wait_ge(c["us"], g * 2 * FC + 2 * (j - 1) + i + 1)
                        three(ps[:, 2 + 2 * i, 0:gs], [(bg_hi[:, f0:f1], bg_lo[:, f0:f1],
                              am_hi[:, i, 0:gs], am_lo[:, i, 0:gs])]).then_inc(c["lora"], 1)
                        three(ps[:, 3 + 2 * i, 0:gs], [(bu_hi[:, f0:f1], bu_lo[:, f0:f1],
                              am_hi[:, 2 + i, 0:gs], am_lo[:, 2 + i, 0:gs])]).then_inc(c["lora"], 1)
                    if j:
                        down_factors(j - 1)
                down_factors(FC - 1)
                pe.wait_ge(c["gs"], g * 2 * FC + 2 * FC)
                pe.wait_ge(c["us"], g * 2 * FC + 2 * FC)
                for t in range(nt):
                    a, b = t * tm, (t + 1) * tm
                    if t == 0:
                        pe.wait_ge(c["dlo"], g + 1)
                    three(ps[0:tm, t, :],
                          [(hb_hi[:, j, a:b], hb_lo[:, j, a:b], wd_hi[:, j, :], wd_lo[:, j, :])
                           for j in range(FC)]
                          + [(d_hi[:, a:b], d_lo[:, a:b], bd_hi[:, :], bd_lo[:, :])]
                          ).then_inc(c["yp"], 1)

            with pe.Fori(0, FULL) as g:
                layer(g, GB)
            if REST:
                layer(FULL, REST)


def kernel(x, ctx_512, L0_attn_wq, L0_attn_wk, L0_attn_wv, L0_attn_wo, L0_attn_q_scale,
           L0_attn_k_scale, L0_xattn_Wq, L0_xattn_Wkv_expand, L0_xattn_Wout, L0_ffn_Wg, L0_ffn_Wu,
           L0_ffn_Wd, L0_ffn_Wr, L0_ffn_Ag, L0_ffn_Bg, L0_ffn_Au, L0_ffn_Bu, L0_ffn_Ad, L0_ffn_Bd):
    import concourse.bacc as bacc
    from concourse.bass_utils import run_bass_kernel_spmd

    def rows(w):
        return np.asarray(w).reshape(-1, np.asarray(w).shape[-1])

    B = x.shape[0]
    laid = {
        "x": rows(x),
        "wq": np.asarray(L0_attn_wq).reshape(E, H * D),
        "wk": np.asarray(L0_attn_wk).reshape(E, H * D),
        "wv": np.asarray(L0_attn_wv).reshape(E, H * D),
        "wo": np.asarray(L0_attn_wo).reshape(H * D, E),
        "q_scale": np.asarray(L0_attn_q_scale).reshape(D, 1),
        "k_scale": np.asarray(L0_attn_k_scale).reshape(D, 1),
        "ctxT": np.asarray(ctx_512).transpose(0, 2, 1),
        "cwq": np.asarray(L0_xattn_Wq).T,
        "cwkv": np.asarray(L0_xattn_Wkv_expand).T,
        "cwo": np.asarray(L0_xattn_Wout).T,
        "wg": np.asarray(L0_ffn_Wg).T,
        "wu": np.asarray(L0_ffn_Wu).T,
        "wd": np.asarray(L0_ffn_Wd).T,
        "ag": rows(L0_ffn_Ag).T,
        "au": rows(L0_ffn_Au).T,
        "ad": rows(L0_ffn_Ad).T,
        "bg": rows(np.asarray(L0_ffn_Bg).transpose(0, 2, 1)),
        "bu": rows(np.asarray(L0_ffn_Bu).transpose(0, 2, 1)),
        "bd": rows(np.asarray(L0_ffn_Bd).transpose(0, 2, 1)),
        "wr": np.asarray(L0_ffn_Wr).T,
    }
    nc = bacc.Bacc("TRN2", target_bir_lowering=False, num_devices=1)
    laid = {n: np.ascontiguousarray(a) for n, a in laid.items()}
    args = [nc.dram_tensor(f"in_{n}", a.shape, F32, kind="ExternalInput").ap()
            for n, a in laid.items()]
    args.append(nc.dram_tensor("x1", (B * S, E), F32, kind="Internal").ap())
    args.append(nc.dram_tensor("out", (B * S, E), F32, kind="ExternalOutput").ap())
    decoder_layer(nc, *args)
    r = run_bass_kernel_spmd(nc, [{f"in_{n}": a for n, a in laid.items()}], core_ids=[0])
    return r.results[0]["out"].reshape(x.shape)
```

```python
from contextlib import ExitStack

import numpy as np

import concourse.bass as bass
from concourse import mybir

ALU = mybir.AluOpType
ACT = mybir.ActivationFunctionType
AX = mybir.AxisListType
F32 = mybir.dt.float32
F16 = mybir.dt.float16
BF16 = mybir.dt.bfloat16

P = 128
S = 100
E = 512
KC = E // P
H = 16
D = 128
HG = 4
NHG = H // HG
GB = 5
X_SCALE = 16.0
W_SCALE = 64.0
V_SCALE = 8.0


F = 1408
FC = F // P
NE = 8
R = 16
L = 128
CD = E // H
CV_SCALE = 32.0
H_SCALE = 8.0
LORA = 2.0
MEM = 53200


def tiles_of(nb):
    n = -(-nb * S // P)
    assert nb * S % n == 0
    return n, nb * S // n


class Tile:

    def __init__(self, count, hg, t, tm, ahead):
        self.count, self.hg, self.t, self.tm, self.ahead = count, hg, t, tm, ahead
        self.cols = slice(t * tm, (t + 1) * tm)


def first_tiles(nb, count, ahead):
    nt, tm = tiles_of(nb)
    return [Tile(count + t, 0, t, tm, ahead) for t in range(nt)]


def attention_plan(nb, nxt):
    nt, tm = tiles_of(nb)
    steps = NHG * nb
    proj, turn, wo = ([[] for _ in range(steps)] for _ in range(3))
    for hg in range(NHG):
        if hg + 1 < NHG:
            tiles = [Tile((hg + 1) * nt + t, hg + 1, t, tm, False) for t in range(nt)]
        else:
            tiles = first_tiles(nxt, NHG * nt, True) if nxt else []
        for tile in tiles:
            at = hg * nb + (tile.t if nb > nt else 0)
            proj[at].append(tile)
            turn[at + (nb > nt)].append(tile)
        for t in range(nt):
            last = -(-(t + 1) * tm // S) - 1
            wo[min(hg * nb + last + 1, steps - 1)].append(hg * nt + t)
    return proj, turn, wo


def decoder_layer(nc, x, wq, wk, wv, wo, q_scale, k_scale, ctxT_in, cwq, cwkv_in, cwo, wg, wu, wd,
                  ag, au, ad, bg, bu, bd, wr, x1, out):
    NB = x.shape[0] // S
    FULL, REST = NB // GB, NB % GB
    NT, TM = tiles_of(GB)
    GS = GB * S

    with ExitStack() as ctx:
        def sb(name, shape, dt):
            return ctx.enter_context(nc.sbuf_tensor(name, shape, dt))

        def sem(name):
            return ctx.enter_context(nc.semaphore(name))

        mem = sb("mem", [P, MEM], F32)

        class Cut:

            def __init__(self, at):
                self.at = at

            def __call__(self, shape, dt=F32):
                n = int(np.prod(shape))
                words = n if dt == F32 else (n + 1) // 2
                ap = mem[:, self.at:self.at + words]
                self.at += words
                assert self.at <= MEM, self.at
                if dt != F32:
                    ap = ap.bitcast(dt)
                names = "abcd"[:len(shape)]
                sizes = {k: v for k, v in zip(names, shape)}
                return ap.rearrange(f"p ({' '.join(names)}) -> p {' '.join(names)}", **sizes)

        cut = Cut(0)
        ident = cut([P])
        ident16 = cut([P], BF16)
        mask = cut([HG, S], BF16)
        half = cut([16])
        qks = cut([4])
        rank = cut([NT, NE])
        phase_start = cut.at

        wqkv_hi = cut([KC, 3, H * D], F16)
        wqkv_lo = cut([KC, 3, H * D], F16)
        wo_hi = cut([H, E], F16)
        wo_lo = cut([H, E], F16)
        xin = cut([NT, E])
        xres = cut([NT, E])
        xT_hi = cut([KC, GS], F16)
        xT_lo = cut([KC, GS], F16)
        xTn_hi = cut([KC, GS], F16)
        xTn_lo = cut([KC, GS], F16)
        stage_a = Cut(cut.at)([2, KC, 512])
        qkT = cut([2, HG, GS + 12])[:, :, :, 0:GS]
        oT_hi = cut([HG, GS], F16)
        oT_lo = cut([HG, GS], F16)
        v = cut([2, HG * D])
        qk = cut([2, 2 * HG, D])
        sq = cut([2 * HG, D])
        probs = cut([2, HG, S])
        pT = cut([HG, S])
        bst = cut([NT, 6])
        mv = cut([NT, 2])
        var = cut([NT])
        rstd = cut([NT])
        ss = cut([2, 2 * HG])
        ms = cut([2, 2 * HG])
        rr = cut([2, 2 * HG])
        mx = cut([HG])
        den = cut([HG])
        rden = cut([HG])

        cut = Cut(phase_start)
        cwq_hi, cwq_lo = cut([KC, E], F16), cut([KC, E], F16)
        cwo_hi, cwo_lo = cut([KC, E], F16), cut([KC, E], F16)
        cwkv = cut([2 * E])
        wg_hi, wg_lo = cut([KC, F], F16), cut([KC, F], F16)
        wu_hi, wu_lo = cut([KC, F], F16), cut([KC, F], F16)
        wd_hi, wd_lo = cut([FC, E], F16), cut([FC, E], F16)
        ag_hi, ag_lo = cut([KC, P], F16), cut([KC, P], F16)
        au_hi, au_lo = cut([KC, P], F16), cut([KC, P], F16)
        ad_hi, ad_lo = cut([FC, P], F16), cut([FC, P], F16)
        bg_hi, bg_lo = cut([F], F16), cut([F], F16)
        bu_hi, bu_lo = cut([F], F16), cut([F], F16)
        bd_hi, bd_lo = cut([E], F16), cut([E], F16)
        wr_hi, wr_lo = cut([KC, NE], F16), cut([KC, NE], F16)
        stats = [cut([NT, 6]), cut([NT, 2]), cut([NT]), cut([NT])]
        y = cut([NT, E])
        yT_hi, yT_lo = cut([KC, GS], F16), cut([KC, GS], F16)
        part_start = cut.at
        stage_b = Cut(part_start)([2, 2048])
        yn = cut([NT, E])
        ctxT = cut([GS])
        hb_hi, hb_lo = cut([FC, GS], F16), cut([FC, GS], F16)
        d_hi, d_lo = cut([GS], F16), cut([GS], F16)
        shared_end = cut.at
        qpT = cut([KC, GS])
        ckT = cut([KC, GS])
        cv = cut([GB, E])
        cprobs = cut([4, HG, S])
        cpT = cut([2, HG, S])
        cmx = cut([4, HG])
        cden = cut([2, H])
        crden = cut([2, H])
        on = cut([E])
        coT_hi, coT_lo = cut([KC, GS], F16), cut([KC, GS], F16)
        cut = Cut(shared_end)
        am_hi, am_lo = cut([4, GS], F16), cut([4, GS], F16)
        msk = cut([4, GS])
        gb = cut([GS])
        ub = cut([GS])
        gate = cut([3, GS])
        up = cut([2, GS])
        hh = cut([3, GS])
        hs_hi, hs_lo = cut([2, GS], F16), cut([2, GS], F16)
        tmp = cut([4, GS])
        spread = yn[:, :, :].rearrange("p t (k e r) -> p t k e r", k=4, e=NE)
        rt = {n: cut([NT, NE]) for n in ("l", "p", "a", "b")}
        col = {n: cut([NT]) for n in ("m", "d", "r", "w1", "w2")}
        sel = cut([4, NT, NE])

        ps = ctx.enter_context(nc.psum_tensor("ps", [P, 8, 512], F32))
        ps_qk, ps_T = ps[:, 0:2, :], ps[:, 2:4, :]
        ps_vw, ps_s, ps_pT, ps_o = (ps[:, b, :] for b in range(4, 8))

        names = ("ident0 ident half scales wld0 wld1 whi wlo qkl qks "
                 "xin xres bst mv var rstd xn lnT xhi xlo "
                 "xTc qkp raw sq ss ms rr qkn qkT qTe kTe vp ve s mx sub exp den rden norm pTp pTe "
                 "o ohi olo w add x1")
        s = {n: sem("s_" + n) for n in names.split()}
        names = ("wld0 wld1 whi wlo wkv mask rank y yn_in ctx out bst mv var rstd yn lnT lnhi lnlo "
                 "qp qpe ck cke v ve sc mx sub exp den rden pT pTe pv on oT ohi olo w x2 "
                 "rl lg top rexp chain spread mT mTe a am ahi alo base gb sg0 ub lora gs us sgs "
                 "h hhi hlo ad dt dsum dhi dlo yp add")
        c = {n: sem("c_" + n) for n in names.split()}
        block = ctx.enter_context(nc.Block())

        N_STEP, N_QK = NHG * GB, NHG * NT
        STATS_AT, NORM_AT, TURN_AT = N_STEP - 11, N_STEP - 10, (N_STEP - 8, N_STEP - 7)

        def turned_at(n, nxt):
            return [t for t in range(tiles_of(nxt)[0]) if n == TURN_AT[t // 2]] if nxt else []

        def over_groups(eng, group):
            with eng.Fori(0, FULL - 1) as g:
                group(g, GB, GB)
            group(FULL - 1, GB, REST)
            if REST:
                group(FULL, REST, 0)

        LN_STATS_CHUNK, LN_ROWS_CHUNK = FC - 5, FC - 4
        OUT_STEPS = (0, 1, 2, 4)

        def out_tiles(b, nb, last_nb):
            if not last_nb:
                return []
            steps = OUT_STEPS if nb > 2 else (0, 1, 2, 3)
            return [t for t in range(tiles_of(last_nb)[0]) if steps[t] == b]

        w_src = [w.rearrange("(c p) n -> p c n", p=P) for w in (wq, wk, wv)]
        wo_src = wo.rearrange("(h d) n -> d h n", d=D)
        PIECES = [(m, hg) for hg in range(NHG) for m in range(4)]

        B_PIECES = []

        def flat(ap):
            return ap if len(ap.shape) == 2 else ap.rearrange("p a b -> p (a b)")

        def add_pieces(hi, lo, src, chunks, width):
            step = max(1, 2048 // width)
            src = src.rearrange("(c p) n -> p c n", p=P)
            for a in range(0, chunks, step):
                b = min(chunks, a + step)
                B_PIECES.append((flat(hi)[:, a * width:b * width], flat(lo)[:, a * width:b * width],
                                 src[:, a:b, :], (b - a), width))

        add_pieces(cwq_hi, cwq_lo, cwq, KC, E)
        add_pieces(cwo_hi, cwo_lo, cwo, KC, E)
        add_pieces(wr_hi, wr_lo, wr, KC, NE)
        add_pieces(ag_hi, ag_lo, ag, KC, P)
        add_pieces(au_hi, au_lo, au, KC, P)
        add_pieces(wg_hi, wg_lo, wg, KC, F)
        add_pieces(wu_hi, wu_lo, wu, KC, F)
        add_pieces(bg_hi, bg_lo, bg, 1, F)
        add_pieces(bu_hi, bu_lo, bu, 1, F)
        add_pieces(ad_hi, ad_lo, ad, FC, P)
        add_pieces(wd_hi, wd_lo, wd, FC, E)
        add_pieces(bd_hi, bd_lo, bd, 1, E)
        GROUPS = FULL + (REST > 0)
        N_ALL_QK = FULL * NHG * NT + (NHG * tiles_of(REST)[0] if REST else 0)
        LINKS = 18

        def piece(m, hg, hi):
            if m < 3:
                return (wqkv_hi if hi else wqkv_lo)[:, :, m, hg * 512:(hg + 1) * 512]
            return (wo_hi if hi else wo_lo)[:, hg * HG:(hg + 1) * HG, :]

        @block.sync
        def _(sp):
            sp.dma_start(qks[:, 0:1], q_scale).then_inc(s["scales"], 16)
            sp.dma_start(qks[:, 1:2], k_scale).then_inc(s["scales"], 16)

            def rows_of(dram, t0, nb):
                nt, tm = tiles_of(nb)
                return dram[bass.ds(t0, nt * tm), :].rearrange("(t p) e -> p t e", p=tm)

            def load(buffer, src, nb, signal):
                nt, tm = tiles_of(nb)
                sp.dma_start(buffer[0:tm, 0:nt, :], src).then_inc(s[signal], 16)

            def group(g, nb, nxt):
                nt, tm = tiles_of(nb)
                t0 = sp.snap(g * GS) if nxt == GB else g * GS
                ahead = rows_of(x[GS:, :], t0, nxt) if nxt else None
                if nxt:
                    sp.wait_ge(s["lnT"], g * NT + nt)
                    load(xin, ahead, nxt, "xin")
                sp.wait_ge(s["add"], g * N_QK + NHG * nt)
                b0 = sp.snap(g * GB) if nxt == GB else g * GB
                sp.dma_start(rows_of(x1, b0 * S, nb), xres[0:tm, 0:nt, :]).then_inc(s["x1"], 16)
                sp.wait_ge(s["x1"], g * 16 + 16)
                if nxt:
                    load(xres, ahead, nxt, "xres")

            load(xin, rows_of(x, 0, GB), GB, "xin")
            load(xres, rows_of(x, 0, GB), GB, "xres")
            for n, (m, hg) in enumerate(PIECES):
                if n >= 2:
                    sp.wait_ge(s["wlo"], n - 1)
                src = (w_src[m][:, :, hg * 512:(hg + 1) * 512] if m < 3
                       else wo_src[:, hg * HG:(hg + 1) * HG, :])
                sp.dma_start(stage_a[:, n % 2, :, :], src).then_inc(s[f"wld{n % 2}"], 16)
            over_groups(sp, group)

            sp.dma_start(cwkv[:, :], cwkv_in).then_inc(c["wkv"], 16)
            for n, (_, _, src, chunks, width) in enumerate(B_PIECES):
                if n >= 2:
                    sp.wait_ge(c["wlo"], n - 1)
                sp.dma_start(stage_b[:, n % 2, 0:chunks * width].rearrange(
                    "p (c n) -> p c n", c=chunks), src).then_inc(c[f"wld{n % 2}"], 16)

            def keys_of(b0, nb, skip=0):
                return ctxT_in[skip:, :, 0:S][bass.ds(b0, nb), :, :].rearrange("b l k -> l b k")

            def load_rows(buffer, src, nb, signal):
                nt, tm = tiles_of(nb)
                sp.dma_start(buffer[0:tm, 0:nt, :], src).then_inc(c[signal], 16)

            def load_keys(src, nb):
                sp.dma_start(ctxT[:, 0:nb * S].rearrange("l (b k) -> l b k", b=nb),
                             src).then_inc(c["ctx"], 16)

            def layer(g, nb, nxt):
                nt, tm = tiles_of(nb)
                t0 = sp.snap(g * GS) if nxt == GB else g * GS
                b0 = sp.snap(g * GB) if nxt == GB else g * GB
                if nxt:
                    ahead, keys = rows_of(x1[GS:, :], t0, nxt), keys_of(b0, nxt, GB)
                    sp.wait_ge(c["v"], g * GB + nb)
                    load_keys(keys, nxt)
                    sp.wait_ge(c["mT"], g * 4 + 4)
                    load_rows(yn, ahead, nxt, "yn_in")
                sp.wait_ge(c["add"], g * NT + nt)
                b0 = sp.snap(g * GB) if nxt == GB else g * GB
                sp.dma_start(rows_of(out, b0 * S, nb), y[0:tm, 0:nt, :]).then_inc(c["out"], 16)
                sp.wait_ge(c["out"], g * 16 + 16)
                if nxt:
                    load_rows(y, ahead, nxt, "y")

            sp.wait_ge(c["wlo"], len(B_PIECES))
            load_rows(yn, rows_of(x1, 0, GB), GB, "yn_in")
            load_keys(keys_of(0, GB), GB)
            load_rows(y, rows_of(x1, 0, GB), GB, "y")
            over_groups(sp, layer)

        @block.gpsimd
        def _(pool):
            pool.memset(half[:, :], -0.5).then_inc(s["half"], 1)
            pool.memset(ident[:, :], 0.0).then_inc(s["ident0"], 1)
            pool.wait_ge(s["ident0"], 1)
            pool.affine_select(out=ident[:, :], in_=ident[:, :], compare_op=ALU.not_equal, fill=1.0,
                               base=0, pattern=[[-1, P]], channel_multiplier=1).then_inc(s["ident"], 1)
            pool.wait_ge(s["half"], 1)
            pool.memset(ident16[:, :], 0.0).then_inc(c["mask"], 1)
            pool.memset(mask[:, :, :], 0.0).then_inc(c["mask"], 1)
            pool.wait_ge(c["mask"], 2)
            pool.affine_select(out=ident16[:, :], in_=ident16[:, :], compare_op=ALU.not_equal,
                               fill=1.0, base=0, pattern=[[-1, P]],
                               channel_multiplier=1).then_inc(c["mask"], 1)
            pool.affine_select(out=mask[0:S, :, :], in_=mask[0:S, :, :], compare_op=ALU.is_ge,
                               fill=-1e30, base=0, pattern=[[0, HG], [-1, S]],
                               channel_multiplier=1).then_inc(c["mask"], 1)
            for e in range(NE):
                pool.memset(rank[:, :, e:e + 1], float(NE - e)).then_inc(c["rank"], 1)

            def ln_power(g, nb):
                nt, tm = tiles_of(nb)
                pool.wait_ge(s["var"], g + 1)
                pool.tensor_tensor(rstd[0:tm, 0:nt], var[0:tm, 0:nt], half[0:tm, 0:nt],
                                   ALU.pow).then_inc(s["rstd"], 1)

            def rms_power(b_qk, tile):
                i, tm = tile.count % 2, tile.tm
                pool.wait_ge(s["ms"], b_qk + tile.count + 1)
                pool.tensor_tensor(rr[0:tm, i, :], ms[0:tm, i, :], half[0:tm, 0:2 * HG],
                                   ALU.pow).then_inc(s["rr"], 1)

            def norm(b_step, n):
                pool.wait_ge(s["rden"], b_step + n + 1)
                pool.tensor_tensor(probs[0:S, n % 2, :, :], probs[0:S, n % 2, :, :],
                                   rden[0:S, :].unsqueeze(2).to_broadcast([S, HG, S]),
                                   ALU.mult).then_inc(s["norm"], 1)

            def group(g, nb, nxt):
                proj, _, _ = attention_plan(nb, nxt)
                b_step, b_qk, steps = g * N_STEP, g * N_QK, NHG * nb
                for n in range(steps):
                    for tile in (proj[n - 1] if n else []):
                        if nb > tiles_of(nb)[0]:
                            rms_power(b_qk, tile)
                    if n + 1 < steps or nxt:
                        norm(b_step, n + 1)
                    if nb == tiles_of(nb)[0]:
                        for tile in proj[n]:
                            rms_power(b_qk, tile)
                    if nxt and n == STATS_AT:
                        ln_power(g + 1, nxt)

            ln_power(0, GB)
            for tile in first_tiles(GB, 0, True):
                rms_power(0, tile)
            norm(0, 0)
            over_groups(pool, group)

            def power(a, b, tm, count):
                pool.wait_ge(c["var"], count)
                pool.tensor_tensor(stats[3][0:tm, a:b], stats[2][0:tm, a:b], half[0:tm, a:b],
                                   ALU.pow).then_inc(c["rstd"], 1)

            def layer(g, nb, nxt):
                gs = nb * S
                for j in range(FC):
                    for i in range(3):
                        if i == 0:
                            pool.wait_ge(c["sg0"], g * FC + j + 1)
                            pool.wait_ge(c["ub"], g * FC + j + 1)
                        else:
                            pool.wait_ge(c["sgs"], g * 2 * FC + 2 * j + i)
                            pool.wait_ge(c["us"], g * 2 * FC + 2 * j + i)
                        if j:
                            pool.wait_ge(c["hlo"], g * 3 * FC + 3 * (j - 1) + i + 1)
                        pool.tensor_tensor(hh[:, i, 0:gs], gate[:, i, 0:gs],
                                           ub[:, 0:gs] if i == 0 else up[:, i - 1, 0:gs],
                                           ALU.mult).then_inc(c["h"], 1)
                    if nxt and j == LN_STATS_CHUNK:
                        nt, tm = tiles_of(nxt)
                        power(0, nt, tm, (g + 1) * (NT + 1) + 1)
                if nxt:
                    nt, tm = tiles_of(nxt)
                    for t in range(nt):
                        power(t, t + 1, tm, (g + 1) * (NT + 1) + t + 2)

            power(0, NT, TM, 1)
            for t in range(NT):
                power(t, t + 1, TM, t + 2)
            over_groups(pool, layer)

        @block.scalar
        def _(act):
            for n, (m, hg) in enumerate(PIECES):
                act.wait_ge(s[f"wld{n % 2}"], 16 * (n // 2 + 1))
                act.activation(piece(m, hg, True), stage_a[:, n % 2, :, :], ACT.Copy,
                               scale=W_SCALE).then_inc(s["whi"], 1)

            def rows_hi(b_t, t, tm):
                act.wait_ge(s["lnT"], b_t + t + 1)
                act.activation(xTn_hi[:, :, t * tm:(t + 1) * tm],
                               ps_T[:, t % 2, 0:KC * tm].rearrange("p (c t) -> p c t", c=KC),
                               ACT.Copy).then_inc(s["xhi"], 1)

            def take_raw(b_qk, tile):
                u, tm = tile.count, tile.tm
                src = ps_qk[0:tm, :, :].rearrange("p a (h d) -> p (a h) d", d=D)
                act.wait_ge(s["qkp"], b_qk + u + 1)
                if u:
                    act.wait_ge(s["ss"], b_qk + u)
                act.activation(sq[0:tm, :, :], src, ACT.Square).then_inc(s["sq"], 1)
                if u >= 2:
                    act.wait_ge(s["qkT"], b_qk + u - 1)
                act.activation(qk[0:tm, u % 2, :, :], src, ACT.Copy).then_inc(s["raw"], 1)

            def take_qT(b_qk, tile):
                act.wait_ge(s["qkT"], b_qk + tile.count + 1)
                act.activation(qkT[:, 0, :, tile.cols],
                               ps_T[:, 0, 0:HG * tile.tm].rearrange("p (h t) -> p h t", h=HG),
                               ACT.Copy, scale=qks[:, 2:3]).then_inc(s["qTe"], 1)

            def exponentials(b_step, n):
                act.wait_ge(s["sub"], b_step + n + 1)
                act.activation(probs[0:S, n % 2, :, :], probs[0:S, n % 2, :, :],
                               ACT.Exp).then_inc(s["exp"], 1)

            def take_v(b_step, n):
                act.wait_ge(s["vp"], b_step + n + 1)
                if n >= 2:
                    act.wait_ge(s["o"], b_step + n - 1)
                act.activation(v[0:S, n % 2, :], ps_vw[0:S, :], ACT.Copy,
                               scale=V_SCALE / (X_SCALE * W_SCALE)).then_inc(s["ve"], 1)

            def group(g, nb, nxt):
                proj, turn, _ = attention_plan(nb, nxt)
                b_step, b_qk, steps = g * N_STEP, g * N_QK, NHG * nb
                for n in range(steps):
                    b = n % nb
                    act.wait_ge(s["pTp"], b_step + n + 1)
                    if n:
                        act.wait_ge(s["o"], b_step + n)
                    act.activation(pT[0:S, :, :], ps_pT[0:S, 0:HG * S].rearrange(
                        "p (h t) -> p h t", h=HG), ACT.Copy).then_inc(s["pTe"], 1)
                    if n + 1 < steps or nxt:
                        exponentials(b_step, n + 1)
                        take_v(b_step, n + 1)
                    act.wait_ge(s["o"], b_step + n + 1)
                    act.activation(oT_hi[:, :, b * S:(b + 1) * S],
                                   ps_o[:, 0:HG * S].rearrange("p (h t) -> p h t", h=HG),
                                   ACT.Copy).then_inc(s["ohi"], 1)
                    for tile in proj[n]:
                        take_raw(b_qk, tile)
                    for tile in turn[n]:
                        take_qT(b_qk, tile)
                    for t in turned_at(n, nxt):
                        rows_hi(g * NT + NT, t, tiles_of(nxt)[1])

            for t in range(NT):
                rows_hi(0, t, TM)
            tiles = first_tiles(GB, 0, True)
            for tile in tiles:
                take_raw(0, tile)
                if tile.t:
                    take_qT(0, tiles[tile.t - 1])
            take_qT(0, tiles[-1])
            exponentials(0, 0)
            take_v(0, 0)
            over_groups(act, group)

            for n, (hi, _, _, chunks, width) in enumerate(B_PIECES):
                act.wait_ge(c[f"wld{n % 2}"], 16 * (n // 2 + 1))
                act.activation(hi, stage_b[:, n % 2, 0:chunks * width], ACT.Copy,
                               scale=W_SCALE).then_inc(c["whi"], 1)

            def rows_hi(count, t, tm, bank):
                act.wait_ge(c["lnT"], count)
                act.activation(yT_hi[:, :, t * tm:(t + 1) * tm],
                               ps[:, bank + t % 2, 0:KC * tm].rearrange("p (c t) -> p c t", c=KC),
                               ACT.Copy).then_inc(c["lnhi"], 1)

            def cross_attention(g, nb):
                nt, tm = tiles_of(nb)
                gs = nb * S
                for m in range(KC):
                    act.wait_ge(c["qp"], g * KC + m + 1)
                    act.activation(qpT[:, m, 0:gs], ps[:, m, 0:gs], ACT.Copy,
                                   scale=float(CD) ** -0.5 / (X_SCALE * W_SCALE)
                                   ).then_inc(c["qpe"], 1)
                for b in range(nb):
                    act.wait_ge(c["v"], g * GB + b + 1)
                    act.activation(cv[0:S, b, :], ps[0:S, 6 + b % 2, :], ACT.Copy,
                                   scale=CV_SCALE).then_inc(c["ve"], 1)
                for b in range(nb + 2):
                    if b >= 2:
                        act.wait_ge(c["oT"], g * GB + b - 1)
                        act.activation(coT_hi[:, :, (b - 2) * S:(b - 1) * S],
                                       ps[:, 7, 0:KC * S].rearrange("p (c t) -> p c t", c=KC),
                                       ACT.Copy).then_inc(c["ohi"], 1)
                    for i in range(4):
                        if 1 <= b <= nb:
                            r = 4 * (b - 1) + i
                            act.wait_ge(c["pT"], g * 4 * GB + r + 1)
                            if r >= 2:
                                act.wait_ge(c["pv"], g * 4 * GB + r - 1)
                            act.activation(cpT[0:S, r % 2, :, :],
                                           ps[0:S, 4 + r % 2, 0:HG * S].rearrange(
                                               "p (h t) -> p h t", h=HG),
                                           ACT.Copy).then_inc(c["pTe"], 1)
                        if b < nb:
                            act.wait_ge(c["sub"], g * 4 * GB + 4 * b + i + 1)
                            act.activation(cprobs[0:S, i, :, :], cprobs[0:S, i, :, :],
                                           ACT.Exp).then_inc(c["exp"], 1)
                for t in range(nt):
                    rows_hi(g * 2 * NT + nt + t + 1, t, tm, 6)

            def layer(g, nb, nxt):
                nt, tm = tiles_of(nb)
                gs = nb * S
                act.wait_ge(c["top"], g + 1)
                act.activation(rt["p"][0:tm, 0:nt, :], rt["p"][0:tm, 0:nt, :],
                               ACT.Exp).then_inc(c["rexp"], 1)
                for k in range(4):
                    act.wait_ge(c["mT"], g * 4 + k + 1)
                    act.activation(msk[:, k, 0:gs], ps[:, 2 + k % 2, 0:gs],
                                   ACT.Copy).then_inc(c["mTe"], 1)
                for i in range(4):
                    act.wait_ge(c["am"], g * 4 + i + 1)
                    act.activation(am_hi[:, i, 0:gs], tmp[:, i, 0:gs], ACT.Copy).then_inc(c["ahi"], 1)

                def half_h(i, jj):
                    act.wait_ge(c["h"], g * 3 * FC + 3 * jj + i + 1)
                    if i and jj:
                        act.wait_ge(c["ad"], g * FC + jj)
                    act.activation(hb_hi[:, jj, 0:gs] if i == 0 else hs_hi[:, i - 1, 0:gs],
                                   hh[:, i, 0:gs], ACT.Copy).then_inc(c["hhi"], 1)

                for j in range(FC):
                    act.wait_ge(c["base"], g * 2 * FC + 2 * j + 1)
                    if j:
                        act.wait_ge(c["gs"], g * 2 * FC + 2 * j)
                    act.activation(gb[:, 0:gs], ps[:, 0, 0:gs], ACT.Copy).then_inc(c["gb"], 1)
                    if j:
                        act.wait_ge(c["h"], g * 3 * FC + 3 * (j - 1) + 1)
                    act.activation(gate[:, 0, 0:gs], ps[:, 0, 0:gs], ACT.Silu,
                                   scale=1 / (X_SCALE * W_SCALE)).then_inc(c["sg0"], 1)
                    if j:
                        half_h(1, j - 1)
                        half_h(2, j - 1)
                    act.wait_ge(c["base"], g * 2 * FC + 2 * j + 2)
                    if j:
                        act.wait_ge(c["us"], g * 2 * FC + 2 * j)
                    act.activation(ub[:, 0:gs], ps[:, 1, 0:gs], ACT.Copy,
                                   scale=H_SCALE / (X_SCALE * W_SCALE)).then_inc(c["ub"], 1)
                    half_h(0, j)
                    for i in (1, 2):
                        act.wait_ge(c["gs"], g * 2 * FC + 2 * j + i)
                        act.activation(gate[:, i, 0:gs], gate[:, i, 0:gs], ACT.Silu,
                                       scale=1 / (X_SCALE * W_SCALE)).then_inc(c["sgs"], 1)
                half_h(1, FC - 1)
                half_h(2, FC - 1)
                if nxt:
                    for t in range(tiles_of(nxt)[0]):
                        rows_hi((g + 1) * 2 * NT + t + 1, t, tiles_of(nxt)[1], 2)
                act.wait_ge(c["dsum"], g + 1)
                act.activation(d_hi[:, 0:gs], tmp[:, 0, 0:gs], ACT.Copy).then_inc(c["dhi"], 1)
                if nxt:
                    cross_attention(g + 1, nxt)

            for t in range(NT):
                rows_hi(t + 1, t, TM, 2)
            cross_attention(0, GB)
            over_groups(act, layer)

        @block.vector
        def _(dve):
            dve.wait_ge(s["scales"], 32)
            dve.tensor_tensor(qks[:, 2:3], qks[:, 0:1], qks[:, 1:2], ALU.mult).then_inc(s["qks"], 1)
            for n, (m, hg) in enumerate(PIECES):
                dve.wait_ge(s["whi"], n + 1)
                dve.scalar_tensor_tensor(out=piece(m, hg, False), in0=stage_a[:, n % 2, :, :],
                                         scalar=W_SCALE, in1=piece(m, hg, True), op0=ALU.mult,
                                         op1=ALU.subtract).then_inc(s["wlo"], 1)

            def ln_stats(g, nb):
                nt, tm = tiles_of(nb)
                dve.wait_ge(s["xin"], g * 16 + 16)
                for t in range(nt):
                    dve.bn_stats(bst[0:tm, t, :], xin[0:tm, t, :]).then_inc(s["bst"], 1)
                dve.wait_ge(s["bst"], g * NT + nt)
                dve.memset(var[0:tm, 0:nt], 0.0)
                for t in range(nt):
                    dve.bn_aggr(mv[0:tm, t, :], bst[0:tm, t, :]).then_inc(s["mv"], 1)
                dve.wait_ge(s["mv"], g * NT + nt)
                dve.tensor_scalar(var[0:tm, 0:nt], mv[0:tm, 0:nt, 1], 1e-5, 1 / X_SCALE ** 2, ALU.add,
                                  ALU.mult).then_inc(s["var"], 1)

            def ln_rows(g, nb):
                nt, tm = tiles_of(nb)
                dve.wait_ge(s["rstd"], g + 1)
                for t in range(nt):
                    dve.tensor_scalar(xin[0:tm, t, :], xin[0:tm, t, :], mv[0:tm, t, 0:1],
                                      rstd[0:tm, t:t + 1], ALU.subtract,
                                      ALU.mult).then_inc(s["xn"], 1)

            def rows_lo(b_t, t, tm):
                dve.wait_ge(s["xhi"], b_t + t + 1)
                dve.tensor_tensor(xTn_lo[:, :, t * tm:(t + 1) * tm],
                                  ps_T[:, t % 2, 0:KC * tm].rearrange("p (c t) -> p c t", c=KC),
                                  xTn_hi[:, :, t * tm:(t + 1) * tm],
                                  ALU.subtract).then_inc(s["xlo"], 1)

            def next_rows(b_t, nb):
                cols = slice(0, nb * S)
                dve.wait_ge(s["xlo"], b_t + tiles_of(nb)[0])
                dve.tensor_copy(xT_hi[:, :, cols], xTn_hi[:, :, cols]).then_inc(s["xTc"], 1)
                dve.tensor_copy(xT_lo[:, :, cols], xTn_lo[:, :, cols]).then_inc(s["xTc"], 1)

            def mean_square(b_qk, tile):
                u, i, tm = tile.count, tile.count % 2, tile.tm
                dve.wait_ge(s["sq"], b_qk + u + 1)
                dve.tensor_reduce(ss[0:tm, i, :], sq[0:tm, :, :], AX.X, ALU.add).then_inc(s["ss"], 1)
                dve.wait_ge(s["ss"], b_qk + u + 1)
                dve.tensor_scalar(ms[0:tm, i, :], ss[0:tm, i, :], 1.0 / D,
                                  1e-6 * (X_SCALE * W_SCALE) ** 2, ALU.mult,
                                  ALU.add).then_inc(s["ms"], 1)

            def scale_qk(b_qk, tile):
                u, i, tm = tile.count, tile.count % 2, tile.tm
                dve.wait_ge(s["rr"], b_qk + u + 1)
                dve.wait_ge(s["raw"], b_qk + u + 1)
                dve.tensor_tensor(qk[0:tm, i, :, :], qk[0:tm, i, :, :],
                                  rr[0:tm, i, :].unsqueeze(2).to_broadcast([tm, 2 * HG, D]),
                                  ALU.mult).then_inc(s["qkn"], 1)

            def take_kT(b_qk, tile):
                dve.wait_ge(s["qkT"], b_qk + tile.count + 1)
                dve.tensor_copy(qkT[:, 1, :, tile.cols],
                                ps_T[:, 1, 0:HG * tile.tm].rearrange("p (h t) -> p h t", h=HG)
                                ).then_inc(s["kTe"], 1)

            def subtract_max(b_step, n):
                sc = ps_s[0:S, 0:HG * S].rearrange("p (h t) -> p h t", h=HG)
                dve.wait_ge(s["s"], b_step + n + 1)
                dve.tensor_reduce(mx[0:S, :], sc, AX.X, ALU.max).then_inc(s["mx"], 1)
                if n >= 2:
                    dve.wait_ge(s["pTp"], b_step + n - 1)
                dve.wait_ge(s["mx"], b_step + n + 1)
                dve.tensor_tensor(probs[0:S, n % 2, :, :], sc,
                                  mx[0:S, :].unsqueeze(2).to_broadcast([S, HG, S]),
                                  ALU.subtract).then_inc(s["sub"], 1)

            def inverse_sum(b_step, n):
                dve.wait_ge(s["exp"], b_step + n + 1)
                dve.tensor_reduce(den[0:S, :], probs[0:S, n % 2, :, :], AX.X,
                                  ALU.add).then_inc(s["den"], 1)
                if n:
                    dve.wait_ge(s["norm"], b_step + n)
                dve.wait_ge(s["den"], b_step + n + 1)
                dve.reciprocal(rden[0:S, :], den[0:S, :]).then_inc(s["rden"], 1)

            def add_wo(b_qk, w, t, tm):
                dve.wait_ge(s["w"], b_qk + w + 1)
                if w:
                    dve.wait_ge(s["add"], b_qk + w)
                dve.scalar_tensor_tensor(out=xres[0:tm, t, :], in0=ps_vw[0:tm, :],
                                         scalar=1.0 / (V_SCALE * W_SCALE), in1=xres[0:tm, t, :],
                                         op0=ALU.mult, op1=ALU.add).then_inc(s["add"], 1)

            def group(g, nb, nxt):
                nt, tm = tiles_of(nb)
                proj, turn, wo_at = attention_plan(nb, nxt)
                b_step, b_qk, steps = g * N_STEP, g * N_QK, NHG * nb
                for n in range(steps):
                    for w in (wo_at[n - 1] if n else []):
                        if w == 0:
                            dve.wait_ge(s["xres"], g * 16 + 16)
                        add_wo(b_qk, w, w % nt, tm)
                    if n + 1 < steps or nxt:
                        subtract_max(b_step, n + 1)
                    ready = proj[n - 1] if n and nb > nt else []
                    for tile in ready:
                        mean_square(b_qk, tile)
                    if n + 1 < steps or nxt:
                        inverse_sum(b_step, n + 1)
                    for tile in ready:
                        scale_qk(b_qk, tile)
                    b = n % nb
                    dve.wait_ge(s["ohi"], b_step + n + 1)
                    dve.tensor_tensor(oT_lo[:, :, b * S:(b + 1) * S],
                                      ps_o[:, 0:HG * S].rearrange("p (h t) -> p h t", h=HG),
                                      oT_hi[:, :, b * S:(b + 1) * S],
                                      ALU.subtract).then_inc(s["olo"], 1)
                    if nb == nt:
                        for tile in proj[n]:
                            mean_square(b_qk, tile)
                            scale_qk(b_qk, tile)
                    if nxt and n == STATS_AT:
                        ln_stats(g + 1, nxt)
                    if nxt and n == NORM_AT:
                        ln_rows(g + 1, nxt)
                    if nxt and n == steps - 2:
                        dve.wait_ge(s["vp"], b_step + steps)
                        next_rows(g * NT + NT, nxt)
                    for tile in turn[n]:
                        take_kT(b_qk, tile)
                    for t in turned_at(n, nxt):
                        rows_lo(g * NT + NT, t, tiles_of(nxt)[1])
                for w in wo_at[steps - 1]:
                    add_wo(b_qk, w, w % nt, tm)

            ln_stats(0, GB)
            ln_rows(0, GB)
            for t in range(NT):
                rows_lo(0, t, TM)
            next_rows(0, GB)
            tiles = first_tiles(GB, 0, True)
            for tile in tiles:
                mean_square(0, tile)
                scale_qk(0, tile)
                if tile.t:
                    take_kT(0, tiles[tile.t - 1])
            take_kT(0, tiles[-1])
            subtract_max(0, 0)
            inverse_sum(0, 0)
            over_groups(dve, group)

            for n, (hi, lo, _, chunks, width) in enumerate(B_PIECES):
                dve.wait_ge(c["whi"], n + 1)
                dve.scalar_tensor_tensor(out=lo, in0=stage_b[:, n % 2, 0:chunks * width],
                                         scalar=W_SCALE, in1=hi, op0=ALU.mult,
                                         op1=ALU.subtract).then_inc(c["wlo"], 1)

            def row_stats(count, src, a, b, tm):
                bst, mv, var, _ = stats
                for t in range(a, b):
                    dve.bn_stats(bst[0:tm, t, :], src[0:tm, t, :]).then_inc(c["bst"], 1)
                dve.wait_ge(c["bst"], count + b - a)
                dve.memset(var[0:tm, a:b], 0.0)
                for t in range(a, b):
                    dve.bn_aggr(mv[0:tm, t, :], bst[0:tm, t, :]).then_inc(c["mv"], 1)
                dve.wait_ge(c["mv"], count + b - a)
                dve.tensor_scalar(var[0:tm, a:b], mv[0:tm, a:b, 1], 1e-5, 1 / X_SCALE ** 2,
                                  ALU.add, ALU.mult).then_inc(c["var"], 1)

            def norm_row(src, t, tm, rstd_count):
                _, mv, _, rstd = stats
                dve.wait_ge(c["rstd"], rstd_count)
                dve.tensor_scalar(yn[0:tm, t, :], src[0:tm, t, :], mv[0:tm, t, 0:1],
                                  rstd[0:tm, t:t + 1], ALU.subtract, ALU.mult).then_inc(c["yn"], 1)

            def row_lo(count, t, tm, bank):
                dve.wait_ge(c["lnhi"], count)
                dve.tensor_tensor(yT_lo[:, :, t * tm:(t + 1) * tm],
                                  ps[:, bank + t % 2, 0:KC * tm].rearrange("p (c t) -> p c t", c=KC),
                                  yT_hi[:, :, t * tm:(t + 1) * tm], ALU.subtract).then_inc(c["lnlo"], 1)

            def first_stats(g, nb):
                nt, tm = tiles_of(nb)
                dve.wait_ge(c["yn_in"], g * 16 + 16)
                row_stats(g * 2 * NT, yn, 0, nt, tm)

            def first_rows(g, nb):
                nt, tm = tiles_of(nb)
                for t in range(nt):
                    norm_row(yn, t, tm, g * (NT + 1) + 1)

            def add_out(g, t, tm):
                dve.wait_ge(c["yp"], g * NT + t + 1)
                dve.scalar_tensor_tensor(out=y[0:tm, t, :], in0=ps[0:tm, 7, :],
                                         scalar=1 / (H_SCALE * W_SCALE), in1=y[0:tm, t, :],
                                         op0=ALU.mult, op1=ALU.add).then_inc(c["add"], 1)

            def cross_attention(g, nb, last_nb):
                nt, tm = tiles_of(nb)
                gs = nb * S
                for m in range(KC):
                    dve.wait_ge(c["ck"], g * KC + m + 1)
                    dve.tensor_copy(ckT[:, m, 0:gs], ps[:, 4 + m % 2, 0:gs]).then_inc(c["cke"], 1)
                for b in range(nb + 2):
                    for t in (out_tiles(b - 1, nb, last_nb) if b else []):
                        add_out(g - 1, t, tiles_of(last_nb)[1])
                    if b >= 2:
                        dve.wait_ge(c["ohi"], g * GB + b - 1)
                        dve.tensor_tensor(coT_lo[:, :, (b - 2) * S:(b - 1) * S],
                                          ps[:, 7, 0:KC * S].rearrange("p (c t) -> p c t", c=KC),
                                          coT_hi[:, :, (b - 2) * S:(b - 1) * S],
                                          ALU.subtract).then_inc(c["olo"], 1)
                    if b < nb:
                        for i in range(4):
                            n = g * 4 * GB + 4 * b + i
                            sc = ps[0:S, i, 0:HG * S].rearrange("p (h t) -> p h t", h=HG)
                            dve.wait_ge(c["sc"], n + 1)
                            dve.tensor_reduce(cmx[0:S, i, :], sc, AX.X, ALU.max).then_inc(c["mx"], 1)
                            if b:
                                dve.wait_ge(c["pT"], n - 3)
                            dve.wait_ge(c["mx"], n + 1)
                            dve.tensor_tensor(cprobs[0:S, i, :, :], sc,
                                              cmx[0:S, i, :].unsqueeze(2).to_broadcast([S, HG, S]),
                                              ALU.subtract).then_inc(c["sub"], 1)
                    if 1 <= b <= nb:
                        dve.wait_ge(c["pv"], g * 4 * GB + 4 * b)
                        if b >= 2:
                            dve.wait_ge(c["oT"], g * GB + b - 1)
                        dve.tensor_tensor(on[0:S, :].rearrange("p (h d) -> p h d", h=H),
                                          ps[0:S, 6, :].rearrange("p (h d) -> p h d", h=H),
                                          crden[0:S, (b - 1) % 2, :].unsqueeze(2).to_broadcast(
                                              [S, H, CD]), ALU.mult).then_inc(c["on"], 1)
                    if b < nb:
                        for i in range(4):
                            dve.wait_ge(c["exp"], g * 4 * GB + 4 * b + i + 1)
                            dve.tensor_reduce(cden[0:S, b % 2, i::4], cprobs[0:S, i, :, :], AX.X,
                                              ALU.add).then_inc(c["den"], 1)
                        dve.wait_ge(c["den"], g * 4 * GB + 4 * b + 4)
                        dve.reciprocal(crden[0:S, b % 2, :], cden[0:S, b % 2, :]).then_inc(c["rden"], 1)
                        dve.wait_ge(c["rden"], g * GB + b + 1)
                for t in out_tiles(nb + 1, nb, last_nb):
                    add_out(g - 1, t, tiles_of(last_nb)[1])
                dve.wait_ge(c["y"], g * 16 + 16)
                for t in range(nt):
                    dve.wait_ge(c["w"], g * NT + t + 1)
                    dve.scalar_tensor_tensor(out=y[0:tm, t, :], in0=ps[0:tm, 4 + t % 2, :],
                                             scalar=1 / (CV_SCALE * W_SCALE), in1=y[0:tm, t, :],
                                             op0=ALU.mult, op1=ALU.add).then_inc(c["x2"], 1)
                    dve.wait_ge(c["x2"], g * NT + t + 1)
                    row_stats(g * 2 * NT + nt + t, y, t, t + 1, tm)
                    if t:
                        norm_row(y, t - 1, tm, g * (NT + 1) + t + 1)
                norm_row(y, nt - 1, tm, g * (NT + 1) + nt + 1)
                for t in range(nt):
                    row_lo(g * 2 * NT + nt + t + 1, t, tm, 6)

            def layer(g, nb, nxt):
                nt, tm = tiles_of(nb)
                gs = nb * S
                dve.wait_ge(c["rl"], g + 1)
                chain = [g * LINKS]

                def link(ins):
                    ins.then_inc(c["chain"], 1)
                    chain[0] = chain[0] + 1
                    dve.wait_ge(c["chain"], chain[0])

                def wide(name):
                    return col[name][0:tm, 0:nt].unsqueeze(2).to_broadcast([tm, nt, NE])

                lg, p, a, z = (rt[n][0:tm, 0:nt, :] for n in "lpab")
                link(dve.tensor_scalar(lg, ps[0:tm, 4, 0:nt * NE].rearrange("p (t e) -> p t e", e=NE),
                                       1 / (X_SCALE * W_SCALE), None, ALU.mult))
                link(dve.tensor_reduce(col["m"][0:tm, 0:nt], lg, AX.X, ALU.max))
                dve.tensor_tensor(p, lg, wide("m"), ALU.subtract).then_inc(c["top"], 1)
                dve.wait_ge(c["rexp"], g + 1)
                link(dve.tensor_reduce(col["d"][0:tm, 0:nt], p, AX.X, ALU.add))
                link(dve.reciprocal(col["r"][0:tm, 0:nt], col["d"][0:tm, 0:nt]))
                link(dve.tensor_tensor(p, p, wide("r"), ALU.mult))
                for k, w in enumerate(("w1", "w2")):
                    link(dve.tensor_reduce(col[w][0:tm, 0:nt], p, AX.X, ALU.max))
                    link(dve.tensor_tensor(a, p, wide(w), ALU.is_equal))
                    link(dve.tensor_tensor(a, a, rank[0:tm, 0:nt, :], ALU.mult))
                    link(dve.tensor_reduce(col["m"][0:tm, 0:nt], a, AX.X, ALU.max))
                    link(dve.tensor_tensor(sel[0:tm, k, 0:nt, :], a, wide("m"), ALU.is_equal))
                    link(dve.tensor_tensor(sel[0:tm, 2 + k, 0:nt, :], sel[0:tm, k, 0:nt, :], wide(w),
                                           ALU.mult))
                    if k == 0:
                        link(dve.scalar_tensor_tensor(out=p, in0=sel[0:tm, 0, 0:nt, :], scalar=-2.0,
                                                      in1=p, op0=ALU.mult, op1=ALU.add))
                for k in range(4):
                    dve.tensor_copy(spread[0:tm, 0:nt, k, :, :],
                                    sel[0:tm, k, 0:nt, :].unsqueeze(3).to_broadcast([tm, nt, NE, R])
                                    ).then_inc(c["spread"], 1)

                for i in range(4):
                    if i == 0:
                        dve.wait_ge(c["mTe"], g * 4 + 4)
                        dve.wait_ge(c["a"], g * 2 + 2)
                    dve.scalar_tensor_tensor(out=tmp[:, i, 0:gs], in0=ps[:, i // 2, 0:gs],
                                             scalar=X_SCALE * LORA / (X_SCALE * W_SCALE),
                                             in1=msk[:, i % 2, 0:gs], op0=ALU.mult,
                                             op1=ALU.mult).then_inc(c["am"], 1)
                for i in range(4):
                    dve.wait_ge(c["ahi"], g * 4 + i + 1)
                    dve.tensor_tensor(am_lo[:, i, 0:gs], tmp[:, i, 0:gs], am_hi[:, i, 0:gs],
                                      ALU.subtract).then_inc(c["alo"], 1)
                def lo_h(i, j):
                    dve.wait_ge(c["hhi"], g * 3 * FC + 3 * j + i + 1)
                    hi = hb_hi[:, j, 0:gs] if i == 0 else hs_hi[:, i - 1, 0:gs]
                    lo = hb_lo[:, j, 0:gs] if i == 0 else hs_lo[:, i - 1, 0:gs]
                    dve.tensor_tensor(lo, hh[:, i, 0:gs], hi, ALU.subtract).then_inc(c["hlo"], 1)

                for j in range(FC):
                    if j:
                        lo_h(1, j - 1)
                        lo_h(2, j - 1)
                    for i in (1, 2):
                        dve.wait_ge(c["lora"], g * 4 * FC + 4 * j + 2 * i)
                        dve.wait_ge(c["gb"], g * FC + j + 1)
                        if j:
                            dve.wait_ge(c["h"], g * 3 * FC + 3 * (j - 1) + i + 1)
                        dve.tensor_tensor(gate[:, i, 0:gs], ps[:, 2 * i, 0:gs], gb[:, 0:gs],
                                          ALU.add).then_inc(c["gs"], 1)
                        dve.wait_ge(c["ub"], g * FC + j + 1)
                        dve.scalar_tensor_tensor(out=up[:, i - 1, 0:gs], in0=ps[:, 2 * i + 1, 0:gs],
                                                 scalar=H_SCALE / (X_SCALE * W_SCALE),
                                                 in1=ub[:, 0:gs], op0=ALU.mult,
                                                 op1=ALU.add).then_inc(c["us"], 1)
                        if i == 1:
                            lo_h(0, j)
                    if nxt and j == LN_STATS_CHUNK:
                        first_stats(g + 1, nxt)
                    if nxt and j == LN_ROWS_CHUNK:
                        first_rows(g + 1, nxt)
                lo_h(1, FC - 1)
                lo_h(2, FC - 1)
                if nxt:
                    for t in range(tiles_of(nxt)[0]):
                        row_lo((g + 1) * 2 * NT + t + 1, t, tiles_of(nxt)[1], 2)
                dve.wait_ge(c["ad"], g * FC + FC)
                for i in range(2):
                    dve.scalar_tensor_tensor(out=tmp[:, i, 0:gs], in0=ps[:, 6 + i, 0:gs],
                                             scalar=LORA / W_SCALE, in1=msk[:, 2 + i, 0:gs],
                                             op0=ALU.mult, op1=ALU.mult).then_inc(c["dt"], 1)
                dve.wait_ge(c["dt"], g * 2 + 2)
                dve.tensor_tensor(tmp[:, 0, 0:gs], tmp[:, 0, 0:gs], tmp[:, 1, 0:gs],
                                  ALU.add).then_inc(c["dsum"], 1)
                dve.wait_ge(c["dhi"], g + 1)
                dve.tensor_tensor(d_lo[:, 0:gs], tmp[:, 0, 0:gs], d_hi[:, 0:gs],
                                  ALU.subtract).then_inc(c["dlo"], 1)
                if nxt:
                    cross_attention(g + 1, nxt, nb)
                else:
                    for t in range(nt):
                        add_out(g, t, tm)

            first_stats(0, GB)
            first_rows(0, GB)
            for t in range(NT):
                row_lo(t + 1, t, TM, 2)
            cross_attention(0, GB, 0)
            over_groups(dve, layer)

        @block.tensor
        def _(pe):
            pe.wait_ge(s["ident"], 1)
            pe.wait_ge(s["wlo"], len(PIECES))

            def three(out_ap, pairs, first=True):
                mm = None
                for i, (ah, al, bh, bl) in enumerate(pairs):
                    pe.matmul(out_ap, ah, bh, start=(i == 0), stop=False)
                    pe.matmul(out_ap, ah, bl, start=False, stop=False)
                    mm = pe.matmul(out_ap, al, bh, start=False, stop=(i == len(pairs) - 1))
                return mm

            def turn_rows(b_t, t, tm, b_qk=0, turned=0):
                pe.wait_ge(s["xn"], b_t + t + 1)
                if turned:
                    pe.wait_ge(s["qTe"], b_qk + turned)
                    pe.wait_ge(s["kTe"], b_qk + turned)
                if t >= 2:
                    pe.wait_ge(s["xlo"], b_t + t - 1)
                for c_ in range(KC):
                    mm = pe.transpose(ps_T[:, t % 2, c_ * tm:(c_ + 1) * tm],
                                      xin[0:tm, t, c_ * P:(c_ + 1) * P], ident[0:tm, 0:tm])
                mm.then_inc(s["lnT"], 1)

            def project_qk(b_qk, b_t, tile):
                u, tm = tile.count, tile.tm
                hi, lo = (xTn_hi, xTn_lo) if tile.ahead else (xT_hi, xT_lo)
                cols = slice(tile.hg * 512, (tile.hg + 1) * 512)
                if tile.ahead:
                    pe.wait_ge(s["xlo"], b_t + tile.t + 1)
                if u:
                    pe.wait_ge(s["raw"], b_qk + u)
                for m in range(2):
                    mm = three(ps_qk[0:tm, m, :], [
                        (hi[:, e, tile.cols], lo[:, e, tile.cols],
                         wqkv_hi[:, e, m, cols], wqkv_lo[:, e, m, cols]) for e in range(KC)])
                mm.then_inc(s["qkp"], 1)

            def turn_qk(b_qk, tile):
                u, tm = tile.count, tile.tm
                pe.wait_ge(s["qkn"], b_qk + u + 1)
                if u:
                    pe.wait_ge(s["qTe"], b_qk + u)
                    pe.wait_ge(s["kTe"], b_qk + u)
                for m in range(2):
                    for h in range(HG):
                        mm = pe.transpose(ps_T[:, m, h * tm:(h + 1) * tm],
                                          qk[0:tm, u % 2, m * HG + h, :], ident[0:tm, 0:tm])
                mm.then_inc(s["qkT"], 1)

            def scores(b_step, b_qk, n, nb, b, u):
                pe.wait_ge(s["qTe"], b_qk + u + 1)
                pe.wait_ge(s["kTe"], b_qk + u + 1)
                if n:
                    pe.wait_ge(s["sub"], b_step + n)
                for h in range(HG):
                    mm = pe.matmul(ps_s[0:S, h * S:(h + 1) * S],
                                   qkT[:, 0, h, b * S:(b + 1) * S],
                                   qkT[:, 1, h, b * S:(b + 1) * S], start=True, stop=True)
                mm.then_inc(s["s"], 1)

            def project_v(b_step, n, hg, b):
                three(ps_vw[0:S, :], [
                    (xT_hi[:, e, b * S:(b + 1) * S], xT_lo[:, e, b * S:(b + 1) * S],
                     wqkv_hi[:, e, 2, hg * 512:(hg + 1) * 512],
                     wqkv_lo[:, e, 2, hg * 512:(hg + 1) * 512])
                    for e in range(KC)]).then_inc(s["vp"], 1)

            def group(g, nb, nxt):
                nt, tm = tiles_of(nb)
                proj, turn, wo_at = attention_plan(nb, nxt)
                b_step, b_qk, steps = g * N_STEP, g * N_QK, NHG * nb
                added = turned = rows = 0

                def turn_tiles(n):
                    nonlocal turned, rows
                    for tile in turn[n]:
                        if nxt and n > TURN_AT[0]:
                            pe.wait_ge(s["xlo"], g * NT + NT + rows)
                        turn_qk(b_qk, tile)
                        turned = tile.count + 1
                    for t in turned_at(n, nxt):
                        turn_rows(g * NT + NT, t, tiles_of(nxt)[1], b_qk, turned)
                        rows = t + 1

                for n in range(steps):
                    hg, b = (n + 1) // nb, (n + 1) % nb
                    own = n + 1 < steps
                    if own:
                        scores(b_step, b_qk, n + 1, nb, b, hg * nt + -(-S * (b + 1) // tm) - 1)
                    elif nxt:
                        scores(b_step, b_qk, steps, nxt, 0, N_QK)
                    pe.wait_ge(s["norm"], b_step + n + 1)
                    if n:
                        pe.wait_ge(s["pTe"], b_step + n)
                    for h in range(HG):
                        mm = pe.transpose(ps_pT[0:S, h * S:(h + 1) * S],
                                          probs[0:S, n % 2, h, :], ident[0:S, 0:S])
                    mm.then_inc(s["pTp"], 1)
                    if own or nxt:
                        pe.wait_ge(s["ve"], b_step + n + 1)
                        if added:
                            pe.wait_ge(s["add"], b_qk + added)
                        if own:
                            project_v(b_step, n + 1, hg, b)
                        else:
                            pe.wait_ge(s["xTc"], g * 2 + 4)
                            project_v(b_step, n + 1, 0, 0)
                    pe.wait_ge(s["pTe"], b_step + n + 1)
                    pe.wait_ge(s["ve"], b_step + n + 1)
                    if n:
                        pe.wait_ge(s["olo"], b_step + n)
                    for h in range(HG):
                        mm = pe.matmul(ps_o[:, h * S:(h + 1) * S],
                                       v[0:S, n % 2, h * D:(h + 1) * D],
                                       pT[0:S, h, :], start=True, stop=True)
                    mm.then_inc(s["o"], 1)
                    for tile in proj[n]:
                        project_qk(b_qk, g * NT + NT, tile)
                    late = nb > nt and not proj[n] and own
                    if not late:
                        turn_tiles(n)
                    for w in wo_at[n]:
                        h_, t = w // nt, w % nt
                        b_last = -(-(t + 1) * tm // S) - 1
                        pe.wait_ge(s["olo"], b_step + h_ * nb + b_last + 1)
                        pe.wait_ge(s["ve"], b_step + n + 1 + (own or nxt > 0))
                        if w:
                            pe.wait_ge(s["add"], b_qk + w)
                        three(ps_vw[0:tm, :], [
                            (oT_hi[:, h, t * tm:(t + 1) * tm], oT_lo[:, h, t * tm:(t + 1) * tm],
                             wo_hi[:, h_ * HG + h, :], wo_lo[:, h_ * HG + h, :])
                            for h in range(HG)]).then_inc(s["w"], 1)
                        added += 1
                    if late:
                        turn_tiles(n)
                if nxt:
                    pe.wait_ge(s["add"], b_qk + NHG * nt)

            for t in range(NT):
                turn_rows(0, t, TM)
            tiles = first_tiles(GB, 0, True)
            for tile in tiles:
                project_qk(0, 0, tile)
                if tile.t:
                    turn_qk(0, tiles[tile.t - 1])
            turn_qk(0, tiles[-1])
            scores(0, 0, 0, GB, 0, 0)
            pe.wait_ge(s["xTc"], 2)
            project_v(0, 0, 0, 0)
            over_groups(pe, group)

            pe.wait_ge(c["wlo"], len(B_PIECES))
            pe.wait_ge(c["wkv"], 16)
            pe.wait_ge(c["mask"], 4)
            pe.wait_ge(c["rank"], NE)

            def turn_row(count, t, tm, bank):
                pe.wait_ge(c["yn"], count + t + 1)
                if t >= 2:
                    pe.wait_ge(c["lnlo"], count + t - 1)
                for e in range(KC):
                    mm = pe.transpose(ps[:, bank + t % 2, e * tm:(e + 1) * tm],
                                      yn[0:tm, t, e * P:(e + 1) * P], ident[0:tm, 0:tm])
                mm.then_inc(c["lnT"], 1)

            def wide(out_ap, w_hi, w_lo, a, b, gs):
                return three(out_ap, [(w_hi[:, e, a:b], w_lo[:, e, a:b],
                                       yT_hi[:, e, 0:gs], yT_lo[:, e, 0:gs]) for e in range(KC)])

            def project_out(g, t, tm):
                a, b = t * tm, (t + 1) * tm
                pe.wait_ge(c["dlo"], g + 1)
                three(ps[0:tm, 7, :],
                      [(hb_hi[:, j, a:b], hb_lo[:, j, a:b], wd_hi[:, j, :], wd_lo[:, j, :])
                       for j in range(FC)]
                      + [(d_hi[:, a:b], d_lo[:, a:b], bd_hi[:, :], bd_lo[:, :])]
                      ).then_inc(c["yp"], 1)

            def cross_attention(g, nb, last_nb):
                nt, tm = tiles_of(nb)
                gs = nb * S
                pe.wait_ge(c["lnlo"], g * 2 * NT + nt)
                for m in range(KC):
                    wide(ps[:, m, 0:gs], cwq_hi, cwq_lo, m * P, (m + 1) * P, gs
                         ).then_inc(c["qp"], 1)
                pe.wait_ge(c["ctx"], g * 16 + 16)
                for m in range(KC):
                    if m >= 2:
                        pe.wait_ge(c["cke"], g * KC + m - 1)
                    pe.matmul(ps[:, 4 + m % 2, 0:gs], cwkv[:, m * P:(m + 1) * P], ctxT[:, 0:gs],
                              start=True, stop=True).then_inc(c["ck"], 1)
                if last_nb:
                    pe.wait_ge(c["dt"], g * 2)
                for b in range(nb):
                    if b >= 2:
                        pe.wait_ge(c["ve"], g * GB + b - 1)
                    pe.matmul(ps[0:S, 6 + b % 2, :], ctxT[:, b * S:(b + 1) * S], cwkv[:, E:2 * E],
                              start=True, stop=True).then_inc(c["v"], 1)
                pe.wait_ge(c["qpe"], g * KC + KC)
                pe.wait_ge(c["cke"], g * KC + KC)
                made = 0
                for b in range(nb + 2):
                    if b < nb:
                        for i in range(4):
                            if b:
                                pe.wait_ge(c["sub"], g * 4 * GB + 4 * (b - 1) + i + 1)
                            pe.matmul(ps[0:S, i, 0:HG * S], ident16[0:S, 0:S],
                                      mask[0:S, :, :].rearrange("p h k -> p (h k)"),
                                      start=True, stop=False)
                        for m in range(KC):
                            for i in range(4):
                                r0 = i * CD
                                mm = pe.matmul(ps[0:S, i, m * S:(m + 1) * S],
                                               qpT[r0:r0 + CD, m, b * S:(b + 1) * S],
                                               ckT[r0:r0 + CD, m, b * S:(b + 1) * S],
                                               start=False, stop=(m == KC - 1))
                                if m == KC - 1:
                                    mm.then_inc(c["sc"], 1)
                    if b == 0:
                        pe.wait_ge(c["ve"], g * GB + nb)
                    if b >= 2:
                        pe.wait_ge(c["on"], g * GB + b - 1)
                        if made:
                            pe.wait_ge(c["add"], (g - 1) * NT + made)
                        for e in range(KC):
                            mm = pe.transpose(ps[:, 7, e * S:(e + 1) * S],
                                              on[0:S, e * P:(e + 1) * P], ident[0:S, 0:S])
                        mm.then_inc(c["oT"], 1)
                    if 1 <= b <= nb:
                        def mix(i):
                            n = 4 * (b - 1) + i
                            pe.wait_ge(c["pTe"], g * 4 * GB + n + 1)
                            if i == 0 and b >= 2:
                                pe.wait_ge(c["on"], g * GB + b - 1)
                            for m in range(KC):
                                h = 4 * m + i
                                mm = pe.matmul(ps[0:S, 6, h * CD:(h + 1) * CD], cpT[0:S, n % 2, m, :],
                                               cv[0:S, b - 1, h * CD:(h + 1) * CD],
                                               start=True, stop=True)
                            mm.then_inc(c["pv"], 1)

                        for i in range(4):
                            n = 4 * (b - 1) + i
                            pe.wait_ge(c["exp"], g * 4 * GB + n + 1)
                            if n >= 2:
                                pe.wait_ge(c["pTe"], g * 4 * GB + n - 1)
                            for m in range(KC):
                                mm = pe.transpose(ps[0:S, 4 + n % 2, m * S:(m + 1) * S],
                                                  cprobs[0:S, i, m, :], ident[0:S, 0:S])
                            mm.then_inc(c["pT"], 1)
                            if i:
                                mix(i - 1)
                        mix(3)
                    for t in out_tiles(b, nb, last_nb):
                        if b >= 2:
                            pe.wait_ge(c["olo"], g * GB + b - 1)
                        elif made:
                            pe.wait_ge(c["add"], (g - 1) * NT + made)
                        project_out(g - 1, t, tiles_of(last_nb)[1])
                        made += 1
                pe.wait_ge(c["olo"], g * GB + nb)
                for t in range(nt):
                    if t >= 2:
                        pe.wait_ge(c["x2"], g * NT + t - 1)
                    three(ps[0:tm, 4 + t % 2, :], [
                        (coT_hi[:, e, t * tm:(t + 1) * tm], coT_lo[:, e, t * tm:(t + 1) * tm],
                         cwo_hi[:, e, :], cwo_lo[:, e, :]) for e in range(KC)]).then_inc(c["w"], 1)
                if made:
                    pe.wait_ge(c["add"], (g - 1) * NT + made)
                for t in range(nt):
                    turn_row(g * 2 * NT + nt, t, tm, 6)

            def layer(g, nb, nxt):
                nt, tm = tiles_of(nb)
                gs = nb * S
                pe.wait_ge(c["x2"], g * NT + nt)
                pe.wait_ge(c["lnlo"], g * 2 * NT + 2 * nt)
                for t in range(nt):
                    mm = three(ps[0:tm, 4, t * NE:(t + 1) * NE], [
                        (yT_hi[:, e, t * tm:(t + 1) * tm], yT_lo[:, e, t * tm:(t + 1) * tm],
                         wr_hi[:, e, :], wr_lo[:, e, :]) for e in range(KC)])
                mm.then_inc(c["rl"], 1)
                wide(ps[:, 0, 0:gs], ag_hi, ag_lo, 0, P, gs).then_inc(c["a"], 1)
                wide(ps[:, 1, 0:gs], au_hi, au_lo, 0, P, gs).then_inc(c["a"], 1)
                for k in range(4):
                    pe.wait_ge(c["spread"], g * 4 + k + 1)
                    if k >= 2:
                        pe.wait_ge(c["mTe"], g * 4 + k - 1)
                    for t in range(nt):
                        mm = pe.transpose(ps[:, 2 + k % 2, t * tm:(t + 1) * tm],
                                          spread[0:tm, t, k, :, :].rearrange("p e r -> p (e r)"),
                                          ident[0:tm, 0:tm])
                    mm.then_inc(c["mT"], 1)

                def down_factors(j):
                    pe.wait_ge(c["hlo"], g * 3 * FC + 3 * j + 3)
                    for i in range(2):
                        pe.matmul(ps[:, 6 + i, 0:gs], ad_hi[:, j, :], hs_hi[:, i, 0:gs],
                                  start=(j == 0), stop=False)
                        pe.matmul(ps[:, 6 + i, 0:gs], ad_hi[:, j, :], hs_lo[:, i, 0:gs],
                                  start=False, stop=False)
                        mm = pe.matmul(ps[:, 6 + i, 0:gs], ad_lo[:, j, :], hs_hi[:, i, 0:gs],
                                       start=False, stop=(j == FC - 1))
                    mm.then_inc(c["ad"], 1)

                pe.wait_ge(c["am"], g * 4 + 4)
                for j in range(FC):
                    f0, f1 = j * P, (j + 1) * P
                    if j:
                        pe.wait_ge(c["sg0"], g * FC + j)
                        pe.wait_ge(c["gb"], g * FC + j)
                    wide(ps[:, 0, 0:gs], wg_hi, wg_lo, f0, f1, gs).then_inc(c["base"], 1)
                    if j:
                        pe.wait_ge(c["ub"], g * FC + j)
                    wide(ps[:, 1, 0:gs], wu_hi, wu_lo, f0, f1, gs).then_inc(c["base"], 1)
                    if j == 0:
                        pe.wait_ge(c["alo"], g * 4 + 4)
                    for i in range(2):
                        if j:
                            pe.wait_ge(c["gs"], g * 2 * FC + 2 * (j - 1) + i + 1)
                            pe.wait_ge(c["us"], g * 2 * FC + 2 * (j - 1) + i + 1)
                        three(ps[:, 2 + 2 * i, 0:gs], [(bg_hi[:, f0:f1], bg_lo[:, f0:f1],
                              am_hi[:, i, 0:gs], am_lo[:, i, 0:gs])]).then_inc(c["lora"], 1)
                        three(ps[:, 3 + 2 * i, 0:gs], [(bu_hi[:, f0:f1], bu_lo[:, f0:f1],
                              am_hi[:, 2 + i, 0:gs], am_lo[:, 2 + i, 0:gs])]).then_inc(c["lora"], 1)
                    if j:
                        down_factors(j - 1)
                if nxt:
                    n_nt, n_tm = tiles_of(nxt)
                    pe.wait_ge(c["gs"], g * 2 * FC + 2 * FC)
                    pe.wait_ge(c["us"], g * 2 * FC + 2 * FC)
                    for t in range(n_nt):
                        if t == 2:
                            down_factors(FC - 1)
                        turn_row((g + 1) * 2 * NT, t, n_tm, 2)
                    if n_nt <= 2:
                        down_factors(FC - 1)
                    pe.wait_ge(c["ub"], g * FC + FC)
                    cross_attention(g + 1, nxt, nb)
                else:
                    down_factors(FC - 1)
                    for t in range(nt):
                        if t:
                            pe.wait_ge(c["add"], g * NT + t)
                        project_out(g, t, tm)

            for t in range(NT):
                turn_row(0, t, TM, 2)
            cross_attention(0, GB, 0)
            over_groups(pe, layer)


def kernel(x, ctx_512, L0_attn_wq, L0_attn_wk, L0_attn_wv, L0_attn_wo, L0_attn_q_scale,
           L0_attn_k_scale, L0_xattn_Wq, L0_xattn_Wkv_expand, L0_xattn_Wout, L0_ffn_Wg, L0_ffn_Wu,
           L0_ffn_Wd, L0_ffn_Wr, L0_ffn_Ag, L0_ffn_Bg, L0_ffn_Au, L0_ffn_Bu, L0_ffn_Ad, L0_ffn_Bd):
    import concourse.bacc as bacc
    from concourse.bass_utils import run_bass_kernel_spmd

    def rows(w):
        return np.asarray(w).reshape(-1, np.asarray(w).shape[-1])

    B = x.shape[0]
    laid = {
        "x": rows(x),
        "wq": np.asarray(L0_attn_wq).reshape(E, H * D),
        "wk": np.asarray(L0_attn_wk).reshape(E, H * D),
        "wv": np.asarray(L0_attn_wv).reshape(E, H * D),
        "wo": np.asarray(L0_attn_wo).reshape(H * D, E),
        "q_scale": np.asarray(L0_attn_q_scale).reshape(D, 1),
        "k_scale": np.asarray(L0_attn_k_scale).reshape(D, 1),
        "ctxT": np.asarray(ctx_512).transpose(0, 2, 1),
        "cwq": np.asarray(L0_xattn_Wq).T,
        "cwkv": np.asarray(L0_xattn_Wkv_expand).T,
        "cwo": np.asarray(L0_xattn_Wout).T,
        "wg": np.asarray(L0_ffn_Wg).T,
        "wu": np.asarray(L0_ffn_Wu).T,
        "wd": np.asarray(L0_ffn_Wd).T,
        "ag": rows(L0_ffn_Ag).T,
        "au": rows(L0_ffn_Au).T,
        "ad": rows(L0_ffn_Ad).T,
        "bg": rows(np.asarray(L0_ffn_Bg).transpose(0, 2, 1)),
        "bu": rows(np.asarray(L0_ffn_Bu).transpose(0, 2, 1)),
        "bd": rows(np.asarray(L0_ffn_Bd).transpose(0, 2, 1)),
        "wr": np.asarray(L0_ffn_Wr).T,
    }
    nc = bacc.Bacc("TRN2", target_bir_lowering=False, num_devices=1)
    laid = {n: np.ascontiguousarray(a) for n, a in laid.items()}
    args = [nc.dram_tensor(f"in_{n}", a.shape, F32, kind="ExternalInput").ap()
            for n, a in laid.items()]
    args.append(nc.dram_tensor("x1", (B * S, E), F32, kind="Internal").ap())
    args.append(nc.dram_tensor("out", (B * S, E), F32, kind="ExternalOutput").ap())
    decoder_layer(nc, *args)
    r = run_bass_kernel_spmd(nc, [{f"in_{n}": a for n, a in laid.items()}], core_ids=[0])
    return r.results[0]["out"].reshape(x.shape)
```

```python
from contextlib import ExitStack

import numpy as np

import concourse.bass as bass
from concourse import mybir

ALU = mybir.AluOpType
ACT = mybir.ActivationFunctionType
AX = mybir.AxisListType
F32 = mybir.dt.float32
F16 = mybir.dt.float16
BF16 = mybir.dt.bfloat16

P = 128
S = 100
E = 512
KC = E // P
H = 16
D = 128
HG = 4
NHG = H // HG
GB = 5
X_SCALE = 16.0
W_SCALE = 64.0
V_SCALE = 8.0
F = 1408
FC = F // P
NE = 8
R = 16
L = 128
CD = E // H
CV_SCALE = 32.0
H_SCALE = 8.0
LORA = 2.0
BLOCK = KC * 4 * HG * D
MEM = 53200


def tiles_of(nb):
    n = -(-nb * S // P)
    assert nb * S % n == 0
    return n, nb * S // n


class Tile:

    def __init__(self, count, hg, t, tm, ahead):
        self.count, self.hg, self.t, self.tm, self.ahead = count, hg, t, tm, ahead
        self.cols = slice(t * tm, (t + 1) * tm)


def first_tiles(nb, count, ahead):
    nt, tm = tiles_of(nb)
    return [Tile(count + t, 0, t, tm, ahead) for t in range(nt)]


def attention_plan(nb, nxt):
    nt, tm = tiles_of(nb)
    steps = NHG * nb
    proj, turn, wo = ([[] for _ in range(steps)] for _ in range(3))
    for hg in range(NHG):
        if hg + 1 < NHG:
            tiles = [Tile((hg + 1) * nt + t, hg + 1, t, tm, False) for t in range(nt)]
        else:
            tiles = first_tiles(nxt, NHG * nt, True) if nxt else []
        for tile in tiles:
            at = hg * nb + (tile.t if nb > nt else 0)
            proj[at].append(tile)
            turn[at + (nb > nt)].append(tile)
        for t in range(nt):
            last = -(-(t + 1) * tm // S) - 1
            wo[min(hg * nb + last + 1, steps - 1)].append(hg * nt + t)
    return proj, turn, wo


def decoder_layer(nc, x, wq, wk, wv, wo, q_scale, k_scale, ctxT_in, cwq, cwkv_in, cwo, wg, wu, wd,
                  ag, au, ad, bg, bu, bd, wr, x1, out):
    NB = x.shape[0] // S
    FULL, REST = NB // GB, NB % GB
    NT, TM = tiles_of(GB)
    GS = GB * S

    with ExitStack() as ctx:
        def sb(name, shape, dt):
            return ctx.enter_context(nc.sbuf_tensor(name, shape, dt))

        def sem(name):
            return ctx.enter_context(nc.semaphore(name))

        mem = sb("mem", [P, MEM], F32)

        class Cut:

            def __init__(self, at):
                self.at = at

            def __call__(self, shape, dt=F32):
                n = int(np.prod(shape))
                words = n if dt == F32 else (n + 1) // 2
                ap = mem[:, self.at:self.at + words]
                self.at += words
                assert self.at <= MEM, self.at
                if dt != F32:
                    ap = ap.bitcast(dt)
                names = "abcd"[:len(shape)]
                sizes = {k: v for k, v in zip(names, shape)}
                return ap.rearrange(f"p ({' '.join(names)}) -> p {' '.join(names)}", **sizes)

        cut = Cut(0)
        ident = cut([P])
        ident16 = cut([P], BF16)
        mask = cut([HG, S], BF16)
        half = cut([16])
        one = cut([1])
        qks = cut([4])
        rank = cut([NT, NE])
        phase_start = cut.at

        stages = Cut(cut.at + (NHG - 1) * BLOCK)([4, KC, 512])
        wqkv_hi, wqkv_lo, wo_hi, wo_lo = ([None] * NHG for _ in range(4))
        for hg in range(NHG):
            wqkv_hi[hg], wqkv_lo[hg] = cut([KC, 3, HG * D], F16), cut([KC, 3, HG * D], F16)
            wo_hi[hg], wo_lo[hg] = cut([HG, E], F16), cut([HG, E], F16)
            assert cut.at == phase_start + (hg + 1) * BLOCK
        xres = cut([NT, E])
        stage_b = Cut(cut.at)([2, 2048])
        xin = cut([NT, E])
        xTn_hi = cut([KC, GS], F16)
        xTn_lo = cut([KC, GS], F16)
        cut([48])
        xT_hi = cut([KC, GS], F16)
        xT_lo = cut([KC, GS], F16)
        qkT = cut([2, HG, GS + 12])[:, :, :, 0:GS]
        oT_hi = cut([HG, GS], F16)
        oT_lo = cut([HG, GS], F16)
        v = cut([2, HG * D])
        qk = cut([2, 2 * HG, D])
        sq = cut([2 * HG, D])
        probs = cut([2, HG, S])
        pT = cut([HG, S])
        bst = cut([NT, 6])
        mv = cut([NT, 2])
        var = cut([NT])
        rstd = cut([NT])
        ss = cut([2, 2 * HG])
        ms = cut([2, 2 * HG])
        rr = cut([2, 2 * HG])
        mx = cut([HG])
        den = cut([HG])
        rden = cut([HG])

        cut = Cut(phase_start)
        cwq_hi, cwq_lo = cut([KC, E], F16), cut([KC, E], F16)
        cwo_hi, cwo_lo = cut([KC, E], F16), cut([KC, E], F16)
        cwkv = cut([2 * E])
        wr_hi, wr_lo = cut([KC, NE], F16), cut([KC, NE], F16)
        ag_hi, ag_lo = cut([KC, P], F16), cut([KC, P], F16)
        au_hi, au_lo = cut([KC, P], F16), cut([KC, P], F16)
        ad_hi, ad_lo = cut([FC, P], F16), cut([FC, P], F16)
        block_ends = [(6, cut.at)]
        bg_hi, bg_lo = cut([F], F16), cut([F], F16)
        bu_hi, bu_lo = cut([F], F16), cut([F], F16)
        wg_hi, wg_lo = cut([KC, F], F16), cut([KC, F], F16)
        block_ends.append((12, cut.at))
        wu_hi, wu_lo = cut([KC, F], F16), cut([KC, F], F16)
        yn = cut([NT, E])
        ctxT = cut([GS])
        stats = [cut([NT, 6]), cut([NT, 2]), cut([NT]), cut([NT])]
        block_ends.append((16, cut.at))
        bd_hi, bd_lo = cut([E], F16), cut([E], F16)
        wd_hi, wd_lo = cut([FC, E], F16), cut([FC, E], F16)
        block_ends.append((20, cut.at))
        for k, (_, end) in enumerate(block_ends):
            assert end <= phase_start + (k + 1) * BLOCK
        yT_hi, yT_lo = cut([KC, GS], F16), cut([KC, GS], F16)
        y = cut([NT, E])
        hb_hi, hb_lo = cut([FC, GS], F16), cut([FC, GS], F16)
        d_hi, d_lo = cut([GS], F16), cut([GS], F16)
        shared_end = cut.at
        coT_hi, coT_lo = cut([KC, GS], F16), cut([KC, GS], F16)
        nrm = Cut(cut.at)([NT, E])
        qpT = cut([KC, GS])
        ckT = cut([KC, GS])
        cv = cut([GB, E])
        cprobs = cut([4, HG, S])
        cpT = cut([2, HG, S])
        cmx = cut([4, HG])
        cden = cut([4, HG])
        crden = cut([4, HG])
        cut = Cut(shared_end)
        am_hi, am_lo = cut([4, GS], F16), cut([4, GS], F16)
        msk = cut([4, GS])
        spread = Cut(cut.at)([NT, 4, NE, R])
        gb = cut([GS])
        ub = cut([GS])
        gate = cut([3, GS])
        up = cut([2, GS])
        hh = cut([3, GS])
        hs_hi, hs_lo = cut([2, GS], F16), cut([2, GS], F16)
        tmp = cut([4, GS])
        rt = {n: cut([NT, NE]) for n in ("l", "p", "a", "b")}
        col = {n: cut([NT]) for n in ("m", "d", "r", "w1", "w2")}
        sel = cut([4, NT, NE])

        ps = ctx.enter_context(nc.psum_tensor("ps", [P, 8, 512], F32))
        ps_qk, ps_T = ps[:, 0:2, :], ps[:, 2:4, :]
        ps_vw, ps_s, ps_pT, ps_o = (ps[:, b, :] for b in range(4, 8))

        names = ("ident0 ident half scales wld0 wld1 wld2 wld3 wld4 wld5 whi wlo qks "
                 "xin xres bst mv var rstd xn lnT xhi xlo "
                 "xTc qkp raw sq ss ms rr qkn qkT qTe kTe vp ve s mx sub exp den rden norm pTp pTe "
                 "o ohi olo w add x1")
        s = {n: sem("s_" + n) for n in names.split()}
        names = ("wld0 wld1 whi wlo wkv mask rank y yn_in ctx out bst mv var rstd yn lnT lnhi lnlo "
                 "qp qpe ck cke v ve sc mx sub exp den rden norm pT pTe pv ohi olo w x2 "
                 "rl top rexp chain spread mT mTe a am ahi alo base gb sg0 ub lora gs us sgs "
                 "h hhi hlo ad dt dsum dhi dlo yp add moved")
        c = {n: sem("c_" + n) for n in names.split()}
        block = ctx.enter_context(nc.Block())

        N_STEP, N_QK = NHG * GB, NHG * NT
        LAST_QK, LAST_NT = (FULL if REST else FULL - 1) * N_QK, tiles_of(REST or GB)[0]
        STATS_AT, NORM_AT, TURN_AT = N_STEP - 11, N_STEP - 10, (N_STEP - 8, N_STEP - 7)

        def turned_at(n, nxt):
            return [t for t in range(tiles_of(nxt)[0]) if n == TURN_AT[t // 2]] if nxt else []

        def over_groups(eng, group):
            with eng.Fori(0, FULL - 1) as g:
                group(g, GB, GB)
            group(FULL - 1, GB, REST)
            if REST:
                group(FULL, REST, 0)

        LN_STATS_CHUNK, LN_ROWS_CHUNK = FC - 5, FC - 4
        OUT_PIECES = NT * (FC + 1)
        OUT_AT, OUT_AFTER = {}, (6, 6)
        for nb in (GB, REST):
            n = (OUT_PIECES - sum(OUT_AFTER)) // (nb + 1) // 6
            OUT_AT[nb] = [[0, 0, 0, 0, 6 * n]] + [[n, n, n, n, 2 * n]] * (nb - 1) + [[n, n, n, 0, 3 * n]]
            assert sum(map(sum, OUT_AT[nb])) + sum(OUT_AFTER) == OUT_PIECES

        def out_tiles_at(b, nb, last_nb):
            done = [sum(map(sum, OUT_AT[nb][:n])) // (FC + 1) for n in (max(b - 1, 0), b)]
            return range(*done) if last_nb else range(0)

        QP_BANKS = (0, 1, 4, 5)

        def early_tiles(nb):
            nt, tm = tiles_of(nb)
            return [t for t in range(nt) if -(-(t + 1) * tm // S) <= nb - 1]

        w_src = [w.rearrange("(c p) n -> p c n", p=P) for w in (wq, wk, wv)]
        wo_src = wo.rearrange("(h d) n -> d h n", d=D)
        LAST = NHG - 1
        PIECES = ([(m, hg) for hg in range(LAST) for m in range(3)]
                  + [(3, hg) for hg in range(LAST)] + [(m, LAST) for m in range(4)])
        N_STAGED = 4 * LAST

        SPLIT_AT = (6, 8, 10, 12, 14)

        def stage_of(n):
            if n < N_STAGED:
                return stages[:, n % 4, :, :], n % 4, n // 4 + 1
            k = n - N_STAGED
            return (xin if k % 2 else xres)[:, :, :], 4 + k % 2, k // 2 + 1

        B_PIECES = []

        def flat(ap):
            return ap if len(ap.shape) == 2 else ap.rearrange("p a b -> p (a b)")

        def add_pieces(hi, lo, src, chunks, width):
            step = max(1, 2048 // width)
            src = src.rearrange("(c p) n -> p c n", p=P)
            for a in range(0, chunks, step):
                b = min(chunks, a + step)
                B_PIECES.append((flat(hi)[:, a * width:b * width], flat(lo)[:, a * width:b * width],
                                 src[:, a:b, :], (b - a), width))

        for args in ((cwq_hi, cwq_lo, cwq, KC, E), (cwo_hi, cwo_lo, cwo, KC, E),
                     (wr_hi, wr_lo, wr, KC, NE), (ag_hi, ag_lo, ag, KC, P),
                     (au_hi, au_lo, au, KC, P), (ad_hi, ad_lo, ad, FC, P),
                     (bg_hi, bg_lo, bg, 1, F), (bu_hi, bu_lo, bu, 1, F),
                     (wg_hi, wg_lo, wg, KC, F), (wu_hi, wu_lo, wu, KC, F),
                     (bd_hi, bd_lo, bd, 1, E), (wd_hi, wd_lo, wd, FC, E)):
            add_pieces(*args)
        assert len(B_PIECES) == 20
        B_FIRST = block_ends[0][0]
        B_IN_A = 10
        assert B_FIRST <= B_IN_A <= block_ends[1][0]

        def beside_step(n, nb, place, nxt):
            pairs = [nb + 1 + p for p in range(B_FIRST // 2)]
            while len(pairs) < B_IN_A // 2:
                pairs.append(max(2 * nb + 1, pairs[-1] + 1))
            return [2 * pairs.index(n) + place] if not nxt and n in pairs else []

        def beside_first(b):
            return range(len(B_PIECES))[B_IN_A + 2 * b:B_IN_A + 2 * b + 2]

        def block_of(n):
            return next(k for k, (pieces, _) in enumerate(block_ends) if n < pieces)

        LINKS = 18

        def piece(m, hg, hi):
            if m < 3:
                return (wqkv_hi if hi else wqkv_lo)[hg][:, :, m, :]
            return (wo_hi if hi else wo_lo)[hg][:, :, :]

        @block.sync
        def _(sp):
            def rows_of(dram, t0, nb):
                nt, tm = tiles_of(nb)
                return dram[bass.ds(t0, nt * tm), :].rearrange("(t p) e -> p t e", p=tm)

            def load(buffer, src, nb, signal):
                nt, tm = tiles_of(nb)
                sp.dma_start(buffer[0:tm, 0:nt, :], src).then_inc(s[signal], 16)

            def keys_of(b0, nb, skip=0):
                return ctxT_in[skip:, :, 0:S][bass.ds(b0, nb), :, :].rearrange("b l k -> l b k")

            def load_rows(buffer, src, nb, signal):
                nt, tm = tiles_of(nb)
                sp.dma_start(buffer[0:tm, 0:nt, :], src).then_inc(c[signal], 16)

            def load_keys(src, nb):
                sp.dma_start(ctxT[:, 0:nb * S].rearrange("l (b k) -> l b k", b=nb),
                             src).then_inc(c["ctx"], 16)

            def load_pieces(first, last):
                for n in range(first, last):
                    _, _, src, chunks, width = B_PIECES[n]
                    if n >= 2:
                        sp.wait_ge(c["wlo"], n - 1)
                    if n == 3:
                        sp.wait_ge(s["w"], LAST_QK + LAST_NT)
                        sp.dma_start(cwkv[:, :], cwkv_in).then_inc(c["wkv"], 16)
                    sp.dma_start(stage_b[:, n % 2, 0:chunks * width].rearrange(
                        "p (c n) -> p c n", c=chunks), src).then_inc(c[f"wld{n % 2}"], 16)

            def group(g, nb, nxt):
                nt, tm = tiles_of(nb)
                t0 = sp.snap(g * GS) if nxt == GB else g * GS
                ahead = rows_of(x[GS:, :], t0, nxt) if nxt else None
                if nxt:
                    sp.wait_ge(s["lnT"], g * NT + nt)
                    load(xin, ahead, nxt, "xin")
                else:
                    sp.wait_ge(s["xTc"], 2 * g + 2)
                    load_pieces(0, B_IN_A)
                    sp.wait_ge(s["w"], g * N_QK + 3 * nt)
                    load_rows(yn, rows_of(x1, 0, GB), GB, "yn_in")
                    load_keys(keys_of(0, GB), GB)
                sp.wait_ge(s["add"], g * N_QK + NHG * nt)
                b0 = sp.snap(g * GB) if nxt == GB else g * GB
                sp.dma_start(rows_of(x1, b0 * S, nb), xres[0:tm, 0:nt, :]).then_inc(s["x1"], 16)
                sp.wait_ge(s["x1"], g * 16 + 16)
                if nxt:
                    load(xres, ahead, nxt, "xres")

            load(xin, rows_of(x, 0, GB), GB, "xin")
            sp.dma_start(qks[:, 0:1], q_scale).then_inc(s["scales"], 16)
            sp.dma_start(qks[:, 1:2], k_scale).then_inc(s["scales"], 16)
            for n, (m, hg) in enumerate(PIECES):
                if 4 <= n < N_STAGED:
                    sp.wait_ge(s["wlo"], n - 3)
                elif n >= N_STAGED + 2:
                    sp.wait_ge(s["wlo"], n - 1)
                elif n == N_STAGED + 1:
                    sp.wait_ge(s["lnT"], NT)
                src = (w_src[m][:, :, hg * 512:(hg + 1) * 512] if m < 3
                       else wo_src[:, hg * HG:(hg + 1) * HG, :])
                stage, slot, _ = stage_of(n)
                sp.dma_start(stage, src).then_inc(s[f"wld{slot}"], 16)
            sp.wait_ge(s["wlo"], len(PIECES))
            load(xres, rows_of(x, 0, GB), GB, "xres")
            over_groups(sp, group)

            def layer(g, nb, nxt):
                nt, tm = tiles_of(nb)
                t0 = sp.snap(g * GS) if nxt == GB else g * GS
                b0 = sp.snap(g * GB) if nxt == GB else g * GB
                if nxt:
                    ahead, keys = rows_of(x1[GS:, :], t0, nxt), keys_of(b0, nxt, GB)
                    sp.wait_ge(c["v"], g * GB + nb)
                    load_keys(keys, nxt)
                    sp.wait_ge(c["moved"], g + 1)
                    sp.wait_ge(c["yn"], g * 2 * NT + 2 * nt)
                    load_rows(yn, ahead, nxt, "yn_in")
                    sp.wait_ge(c["lnT"], (g + 1) * 2 * NT + tiles_of(nxt)[0])
                    load_rows(yn, ahead, nxt, "y")
                sp.wait_ge(c["add"], g * NT + nt)
                b0 = sp.snap(g * GB) if nxt == GB else g * GB
                sp.dma_start(rows_of(out, b0 * S, nb), y[0:tm, 0:nt, :]).then_inc(c["out"], 16)

            load_pieces(B_IN_A, len(B_PIECES))
            sp.wait_ge(c["lnT"], NT)
            load_rows(yn, rows_of(x1, 0, GB), GB, "y")
            over_groups(sp, layer)
            sp.wait_ge(c["out"], 16 * (FULL + (REST > 0)))

        @block.gpsimd
        def _(pool):
            pool.memset(half[:, :], -0.5).then_inc(s["half"], 1)
            pool.memset(ident[:, :], 0.0).then_inc(s["ident0"], 1)
            pool.wait_ge(s["ident0"], 1)
            pool.affine_select(out=ident[:, :], in_=ident[:, :], compare_op=ALU.not_equal, fill=1.0,
                               base=0, pattern=[[-1, P]], channel_multiplier=1).then_inc(s["ident"], 1)
            pool.wait_ge(s["half"], 1)
            pool.memset(one[:, :], 1.0).then_inc(c["mask"], 1)
            pool.memset(ident16[:, :], 0.0).then_inc(c["mask"], 1)
            pool.memset(mask[:, :, :], 0.0).then_inc(c["mask"], 1)
            pool.wait_ge(c["mask"], 3)
            pool.affine_select(out=ident16[:, :], in_=ident16[:, :], compare_op=ALU.not_equal,
                               fill=1.0, base=0, pattern=[[-1, P]],
                               channel_multiplier=1).then_inc(c["mask"], 1)
            pool.affine_select(out=mask[0:S, :, :], in_=mask[0:S, :, :], compare_op=ALU.is_ge,
                               fill=-1e30, base=0, pattern=[[0, HG], [-1, S]],
                               channel_multiplier=1).then_inc(c["mask"], 1)
            for e in range(NE):
                pool.memset(rank[:, :, e:e + 1], float(NE - e)).then_inc(c["rank"], 1)

            def ln_power(g, nb):
                nt, tm = tiles_of(nb)
                pool.wait_ge(s["var"], g + 1)
                pool.tensor_tensor(rstd[0:tm, 0:nt], var[0:tm, 0:nt], half[0:tm, 0:nt],
                                   ALU.pow).then_inc(s["rstd"], 1)

            def rms_power(b_qk, tile):
                i, tm = tile.count % 2, tile.tm
                pool.wait_ge(s["ms"], b_qk + tile.count + 1)
                pool.tensor_tensor(rr[0:tm, i, :], ms[0:tm, i, :], half[0:tm, 0:2 * HG],
                                   ALU.pow).then_inc(s["rr"], 1)

            def norm(b_step, n):
                pool.wait_ge(s["rden"], b_step + n + 1)
                pool.tensor_tensor(probs[0:S, n % 2, :, :], probs[0:S, n % 2, :, :],
                                   rden[0:S, :].unsqueeze(2).to_broadcast([S, HG, S]),
                                   ALU.mult).then_inc(s["norm"], 1)

            def group(g, nb, nxt):
                proj, _, _ = attention_plan(nb, nxt)
                b_step, b_qk, steps = g * N_STEP, g * N_QK, NHG * nb
                for n in range(steps):
                    for tile in (proj[n - 1] if n else []):
                        if nb > tiles_of(nb)[0]:
                            rms_power(b_qk, tile)
                    if n + 1 < steps or nxt:
                        norm(b_step, n + 1)
                    if nb == tiles_of(nb)[0]:
                        for tile in proj[n]:
                            rms_power(b_qk, tile)
                    if nxt and n == STATS_AT:
                        ln_power(g + 1, nxt)

            ln_power(0, GB)
            for tile in first_tiles(GB, 0, True):
                rms_power(0, tile)
            norm(0, 0)
            over_groups(pool, group)

            def power(a, b, tm, count):
                pool.wait_ge(c["var"], count)
                pool.tensor_tensor(stats[3][0:tm, a:b], stats[2][0:tm, a:b], half[0:tm, a:b],
                                   ALU.pow).then_inc(c["rstd"], 1)

            def layer(g, nb, nxt):
                gs = nb * S
                for j in range(FC):
                    for i in range(3):
                        if i == 0:
                            pool.wait_ge(c["sg0"], g * FC + j + 1)
                            pool.wait_ge(c["ub"], g * FC + j + 1)
                        else:
                            pool.wait_ge(c["sgs"], g * 2 * FC + 2 * j + i)
                            pool.wait_ge(c["us"], g * 2 * FC + 2 * j + i)
                        if j:
                            pool.wait_ge(c["hlo"], g * 3 * FC + 3 * (j - 1) + i + 1)
                        pool.tensor_tensor(hh[:, i, 0:gs], gate[:, i, 0:gs],
                                           ub[:, 0:gs] if i == 0 else up[:, i - 1, 0:gs],
                                           ALU.mult).then_inc(c["h"], 1)
                    if nxt and j == LN_STATS_CHUNK:
                        nt, tm = tiles_of(nxt)
                        power(0, nt, tm, (g + 1) * (NT + 1) + 1)
                if nxt:
                    cross_attention(g + 1, nxt, nb)

            def cross_attention(g, nb, last_nb):
                nt, tm = tiles_of(nb)
                for b in range(nb):
                    for i in range(4):
                        pool.wait_ge(c["rden"], g * 4 * GB + 4 * b + i + 1)
                        pool.tensor_tensor(cprobs[0:S, i, :, :], cprobs[0:S, i, :, :],
                                           crden[0:S, i, :].unsqueeze(2).to_broadcast([S, HG, S]),
                                           ALU.mult).then_inc(c["norm"], 1)
                for t in range(nt):
                    power(t, t + 1, tm, g * (NT + 1) + t + 2)
                if last_nb:
                    pool.wait_ge(c["out"], g * 16)
                pool.wait_ge(c["x2"], g * NT + nt)
                pool.tensor_tensor(y[0:tm, 0:nt, :], yn[0:tm, 0:nt, :],
                                   one[0:tm, :].unsqueeze(2).to_broadcast([tm, nt, E]),
                                   ALU.mult).then_inc(c["moved"], 1)

            power(0, NT, TM, 1)
            cross_attention(0, GB, 0)
            over_groups(pool, layer)

        @block.scalar
        def _(act):
            def split_hi(first, last):
                for n in range(first, last):
                    stage, slot, fills = stage_of(n)
                    act.wait_ge(s[f"wld{slot}"], 16 * fills)
                    if n == N_STAGED:
                        act.wait_ge(s["wlo"], N_STAGED)
                    act.activation(piece(*PIECES[n], True), stage, ACT.Copy,
                                   scale=W_SCALE).then_inc(s["whi"], 1)

            def split_b_hi(n):
                hi, _, _, chunks, width = B_PIECES[n]
                act.wait_ge(c[f"wld{n % 2}"], 16 * (n // 2 + 1))
                if n == 0 or block_of(n) > block_of(n - 1):
                    act.wait_ge(s["w"], LAST_QK + (block_of(n) + 1) * LAST_NT)
                act.activation(hi, stage_b[:, n % 2, 0:chunks * width], ACT.Copy,
                               scale=W_SCALE).then_inc(c["whi"], 1)

            def rows_hi(b_t, t, tm):
                act.wait_ge(s["lnT"], b_t + t + 1)
                act.activation(xTn_hi[:, :, t * tm:(t + 1) * tm],
                               ps_T[:, t % 2, 0:KC * tm].rearrange("p (c t) -> p c t", c=KC),
                               ACT.Copy).then_inc(s["xhi"], 1)

            def take_raw(b_qk, tile):
                u, tm = tile.count, tile.tm
                src = ps_qk[0:tm, :, :].rearrange("p a (h d) -> p (a h) d", d=D)
                act.wait_ge(s["qkp"], b_qk + u + 1)
                if u:
                    act.wait_ge(s["ss"], b_qk + u)
                act.activation(sq[0:tm, :, :], src, ACT.Square).then_inc(s["sq"], 1)
                if u >= 2:
                    act.wait_ge(s["qkT"], b_qk + u - 1)
                act.activation(qk[0:tm, u % 2, :, :], src, ACT.Copy).then_inc(s["raw"], 1)

            def take_qT(b_qk, tile):
                act.wait_ge(s["qkT"], b_qk + tile.count + 1)
                act.activation(qkT[:, 0, :, tile.cols],
                               ps_T[:, 0, 0:HG * tile.tm].rearrange("p (h t) -> p h t", h=HG),
                               ACT.Copy, scale=qks[:, 2:3]).then_inc(s["qTe"], 1)

            def exponentials(b_step, n):
                act.wait_ge(s["sub"], b_step + n + 1)
                act.activation(probs[0:S, n % 2, :, :], probs[0:S, n % 2, :, :],
                               ACT.Exp).then_inc(s["exp"], 1)

            def take_v(b_step, n):
                act.wait_ge(s["vp"], b_step + n + 1)
                if n >= 2:
                    act.wait_ge(s["o"], b_step + n - 1)
                act.activation(v[0:S, n % 2, :], ps_vw[0:S, :], ACT.Copy,
                               scale=V_SCALE / (X_SCALE * W_SCALE)).then_inc(s["ve"], 1)

            def group(g, nb, nxt):
                proj, turn, _ = attention_plan(nb, nxt)
                b_step, b_qk, steps = g * N_STEP, g * N_QK, NHG * nb
                for n in range(steps):
                    b = n % nb
                    act.wait_ge(s["pTp"], b_step + n + 1)
                    if n:
                        act.wait_ge(s["o"], b_step + n)
                    act.activation(pT[0:S, :, :], ps_pT[0:S, 0:HG * S].rearrange(
                        "p (h t) -> p h t", h=HG), ACT.Copy).then_inc(s["pTe"], 1)
                    if n + 1 < steps or nxt:
                        exponentials(b_step, n + 1)
                        take_v(b_step, n + 1)
                    for t in turned_at(n, nxt):
                        rows_hi(g * NT + NT, t, tiles_of(nxt)[1])
                    for n_b in beside_step(n, nb, 0, nxt):
                        split_b_hi(n_b)
                    act.wait_ge(s["o"], b_step + n + 1)
                    act.activation(oT_hi[:, :, b * S:(b + 1) * S],
                                   ps_o[:, 0:HG * S].rearrange("p (h t) -> p h t", h=HG),
                                   ACT.Copy).then_inc(s["ohi"], 1)
                    for n_b in beside_step(n, nb, 1, nxt):
                        split_b_hi(n_b)
                    for tile in proj[n]:
                        take_raw(b_qk, tile)
                    for tile in turn[n]:
                        take_qT(b_qk, tile)

            for t in range(NT):
                rows_hi(0, t, TM)
            split_hi(0, SPLIT_AT[0])
            act.wait_ge(s["qks"], 1)
            tiles = first_tiles(GB, 0, True)
            for tile in tiles:
                take_raw(0, tile)
                if tile.t:
                    take_qT(0, tiles[tile.t - 1])
                split_hi(SPLIT_AT[tile.t], SPLIT_AT[tile.t + 1])
            take_qT(0, tiles[-1])
            exponentials(0, 0)
            take_v(0, 0)
            split_hi(SPLIT_AT[-1], len(PIECES))
            over_groups(act, group)

            def row_hi(count, t, tm, bank):
                act.wait_ge(c["lnT"], count + t + 1)
                act.activation(yT_hi[:, :, t * tm:(t + 1) * tm],
                               ps[:, bank, 0:KC * tm].rearrange("p (c t) -> p c t", c=KC),
                               ACT.Copy).then_inc(c["lnhi"], 1)

            def cross_attention(g, nb, last_nb):
                nt, tm = tiles_of(nb)
                gs = nb * S
                for t in range(nt):
                    row_hi(g * 2 * NT, t, tm, t % 2)
                for b in range(nb):
                    act.wait_ge(c["v"], g * GB + b + 1)
                    act.activation(cv[0:S, b, :], ps[0:S, 2 + b % 2, :], ACT.Copy,
                                   scale=CV_SCALE).then_inc(c["ve"], 1)
                if last_nb:
                    act.wait_ge(c["dsum"], g)
                    act.activation(d_hi[:, 0:last_nb * S], tmp[:, 0, 0:last_nb * S],
                                   ACT.Copy).then_inc(c["dhi"], 1)
                for m in range(KC):
                    act.wait_ge(c["qp"], g * KC + m + 1)
                    act.activation(qpT[:, m, 0:gs], ps[:, QP_BANKS[m], 0:gs], ACT.Copy,
                                   scale=float(CD) ** -0.5 / (X_SCALE * W_SCALE)
                                   ).then_inc(c["qpe"], 1)

                for b in range(nb + 1):
                    for i in range(4):
                        if b:
                            r = 4 * (b - 1) + i
                            act.wait_ge(c["pT"], g * 4 * GB + r + 1)
                            if r >= 2:
                                act.wait_ge(c["pv"], g * 4 * GB + r - 1)
                            act.activation(cpT[0:S, r % 2, :, :],
                                           ps[0:S, 4 + i % 2, 0:HG * S].rearrange(
                                               "p (h t) -> p h t", h=HG),
                                           ACT.Copy).then_inc(c["pTe"], 1)
                        if b < nb:
                            act.wait_ge(c["sub"], g * 4 * GB + 4 * b + i + 1)
                            act.activation(cprobs[0:S, i, :, :], cprobs[0:S, i, :, :],
                                           ACT.Exp).then_inc(c["exp"], 1)
                    for n in (beside_first(b) if not last_nb else []):
                        split_b_hi(n)
                    if b:
                        act.wait_ge(c["pv"], g * 4 * GB + 4 * b)
                        act.activation(coT_hi[:, :, (b - 1) * S:b * S],
                                       ps[:, 6, 0:KC * S].rearrange("p (c t) -> p c t", c=KC),
                                       ACT.Copy).then_inc(c["ohi"], 1)
                for t in range(nt):
                    row_hi(g * 2 * NT + nt, t, tm, t)

            def layer(g, nb, nxt):
                nt, tm = tiles_of(nb)
                gs = nb * S
                act.wait_ge(c["top"], g + 1)
                act.activation(rt["p"][0:tm, 0:nt, :], rt["p"][0:tm, 0:nt, :],
                               ACT.Exp).then_inc(c["rexp"], 1)
                for k in range(4):
                    act.wait_ge(c["mT"], g * 4 + k + 1)
                    act.activation(msk[:, k, 0:gs], ps[:, 2 + k % 2, 0:gs],
                                   ACT.Copy).then_inc(c["mTe"], 1)
                for i in range(4):
                    act.wait_ge(c["am"], g * 4 + i + 1)
                    act.activation(am_hi[:, i, 0:gs], tmp[:, i, 0:gs], ACT.Copy).then_inc(c["ahi"], 1)

                def half_h(i, jj):
                    act.wait_ge(c["h"], g * 3 * FC + 3 * jj + i + 1)
                    if i and jj:
                        act.wait_ge(c["ad"], g * FC + jj)
                    act.activation(hb_hi[:, jj, 0:gs] if i == 0 else hs_hi[:, i - 1, 0:gs],
                                   hh[:, i, 0:gs], ACT.Copy).then_inc(c["hhi"], 1)

                for j in range(FC):
                    act.wait_ge(c["base"], g * 2 * FC + 2 * j + 1)
                    if j:
                        act.wait_ge(c["gs"], g * 2 * FC + 2 * j)
                    act.activation(gb[:, 0:gs], ps[:, 0, 0:gs], ACT.Copy).then_inc(c["gb"], 1)
                    if j:
                        act.wait_ge(c["h"], g * 3 * FC + 3 * (j - 1) + 1)
                    act.activation(gate[:, 0, 0:gs], ps[:, 0, 0:gs], ACT.Silu,
                                   scale=1 / (X_SCALE * W_SCALE)).then_inc(c["sg0"], 1)
                    if j:
                        half_h(1, j - 1)
                        half_h(2, j - 1)
                    act.wait_ge(c["base"], g * 2 * FC + 2 * j + 2)
                    if j:
                        act.wait_ge(c["us"], g * 2 * FC + 2 * j)
                    act.activation(ub[:, 0:gs], ps[:, 1, 0:gs], ACT.Copy,
                                   scale=H_SCALE / (X_SCALE * W_SCALE)).then_inc(c["ub"], 1)
                    half_h(0, j)
                    for i in (1, 2):
                        act.wait_ge(c["gs"], g * 2 * FC + 2 * j + i)
                        act.activation(gate[:, i, 0:gs], gate[:, i, 0:gs], ACT.Silu,
                                       scale=1 / (X_SCALE * W_SCALE)).then_inc(c["sgs"], 1)
                half_h(1, FC - 1)
                half_h(2, FC - 1)
                if nxt:
                    cross_attention(g + 1, nxt, nb)
                else:
                    act.wait_ge(c["dsum"], g + 1)
                    act.activation(d_hi[:, 0:gs], tmp[:, 0, 0:gs], ACT.Copy).then_inc(c["dhi"], 1)

            cross_attention(0, GB, 0)
            over_groups(act, layer)

        @block.vector
        def _(dve):
            def split_lo(first, last):
                for n in range(first, last):
                    dve.wait_ge(s["whi"], n + 1)
                    dve.scalar_tensor_tensor(out=piece(*PIECES[n], False), in0=stage_of(n)[0],
                                             scalar=W_SCALE, in1=piece(*PIECES[n], True),
                                             op0=ALU.mult, op1=ALU.subtract).then_inc(s["wlo"], 1)

            def split_b_lo(n):
                hi, lo, _, chunks, width = B_PIECES[n]
                dve.wait_ge(c["whi"], n + 1)
                dve.scalar_tensor_tensor(out=lo, in0=stage_b[:, n % 2, 0:chunks * width],
                                         scalar=W_SCALE, in1=hi, op0=ALU.mult,
                                         op1=ALU.subtract).then_inc(c["wlo"], 1)

            def ln_stats(g, nb):
                nt, tm = tiles_of(nb)
                dve.wait_ge(s["xin"], g * 16 + 16)
                for t in range(nt):
                    dve.bn_stats(bst[0:tm, t, :], xin[0:tm, t, :]).then_inc(s["bst"], 1)
                dve.wait_ge(s["bst"], g * NT + nt)
                dve.memset(var[0:tm, 0:nt], 0.0)
                for t in range(nt):
                    dve.bn_aggr(mv[0:tm, t, :], bst[0:tm, t, :]).then_inc(s["mv"], 1)
                dve.wait_ge(s["mv"], g * NT + nt)
                dve.tensor_scalar(var[0:tm, 0:nt], mv[0:tm, 0:nt, 1], 1e-5, 1 / X_SCALE ** 2, ALU.add,
                                  ALU.mult).then_inc(s["var"], 1)

            def ln_rows(g, nb):
                nt, tm = tiles_of(nb)
                dve.wait_ge(s["rstd"], g + 1)
                for t in range(nt):
                    dve.tensor_scalar(xin[0:tm, t, :], xin[0:tm, t, :], mv[0:tm, t, 0:1],
                                      rstd[0:tm, t:t + 1], ALU.subtract,
                                      ALU.mult).then_inc(s["xn"], 1)

            def rows_lo(b_t, t, tm):
                dve.wait_ge(s["xhi"], b_t + t + 1)
                dve.tensor_tensor(xTn_lo[:, :, t * tm:(t + 1) * tm],
                                  ps_T[:, t % 2, 0:KC * tm].rearrange("p (c t) -> p c t", c=KC),
                                  xTn_hi[:, :, t * tm:(t + 1) * tm],
                                  ALU.subtract).then_inc(s["xlo"], 1)

            def next_rows(b_t, nb):
                cols = slice(0, nb * S)
                dve.wait_ge(s["xlo"], b_t + tiles_of(nb)[0])
                dve.tensor_copy(xT_hi[:, :, cols], xTn_hi[:, :, cols]).then_inc(s["xTc"], 1)
                dve.tensor_copy(xT_lo[:, :, cols], xTn_lo[:, :, cols]).then_inc(s["xTc"], 1)

            def mean_square(b_qk, tile):
                u, i, tm = tile.count, tile.count % 2, tile.tm
                dve.wait_ge(s["sq"], b_qk + u + 1)
                dve.tensor_reduce(ss[0:tm, i, :], sq[0:tm, :, :], AX.X, ALU.add).then_inc(s["ss"], 1)
                dve.wait_ge(s["ss"], b_qk + u + 1)
                dve.tensor_scalar(ms[0:tm, i, :], ss[0:tm, i, :], 1.0 / D,
                                  1e-6 * (X_SCALE * W_SCALE) ** 2, ALU.mult,
                                  ALU.add).then_inc(s["ms"], 1)

            def scale_qk(b_qk, tile):
                u, i, tm = tile.count, tile.count % 2, tile.tm
                dve.wait_ge(s["rr"], b_qk + u + 1)
                dve.wait_ge(s["raw"], b_qk + u + 1)
                dve.tensor_tensor(qk[0:tm, i, :, :], qk[0:tm, i, :, :],
                                  rr[0:tm, i, :].unsqueeze(2).to_broadcast([tm, 2 * HG, D]),
                                  ALU.mult).then_inc(s["qkn"], 1)

            def take_kT(b_qk, tile):
                dve.wait_ge(s["qkT"], b_qk + tile.count + 1)
                dve.tensor_copy(qkT[:, 1, :, tile.cols],
                                ps_T[:, 1, 0:HG * tile.tm].rearrange("p (h t) -> p h t", h=HG)
                                ).then_inc(s["kTe"], 1)

            def subtract_max(b_step, n):
                sc = ps_s[0:S, 0:HG * S].rearrange("p (h t) -> p h t", h=HG)
                dve.wait_ge(s["s"], b_step + n + 1)
                dve.tensor_reduce(mx[0:S, :], sc, AX.X, ALU.max).then_inc(s["mx"], 1)
                if n >= 2:
                    dve.wait_ge(s["pTp"], b_step + n - 1)
                dve.wait_ge(s["mx"], b_step + n + 1)
                dve.tensor_tensor(probs[0:S, n % 2, :, :], sc,
                                  mx[0:S, :].unsqueeze(2).to_broadcast([S, HG, S]),
                                  ALU.subtract).then_inc(s["sub"], 1)

            def inverse_sum(b_step, n):
                dve.wait_ge(s["exp"], b_step + n + 1)
                dve.tensor_reduce(den[0:S, :], probs[0:S, n % 2, :, :], AX.X,
                                  ALU.add).then_inc(s["den"], 1)
                if n:
                    dve.wait_ge(s["norm"], b_step + n)
                dve.wait_ge(s["den"], b_step + n + 1)
                dve.reciprocal(rden[0:S, :], den[0:S, :]).then_inc(s["rden"], 1)

            def add_wo(b_qk, w, t, tm):
                dve.wait_ge(s["w"], b_qk + w + 1)
                if w:
                    dve.wait_ge(s["add"], b_qk + w)
                dve.scalar_tensor_tensor(out=xres[0:tm, t, :], in0=ps_vw[0:tm, :],
                                         scalar=1.0 / (V_SCALE * W_SCALE), in1=xres[0:tm, t, :],
                                         op0=ALU.mult, op1=ALU.add).then_inc(s["add"], 1)

            def row_stats(count, a, b, tm):
                bst, mv, var, _ = stats
                for t in range(a, b):
                    dve.bn_stats(bst[0:tm, t, :], yn[0:tm, t, :]).then_inc(c["bst"], 1)
                dve.wait_ge(c["bst"], count + b - a)
                dve.memset(var[0:tm, a:b], 0.0)
                for t in range(a, b):
                    dve.bn_aggr(mv[0:tm, t, :], bst[0:tm, t, :]).then_inc(c["mv"], 1)
                dve.wait_ge(c["mv"], count + b - a)
                dve.tensor_scalar(var[0:tm, a:b], mv[0:tm, a:b, 1], 1e-5, 1 / X_SCALE ** 2,
                                  ALU.add, ALU.mult).then_inc(c["var"], 1)

            def norm_row(out_rows, t, tm, rstd_count):
                _, mv, _, rstd = stats
                dve.wait_ge(c["rstd"], rstd_count)
                dve.tensor_scalar(out_rows[0:tm, t, :], yn[0:tm, t, :], mv[0:tm, t, 0:1],
                                  rstd[0:tm, t:t + 1], ALU.subtract, ALU.mult).then_inc(c["yn"], 1)

            def row_lo(count, t, tm, bank):
                dve.wait_ge(c["lnhi"], count + t + 1)
                dve.tensor_tensor(yT_lo[:, :, t * tm:(t + 1) * tm],
                                  ps[:, bank, 0:KC * tm].rearrange("p (c t) -> p c t", c=KC),
                                  yT_hi[:, :, t * tm:(t + 1) * tm], ALU.subtract).then_inc(c["lnlo"], 1)

            def first_stats(g, nb):
                nt, tm = tiles_of(nb)
                dve.wait_ge(c["yn_in"], g * 16 + 16)
                row_stats(g * 2 * NT, 0, nt, tm)

            def first_rows(g, nb):
                nt, tm = tiles_of(nb)
                for t in range(nt):
                    norm_row(yn, t, tm, g * (NT + 1) + 1)

            def group(g, nb, nxt):
                nt, tm = tiles_of(nb)
                proj, turn, wo_at = attention_plan(nb, nxt)
                b_step, b_qk, steps = g * N_STEP, g * N_QK, NHG * nb
                for n in range(steps):
                    for w in (wo_at[n - 1] if n else []):
                        if w == 0:
                            dve.wait_ge(s["xres"], g * 16 + 16)
                        add_wo(b_qk, w, w % nt, tm)
                    if n + 1 < steps or nxt:
                        subtract_max(b_step, n + 1)
                    ready = proj[n - 1] if n and nb > nt else []
                    for tile in ready:
                        mean_square(b_qk, tile)
                    if n + 1 < steps or nxt:
                        inverse_sum(b_step, n + 1)
                    for tile in ready:
                        scale_qk(b_qk, tile)
                    for t in turned_at(n, nxt):
                        rows_lo(g * NT + NT, t, tiles_of(nxt)[1])
                    for n_b in beside_step(n, nb, 0, nxt):
                        split_b_lo(n_b)
                    b = n % nb
                    dve.wait_ge(s["ohi"], b_step + n + 1)
                    dve.tensor_tensor(oT_lo[:, :, b * S:(b + 1) * S],
                                      ps_o[:, 0:HG * S].rearrange("p (h t) -> p h t", h=HG),
                                      oT_hi[:, :, b * S:(b + 1) * S],
                                      ALU.subtract).then_inc(s["olo"], 1)
                    for n_b in beside_step(n, nb, 1, nxt):
                        split_b_lo(n_b)
                    if nb == nt:
                        for tile in proj[n]:
                            mean_square(b_qk, tile)
                            scale_qk(b_qk, tile)
                    if nxt and n == STATS_AT:
                        ln_stats(g + 1, nxt)
                    if nxt and n == NORM_AT:
                        ln_rows(g + 1, nxt)
                    if nxt and n == steps - 2:
                        dve.wait_ge(s["vp"], b_step + steps)
                        next_rows(g * NT + NT, nxt)
                    for tile in turn[n]:
                        take_kT(b_qk, tile)
                if not nxt:
                    first_stats(0, GB)
                    first_rows(0, GB)
                for w in wo_at[steps - 1]:
                    add_wo(b_qk, w, w % nt, tm)

            ln_stats(0, GB)
            ln_rows(0, GB)
            for t in range(NT):
                rows_lo(0, t, TM)
            next_rows(0, GB)
            dve.wait_ge(s["scales"], 32)
            dve.tensor_tensor(qks[:, 2:3], qks[:, 0:1], qks[:, 1:2], ALU.mult).then_inc(s["qks"], 1)
            split_lo(0, SPLIT_AT[0])
            tiles = first_tiles(GB, 0, True)
            for tile in tiles:
                mean_square(0, tile)
                scale_qk(0, tile)
                if tile.t:
                    take_kT(0, tiles[tile.t - 1])
                split_lo(SPLIT_AT[tile.t], SPLIT_AT[tile.t + 1])
            take_kT(0, tiles[-1])
            subtract_max(0, 0)
            inverse_sum(0, 0)
            split_lo(SPLIT_AT[-1], len(PIECES))
            over_groups(dve, group)

            def add_out(g, t, tm):
                if t == 0:
                    dve.wait_ge(c["moved"], g + 1)
                dve.wait_ge(c["yp"], g * NT + t + 1)
                dve.scalar_tensor_tensor(out=y[0:tm, t, :], in0=ps[0:tm, 7, :],
                                         scalar=1 / (H_SCALE * W_SCALE), in1=y[0:tm, t, :],
                                         op0=ALU.mult, op1=ALU.add).then_inc(c["add"], 1)

            def sum_down(g, gs):
                dve.wait_ge(c["ad"], g * FC + FC)
                for i in range(2):
                    dve.scalar_tensor_tensor(out=tmp[:, i, 0:gs], in0=ps[:, 6 + i, 0:gs],
                                             scalar=LORA / W_SCALE, in1=msk[:, 2 + i, 0:gs],
                                             op0=ALU.mult, op1=ALU.mult).then_inc(c["dt"], 1)
                dve.wait_ge(c["dt"], g * 2 + 2)
                dve.tensor_tensor(tmp[:, 0, 0:gs], tmp[:, 0, 0:gs], tmp[:, 1, 0:gs],
                                  ALU.add).then_inc(c["dsum"], 1)
                dve.wait_ge(c["dhi"], g + 1)
                dve.tensor_tensor(d_lo[:, 0:gs], tmp[:, 0, 0:gs], d_hi[:, 0:gs],
                                  ALU.subtract).then_inc(c["dlo"], 1)

            def cross_attention(g, nb, last_nb):
                nt, tm = tiles_of(nb)
                gs = nb * S
                for t in range(min(nt, 2)):
                    row_lo(g * 2 * NT, t, tm, t)
                for m in range(KC):
                    dve.wait_ge(c["ck"], g * KC + m + 1)
                    dve.tensor_copy(ckT[:, m, 0:gs], ps[:, 2 + m, 0:gs]).then_inc(c["cke"], 1)
                for t in range(2, nt):
                    row_lo(g * 2 * NT, t, tm, t % 2)
                if last_nb:
                    sum_down(g - 1, last_nb * S)

                def take_o(b):
                    dve.wait_ge(c["ohi"], g * GB + b + 1)
                    dve.tensor_tensor(coT_lo[:, :, b * S:(b + 1) * S],
                                      ps[:, 6, 0:KC * S].rearrange("p (c t) -> p c t", c=KC),
                                      coT_hi[:, :, b * S:(b + 1) * S],
                                      ALU.subtract).then_inc(c["olo"], 1)

                def shift_scores(b, i):
                    n = g * 4 * GB + 4 * b + i
                    sc = ps[0:S, i, 0:HG * S].rearrange("p (h t) -> p h t", h=HG)
                    dve.wait_ge(c["sc"], n + 1)
                    dve.tensor_reduce(cmx[0:S, i, :], sc, AX.X, ALU.max).then_inc(c["mx"], 1)
                    if b:
                        dve.wait_ge(c["pT"], n - 3)
                    dve.wait_ge(c["mx"], n + 1)
                    dve.tensor_tensor(cprobs[0:S, i, :, :], sc,
                                      cmx[0:S, i, :].unsqueeze(2).to_broadcast([S, HG, S]),
                                      ALU.subtract).then_inc(c["sub"], 1)

                def sum_probs(b, i):
                    n = g * 4 * GB + 4 * b + i
                    dve.wait_ge(c["exp"], n + 1)
                    dve.tensor_reduce(cden[0:S, i, :], cprobs[0:S, i, :, :], AX.X,
                                      ALU.add).then_inc(c["den"], 1)
                    dve.wait_ge(c["den"], n + 1)
                    dve.reciprocal(crden[0:S, i, :], cden[0:S, i, :]).then_inc(c["rden"], 1)

                def add_residual(t):
                    dve.wait_ge(c["w"], g * NT + t + 1)
                    dve.scalar_tensor_tensor(out=yn[0:tm, t, :], in0=ps[0:tm, t, :],
                                             scalar=1 / (CV_SCALE * W_SCALE), in1=yn[0:tm, t, :],
                                             op0=ALU.mult, op1=ALU.add).then_inc(c["x2"], 1)
                    dve.wait_ge(c["x2"], g * NT + t + 1)
                    row_stats(g * 2 * NT + nt + t, t, t + 1, tm)

                def norm(t):
                    norm_row(nrm, t, tm, g * (NT + 1) + t + 2)

                early = early_tiles(nb)
                for b in range(nb + 1):
                    for t in out_tiles_at(b, nb, last_nb):
                        add_out(g - 1, t, tiles_of(last_nb)[1])
                    if b < nb:
                        for i in range(4):
                            shift_scores(b, i)
                            if i:
                                sum_probs(b, i - 1)
                        sum_probs(b, 3)
                        for n in (beside_first(b) if not last_nb else []):
                            split_b_lo(n)
                    else:
                        dve.wait_ge(c["y"], g * 16 + 16)
                        for k, t in enumerate(early):
                            add_residual(t)
                            if k == 1:
                                norm(early[0])
                    if b:
                        take_o(b - 1)
                for t in out_tiles_at(nb + 1, nb, last_nb):
                    add_out(g - 1, t, tiles_of(last_nb)[1])
                for t in early[len(early) > 1:]:
                    norm(t)
                for t in range(len(early), nt):
                    add_residual(t)
                for t in early:
                    if t < 2:
                        row_lo(g * 2 * NT + nt, t, tm, t)
                for t in range(len(early), nt):
                    norm(t)
                for t in range(min(2, len(early)), nt):
                    row_lo(g * 2 * NT + nt, t, tm, t)
                if last_nb:
                    add_out(g - 1, tiles_of(last_nb)[0] - 1, tiles_of(last_nb)[1])

            def layer(g, nb, nxt):
                nt, tm = tiles_of(nb)
                gs = nb * S
                dve.wait_ge(c["rl"], g + 1)
                chain = [g * LINKS]

                def link(ins):
                    ins.then_inc(c["chain"], 1)
                    chain[0] = chain[0] + 1
                    dve.wait_ge(c["chain"], chain[0])

                def wide(name):
                    return col[name][0:tm, 0:nt].unsqueeze(2).to_broadcast([tm, nt, NE])

                lg, p, a, z = (rt[n][0:tm, 0:nt, :] for n in "lpab")
                link(dve.tensor_scalar(lg, ps[0:tm, 6, 0:nt * NE].rearrange("p (t e) -> p t e", e=NE),
                                       1 / (X_SCALE * W_SCALE), None, ALU.mult))
                link(dve.tensor_reduce(col["m"][0:tm, 0:nt], lg, AX.X, ALU.max))
                dve.tensor_tensor(p, lg, wide("m"), ALU.subtract).then_inc(c["top"], 1)
                dve.wait_ge(c["rexp"], g + 1)
                link(dve.tensor_reduce(col["d"][0:tm, 0:nt], p, AX.X, ALU.add))
                link(dve.reciprocal(col["r"][0:tm, 0:nt], col["d"][0:tm, 0:nt]))
                link(dve.tensor_tensor(p, p, wide("r"), ALU.mult))
                for k, w in enumerate(("w1", "w2")):
                    link(dve.tensor_reduce(col[w][0:tm, 0:nt], p, AX.X, ALU.max))
                    link(dve.tensor_tensor(a, p, wide(w), ALU.is_equal))
                    link(dve.tensor_tensor(a, a, rank[0:tm, 0:nt, :], ALU.mult))
                    link(dve.tensor_reduce(col["m"][0:tm, 0:nt], a, AX.X, ALU.max))
                    link(dve.tensor_tensor(sel[0:tm, k, 0:nt, :], a, wide("m"), ALU.is_equal))
                    link(dve.tensor_tensor(sel[0:tm, 2 + k, 0:nt, :], sel[0:tm, k, 0:nt, :], wide(w),
                                           ALU.mult))
                    if k == 0:
                        link(dve.scalar_tensor_tensor(out=p, in0=sel[0:tm, 0, 0:nt, :], scalar=-2.0,
                                                      in1=p, op0=ALU.mult, op1=ALU.add))
                for k in range(4):
                    dve.tensor_copy(spread[0:tm, 0:nt, k, :, :],
                                    sel[0:tm, k, 0:nt, :].unsqueeze(3).to_broadcast([tm, nt, NE, R])
                                    ).then_inc(c["spread"], 1)

                for i in range(4):
                    if i == 0:
                        dve.wait_ge(c["mTe"], g * 4 + 4)
                        dve.wait_ge(c["a"], g * 2 + 2)
                    dve.scalar_tensor_tensor(out=tmp[:, i, 0:gs], in0=ps[:, 4 + i // 2, 0:gs],
                                             scalar=X_SCALE * LORA / (X_SCALE * W_SCALE),
                                             in1=msk[:, i % 2, 0:gs], op0=ALU.mult,
                                             op1=ALU.mult).then_inc(c["am"], 1)
                for i in range(4):
                    dve.wait_ge(c["ahi"], g * 4 + i + 1)
                    dve.tensor_tensor(am_lo[:, i, 0:gs], tmp[:, i, 0:gs], am_hi[:, i, 0:gs],
                                      ALU.subtract).then_inc(c["alo"], 1)

                def lo_h(i, j):
                    dve.wait_ge(c["hhi"], g * 3 * FC + 3 * j + i + 1)
                    hi = hb_hi[:, j, 0:gs] if i == 0 else hs_hi[:, i - 1, 0:gs]
                    lo = hb_lo[:, j, 0:gs] if i == 0 else hs_lo[:, i - 1, 0:gs]
                    dve.tensor_tensor(lo, hh[:, i, 0:gs], hi, ALU.subtract).then_inc(c["hlo"], 1)

                for j in range(FC):
                    if j:
                        lo_h(1, j - 1)
                        lo_h(2, j - 1)
                    for i in (1, 2):
                        dve.wait_ge(c["lora"], g * 4 * FC + 4 * j + 2 * i)
                        dve.wait_ge(c["gb"], g * FC + j + 1)
                        if j:
                            dve.wait_ge(c["h"], g * 3 * FC + 3 * (j - 1) + i + 1)
                        dve.tensor_tensor(gate[:, i, 0:gs], ps[:, 2 * i, 0:gs], gb[:, 0:gs],
                                          ALU.add).then_inc(c["gs"], 1)
                        dve.wait_ge(c["ub"], g * FC + j + 1)
                        dve.scalar_tensor_tensor(out=up[:, i - 1, 0:gs], in0=ps[:, 2 * i + 1, 0:gs],
                                                 scalar=H_SCALE / (X_SCALE * W_SCALE),
                                                 in1=ub[:, 0:gs], op0=ALU.mult,
                                                 op1=ALU.add).then_inc(c["us"], 1)
                        if i == 1:
                            lo_h(0, j)
                    if nxt and j == LN_STATS_CHUNK:
                        first_stats(g + 1, nxt)
                    if nxt and j == LN_ROWS_CHUNK:
                        first_rows(g + 1, nxt)
                lo_h(1, FC - 1)
                lo_h(2, FC - 1)
                if nxt:
                    cross_attention(g + 1, nxt, nb)
                else:
                    sum_down(g, gs)
                    for t in range(nt):
                        add_out(g, t, tm)

            cross_attention(0, GB, 0)
            over_groups(dve, layer)

        @block.tensor
        def _(pe):
            pe.wait_ge(s["ident"], 1)

            def three(out_ap, pairs):
                mm = None
                for i, (ah, al, bh, bl) in enumerate(pairs):
                    pe.matmul(out_ap, ah, bh, start=(i == 0), stop=False)
                    pe.matmul(out_ap, ah, bl, start=False, stop=False)
                    mm = pe.matmul(out_ap, al, bh, start=False, stop=(i == len(pairs) - 1))
                return mm

            def turn_rows(b_t, t, tm, b_qk=0, turned=0):
                pe.wait_ge(s["xn"], b_t + t + 1)
                if turned:
                    pe.wait_ge(s["qTe"], b_qk + turned)
                    pe.wait_ge(s["kTe"], b_qk + turned)
                if t >= 2:
                    pe.wait_ge(s["xlo"], b_t + t - 1)
                for e in range(KC):
                    mm = pe.transpose(ps_T[:, t % 2, e * tm:(e + 1) * tm],
                                      xin[0:tm, t, e * P:(e + 1) * P], ident[0:tm, 0:tm])
                mm.then_inc(s["lnT"], 1)

            def project_qk(b_qk, b_t, tile):
                u, tm = tile.count, tile.tm
                hi, lo = (xTn_hi, xTn_lo) if tile.ahead else (xT_hi, xT_lo)
                if tile.ahead:
                    pe.wait_ge(s["xlo"], b_t + tile.t + 1)
                if u:
                    pe.wait_ge(s["raw"], b_qk + u)
                for m in range(2):
                    mm = three(ps_qk[0:tm, m, :], [
                        (hi[:, e, tile.cols], lo[:, e, tile.cols],
                         wqkv_hi[tile.hg][:, e, m, :], wqkv_lo[tile.hg][:, e, m, :])
                        for e in range(KC)])
                mm.then_inc(s["qkp"], 1)

            def turn_qk(b_qk, tile):
                u, tm = tile.count, tile.tm
                pe.wait_ge(s["qkn"], b_qk + u + 1)
                if u:
                    pe.wait_ge(s["qTe"], b_qk + u)
                    pe.wait_ge(s["kTe"], b_qk + u)
                for m in range(2):
                    for h in range(HG):
                        mm = pe.transpose(ps_T[:, m, h * tm:(h + 1) * tm],
                                          qk[0:tm, u % 2, m * HG + h, :], ident[0:tm, 0:tm])
                mm.then_inc(s["qkT"], 1)

            def scores(b_step, b_qk, n, nb, b, u):
                pe.wait_ge(s["qTe"], b_qk + u + 1)
                pe.wait_ge(s["kTe"], b_qk + u + 1)
                if n:
                    pe.wait_ge(s["sub"], b_step + n)
                for h in range(HG):
                    mm = pe.matmul(ps_s[0:S, h * S:(h + 1) * S],
                                   qkT[:, 0, h, b * S:(b + 1) * S],
                                   qkT[:, 1, h, b * S:(b + 1) * S], start=True, stop=True)
                mm.then_inc(s["s"], 1)

            def project_v(b_step, n, hg, b):
                three(ps_vw[0:S, :], [
                    (xT_hi[:, e, b * S:(b + 1) * S], xT_lo[:, e, b * S:(b + 1) * S],
                     wqkv_hi[hg][:, e, 2, :],
                     wqkv_lo[hg][:, e, 2, :])
                    for e in range(KC)]).then_inc(s["vp"], 1)

            def group(g, nb, nxt):
                nt, tm = tiles_of(nb)
                proj, turn, wo_at = attention_plan(nb, nxt)
                b_step, b_qk, steps = g * N_STEP, g * N_QK, NHG * nb
                added = turned = rows = 0

                def turn_tiles(n):
                    nonlocal turned
                    for tile in turn[n]:
                        if nxt and n >= TURN_AT[0]:
                            pe.wait_ge(s["xlo"], g * NT + NT + rows)
                        turn_qk(b_qk, tile)
                        turned = tile.count + 1

                for n in range(steps):
                    hg, b = (n + 1) // nb, (n + 1) % nb
                    own = n + 1 < steps
                    if own:
                        scores(b_step, b_qk, n + 1, nb, b, hg * nt + -(-S * (b + 1) // tm) - 1)
                    elif nxt:
                        scores(b_step, b_qk, steps, nxt, 0, N_QK)
                    pe.wait_ge(s["norm"], b_step + n + 1)
                    if n:
                        pe.wait_ge(s["pTe"], b_step + n)
                    for h in range(HG):
                        mm = pe.transpose(ps_pT[0:S, h * S:(h + 1) * S],
                                          probs[0:S, n % 2, h, :], ident[0:S, 0:S])
                    mm.then_inc(s["pTp"], 1)
                    if own or nxt:
                        pe.wait_ge(s["ve"], b_step + n + 1)
                        if added:
                            pe.wait_ge(s["add"], b_qk + added)
                        if own:
                            project_v(b_step, n + 1, hg, b)
                        else:
                            pe.wait_ge(s["xTc"], g * 2 + 4)
                            project_v(b_step, n + 1, 0, 0)
                    for t in turned_at(n, nxt):
                        turn_rows(g * NT + NT, t, tiles_of(nxt)[1], b_qk, turned)
                        rows = t + 1
                    pe.wait_ge(s["pTe"], b_step + n + 1)
                    pe.wait_ge(s["ve"], b_step + n + 1)
                    if n:
                        pe.wait_ge(s["olo"], b_step + n)
                    for h in range(HG):
                        mm = pe.matmul(ps_o[:, h * S:(h + 1) * S],
                                       v[0:S, n % 2, h * D:(h + 1) * D],
                                       pT[0:S, h, :], start=True, stop=True)
                    mm.then_inc(s["o"], 1)
                    for tile in proj[n]:
                        project_qk(b_qk, g * NT + NT, tile)
                    late = (own or nxt) and (nb == nt or not proj[n])
                    if not late:
                        turn_tiles(n)
                    for w in wo_at[n]:
                        w_hg, t = w // nt, w % nt
                        b_last = -(-(t + 1) * tm // S) - 1
                        pe.wait_ge(s["olo"], b_step + w_hg * nb + b_last + 1)
                        pe.wait_ge(s["ve"], b_step + n + 1 + (own or nxt > 0))
                        if w:
                            pe.wait_ge(s["add"], b_qk + w)
                        three(ps_vw[0:tm, :], [
                            (oT_hi[:, h, t * tm:(t + 1) * tm], oT_lo[:, h, t * tm:(t + 1) * tm],
                             wo_hi[w_hg][:, h, :], wo_lo[w_hg][:, h, :])
                            for h in range(HG)]).then_inc(s["w"], 1)
                        added += 1
                        if late:
                            turn_tiles(n)
                            late = False
                    if late:
                        turn_tiles(n)
                if nxt:
                    pe.wait_ge(s["add"], b_qk + NHG * nt)

            for t in range(NT):
                turn_rows(0, t, TM)
            pe.wait_ge(s["wlo"], 2)
            tiles = first_tiles(GB, 0, True)
            for tile in tiles:
                project_qk(0, 0, tile)
                if tile.t:
                    turn_qk(0, tiles[tile.t - 1])
            turn_qk(0, tiles[-1])
            scores(0, 0, 0, GB, 0, 0)
            pe.wait_ge(s["xTc"], 2)
            pe.wait_ge(s["wlo"], 3)
            project_v(0, 0, 0, 0)
            pe.wait_ge(s["wlo"], SPLIT_AT[-1])
            over_groups(pe, group)

            pe.wait_ge(s["add"], LAST_QK + NHG * LAST_NT)
            pe.wait_ge(c["wlo"], B_FIRST)
            pe.wait_ge(c["wkv"], 16)
            pe.wait_ge(c["mask"], 5)
            pe.wait_ge(c["rank"], NE)

            def turn_row(count, src, t, tm, bank):
                pe.wait_ge(c["yn"], count + t + 1)
                for e in range(KC):
                    mm = pe.transpose(ps[:, bank, e * tm:(e + 1) * tm],
                                      src[0:tm, t, e * P:(e + 1) * P], ident[0:tm, 0:tm])
                mm.then_inc(c["lnT"], 1)

            def wide(out_ap, w_hi, w_lo, a, b, gs):
                return three(out_ap, [(w_hi[:, e, a:b], w_lo[:, e, a:b],
                                       yT_hi[:, e, 0:gs], yT_lo[:, e, 0:gs]) for e in range(KC)])

            def project_out(g, piece, tm):
                t, j = divmod(piece, FC + 1)
                a, b = t * tm, (t + 1) * tm
                if piece == 0:
                    pe.wait_ge(c["dlo"], g + 1)
                elif j == 0:
                    pe.wait_ge(c["add"], g * NT + t)
                h_hi, h_lo, w_hi, w_lo = ((hb_hi[:, j, a:b], hb_lo[:, j, a:b], wd_hi[:, j, :],
                                           wd_lo[:, j, :]) if j < FC else
                                          (d_hi[:, a:b], d_lo[:, a:b], bd_hi[:, :], bd_lo[:, :]))
                pe.matmul(ps[0:tm, 7, :], h_hi, w_hi, start=(j == 0), stop=False)
                pe.matmul(ps[0:tm, 7, :], h_hi, w_lo, start=False, stop=False)
                mm = pe.matmul(ps[0:tm, 7, :], h_lo, w_hi, start=False, stop=(j == FC))
                if j == FC:
                    mm.then_inc(c["yp"], 1)

            def down_factors(g, gs, j):
                pe.wait_ge(c["hlo"], g * 3 * FC + 3 * j + 3)
                for i in range(2):
                    pe.matmul(ps[:, 6 + i, 0:gs], ad_hi[:, j, :], hs_hi[:, i, 0:gs],
                              start=(j == 0), stop=False)
                    pe.matmul(ps[:, 6 + i, 0:gs], ad_hi[:, j, :], hs_lo[:, i, 0:gs],
                              start=False, stop=False)
                    mm = pe.matmul(ps[:, 6 + i, 0:gs], ad_lo[:, j, :], hs_hi[:, i, 0:gs],
                                   start=False, stop=(j == FC - 1))
                mm.then_inc(c["ad"], 1)

            def cross_attention(g, nb, last_nb):
                nt, tm = tiles_of(nb)
                gs = nb * S
                made = [0]

                def some_out(n):
                    for _ in range(n if last_nb else 0):
                        project_out(g - 1, made[0], tiles_of(last_nb)[1])
                        made[0] += 1

                if last_nb:
                    pe.wait_ge(c["ub"], g * FC)
                    pe.wait_ge(c["sg0"], g * FC)
                    pe.wait_ge(c["gb"], g * FC)
                for t in range(min(nt, 2)):
                    turn_row(g * 2 * NT, yn, t, tm, t)
                if last_nb:
                    pe.wait_ge(c["gs"], g * 2 * FC)
                    pe.wait_ge(c["us"], g * 2 * FC)
                pe.wait_ge(c["ctx"], g * 16 + 16)
                for m in range(KC):
                    pe.matmul(ps[:, 2 + m, 0:gs], cwkv[:, m * P:(m + 1) * P], ctxT[:, 0:gs],
                              start=True, stop=True).then_inc(c["ck"], 1)
                if last_nb:
                    down_factors(g - 1, last_nb * S, FC - 1)
                for t in range(2, nt):
                    pe.wait_ge(c["lnlo"], g * 2 * NT + t - 1)
                    turn_row(g * 2 * NT, yn, t, tm, t % 2)
                for b in range(nb):
                    if b < 2:
                        pe.wait_ge(c["cke"], g * KC + b + 1)
                    else:
                        pe.wait_ge(c["ve"], g * GB + b - 1)
                    pe.matmul(ps[0:S, 2 + b % 2, :], ctxT[:, b * S:(b + 1) * S], cwkv[:, E:2 * E],
                              start=True, stop=True).then_inc(c["v"], 1)
                pe.wait_ge(c["lnlo"], g * 2 * NT + nt)
                for m in range(KC):
                    if m == 2:
                        pe.wait_ge(c["cke"], g * KC + KC)
                    wide(ps[:, QP_BANKS[m], 0:gs], cwq_hi, cwq_lo, m * P, (m + 1) * P, gs
                         ).then_inc(c["qp"], 1)
                pe.wait_ge(c["ve"], g * GB + nb)
                pe.wait_ge(c["cke"], g * KC + KC)
                pe.wait_ge(c["qpe"], g * KC + KC)

                def mix(b, i):
                    n = 4 * (b - 1) + i
                    pe.wait_ge(c["pTe"], g * 4 * GB + n + 1)
                    if i == 0 and b >= 2:
                        pe.wait_ge(c["olo"], g * GB + b - 1)
                    for m in range(KC):
                        h = 4 * m + i
                        mm = pe.matmul(ps[i * CD:(i + 1) * CD, 6, m * S:(m + 1) * S],
                                       cv[0:S, b - 1, h * CD:(h + 1) * CD], cpT[0:S, n % 2, m, :],
                                       start=True, stop=True)
                    mm.then_inc(c["pv"], 1)

                def project(t):
                    pe.wait_ge(c["olo"], g * GB + -(-(t + 1) * tm // S))
                    three(ps[0:tm, t, :], [
                        (coT_hi[:, e, t * tm:(t + 1) * tm], coT_lo[:, e, t * tm:(t + 1) * tm],
                         cwo_hi[:, e, :], cwo_lo[:, e, :]) for e in range(KC)]).then_inc(c["w"], 1)

                early = early_tiles(nb)
                for b in range(nb + 1):
                    if b < nb:
                        for i in range(4):
                            if b:
                                pe.wait_ge(c["sub"], g * 4 * GB + 4 * (b - 1) + i + 1)
                            pe.matmul(ps[0:S, i, 0:HG * S], ident16[0:S, 0:S],
                                      mask[0:S, :, :].rearrange("p h k -> p (h k)"),
                                      start=True, stop=False)
                        for m in range(KC):
                            for i in range(4):
                                r0 = i * CD
                                mm = pe.matmul(ps[0:S, i, m * S:(m + 1) * S],
                                               qpT[r0:r0 + CD, m, b * S:(b + 1) * S],
                                               ckT[r0:r0 + CD, m, b * S:(b + 1) * S],
                                               start=False, stop=(m == KC - 1))
                                if m == KC - 1:
                                    mm.then_inc(c["sc"], 1)
                    for i in range(4):
                        if b:
                            pe.wait_ge(c["norm"], g * 4 * GB + 4 * (b - 1) + i + 1)
                            for m in range(KC):
                                mm = pe.transpose(ps[0:S, 4 + i % 2, m * S:(m + 1) * S],
                                                  cprobs[0:S, i, m, :], ident[0:S, 0:S])
                            mm.then_inc(c["pT"], 1)
                            if i:
                                mix(b, i - 1)
                            if b == nb and 1 <= i <= len(early):
                                if i == 1:
                                    pe.wait_ge(c["sub"], g * 4 * GB + 4 * nb)
                                project(early[i - 1])
                        some_out(OUT_AT[nb][b][i])
                    if b:
                        mix(b, 3)
                    some_out(OUT_AT[nb][b][4])

                for t in early[:2]:
                    turn_row(g * 2 * NT + nt, nrm, t, tm, t)
                for t in range(len(early), nt):
                    project(t)
                some_out(OUT_AFTER[0])
                for t in range(min(2, len(early)), nt):
                    turn_row(g * 2 * NT + nt, nrm, t, tm, t)
                some_out(OUT_AFTER[1])

                pe.wait_ge(c["lnlo"], g * 2 * NT + 2 * nt)
                for t in range(nt):
                    mm = three(ps[0:tm, 6, t * NE:(t + 1) * NE], [
                        (yT_hi[:, e, t * tm:(t + 1) * tm], yT_lo[:, e, t * tm:(t + 1) * tm],
                         wr_hi[:, e, :], wr_lo[:, e, :]) for e in range(KC)])
                mm.then_inc(c["rl"], 1)
                wide(ps[:, 4, 0:gs], ag_hi, ag_lo, 0, P, gs).then_inc(c["a"], 1)
                wide(ps[:, 5, 0:gs], au_hi, au_lo, 0, P, gs).then_inc(c["a"], 1)
                if last_nb:
                    pe.wait_ge(c["add"], (g - 1) * NT + tiles_of(last_nb)[0])

            def layer(g, nb, nxt):
                nt, tm = tiles_of(nb)
                gs = nb * S
                for k in range(4):
                    pe.wait_ge(c["spread"], g * 4 + k + 1)
                    if k >= 2:
                        pe.wait_ge(c["mTe"], g * 4 + k - 1)
                    for t in range(nt):
                        mm = pe.transpose(ps[:, 2 + k % 2, t * tm:(t + 1) * tm],
                                          spread[0:tm, t, k, :, :].rearrange("p e r -> p (e r)"),
                                          ident[0:tm, 0:tm])
                    mm.then_inc(c["mT"], 1)
                for j in range(FC):
                    f0, f1 = j * P, (j + 1) * P
                    if j:
                        pe.wait_ge(c["sg0"], g * FC + j)
                        pe.wait_ge(c["gb"], g * FC + j)
                    wide(ps[:, 0, 0:gs], wg_hi, wg_lo, f0, f1, gs).then_inc(c["base"], 1)
                    if j:
                        pe.wait_ge(c["ub"], g * FC + j)
                    wide(ps[:, 1, 0:gs], wu_hi, wu_lo, f0, f1, gs).then_inc(c["base"], 1)
                    if j == 0:
                        pe.wait_ge(c["alo"], g * 4 + 4)
                    for i in range(2):
                        if j:
                            pe.wait_ge(c["gs"], g * 2 * FC + 2 * (j - 1) + i + 1)
                            pe.wait_ge(c["us"], g * 2 * FC + 2 * (j - 1) + i + 1)
                        three(ps[:, 2 + 2 * i, 0:gs], [(bg_hi[:, f0:f1], bg_lo[:, f0:f1],
                              am_hi[:, i, 0:gs], am_lo[:, i, 0:gs])]).then_inc(c["lora"], 1)
                        three(ps[:, 3 + 2 * i, 0:gs], [(bu_hi[:, f0:f1], bu_lo[:, f0:f1],
                              am_hi[:, 2 + i, 0:gs], am_lo[:, 2 + i, 0:gs])]).then_inc(c["lora"], 1)
                    if j:
                        down_factors(g, gs, j - 1)
                if nxt:
                    cross_attention(g + 1, nxt, nb)
                else:
                    down_factors(g, gs, FC - 1)
                    for piece in range(nt * (FC + 1)):
                        project_out(g, piece, tm)

            cross_attention(0, GB, 0)
            pe.wait_ge(c["wlo"], len(B_PIECES))
            over_groups(pe, layer)


def kernel(x, ctx_512, L0_attn_wq, L0_attn_wk, L0_attn_wv, L0_attn_wo, L0_attn_q_scale,
           L0_attn_k_scale, L0_xattn_Wq, L0_xattn_Wkv_expand, L0_xattn_Wout, L0_ffn_Wg, L0_ffn_Wu,
           L0_ffn_Wd, L0_ffn_Wr, L0_ffn_Ag, L0_ffn_Bg, L0_ffn_Au, L0_ffn_Bu, L0_ffn_Ad, L0_ffn_Bd):
    import concourse.bacc as bacc
    from concourse.bass_utils import run_bass_kernel_spmd

    def rows(w):
        return np.asarray(w).reshape(-1, np.asarray(w).shape[-1])

    B = x.shape[0]
    laid = {
        "x": rows(x),
        "wq": np.asarray(L0_attn_wq).reshape(E, H * D),
        "wk": np.asarray(L0_attn_wk).reshape(E, H * D),
        "wv": np.asarray(L0_attn_wv).reshape(E, H * D),
        "wo": np.asarray(L0_attn_wo).reshape(H * D, E),
        "q_scale": np.asarray(L0_attn_q_scale).reshape(D, 1),
        "k_scale": np.asarray(L0_attn_k_scale).reshape(D, 1),
        "ctxT": np.asarray(ctx_512).transpose(0, 2, 1),
        "cwq": np.asarray(L0_xattn_Wq).T,
        "cwkv": np.asarray(L0_xattn_Wkv_expand).T,
        "cwo": np.asarray(L0_xattn_Wout).T,
        "wg": np.asarray(L0_ffn_Wg).T,
        "wu": np.asarray(L0_ffn_Wu).T,
        "wd": np.asarray(L0_ffn_Wd).T,
        "ag": rows(L0_ffn_Ag).T,
        "au": rows(L0_ffn_Au).T,
        "ad": rows(L0_ffn_Ad).T,
        "bg": rows(np.asarray(L0_ffn_Bg).transpose(0, 2, 1)),
        "bu": rows(np.asarray(L0_ffn_Bu).transpose(0, 2, 1)),
        "bd": rows(np.asarray(L0_ffn_Bd).transpose(0, 2, 1)),
        "wr": np.asarray(L0_ffn_Wr).T,
    }
    nc = bacc.Bacc("TRN2", target_bir_lowering=False, num_devices=1)
    laid = {n: np.ascontiguousarray(a) for n, a in laid.items()}
    args = [nc.dram_tensor(f"in_{n}", a.shape, F32, kind="ExternalInput").ap()
            for n, a in laid.items()]
    args.append(nc.dram_tensor("x1", (B * S, E), F32, kind="Internal").ap())
    args.append(nc.dram_tensor("out", (B * S, E), F32, kind="ExternalOutput").ap())
    decoder_layer(nc, *args)
    r = run_bass_kernel_spmd(nc, [{f"in_{n}": a for n, a in laid.items()}], core_ids=[0])
    return r.results[0]["out"].reshape(x.shape)
```
